# Optimizing a Trainium2 kernel written in Bass

```python
import numpy as np
import jax
import jax.numpy as jnp

def _softmax(x, axis=-1):
    return jax.nn.softmax(x, axis=axis)

def _gelu(x):
    return jax.nn.gelu(x, approximate=True)

def _silu(x):
    return jax.nn.silu(x)

def _sigmoid(x):
    return jax.nn.sigmoid(x)

def _layernorm(x, axis=-1, eps=1e-05):
    m = jnp.mean(x, axis=axis, keepdims=True)
    v = jnp.var(x, axis=axis, keepdims=True)
    return (x - m) / jnp.sqrt(v + eps)

def _scatter_add(tgt, idx, src, axis=0):
    return tgt.at[idx].add(src)

def _segment_sum(src, seg, n):
    return jax.ops.segment_sum(src, seg, n)
kernel_name = 'mk_decoder_preln_d1_seqx_r4_e81e9e'

def setup_inputs(seed: int=0):
    np.random.seed(seed)
    _w = jnp.asarray

    def _rec_inputs():
        import jax
        import jax.numpy as jnp
        _rk = jax.random.key(seed)
        x = -0.0002928 + 1 * jax.random.normal(jax.random.fold_in(_rk, 1), (16, 256, 256), jnp.float32)
        _lenS = 256 - jax.random.randint(jax.random.fold_in(_rk, 7), (16,), 0, max(1, 256 // 4) + 1, jnp.int32)
        _lenS2 = 256 - jax.random.randint(jax.random.fold_in(_rk, 8), (16,), 0, max(1, 256 // 4) + 1, jnp.int32)
        _ctx_1024P = jax.random.normal(jax.random.fold_in(_rk, 11), (16, 16, 256), jnp.float32)
        _ctx_1024c = jax.random.dirichlet(jax.random.fold_in(_rk, 511), 0.3 * jnp.ones((16,), jnp.float32), (16, 256))
        _ctx_1024t = jnp.einsum('bsk,bkd->bsd', _ctx_1024c, _ctx_1024P)
        _ctx_1024t = _ctx_1024t * jax.lax.rsqrt(jnp.mean(jnp.square(_ctx_1024t)) + 1e-12) * 0.953939
        ctx_1024 = -1.39393e-06 + 0.999914 * (_ctx_1024t + 0.3 * jax.random.normal(jax.random.fold_in(_rk, 611), (16, 256, 256), jnp.float32))
        return (x, ctx_1024)
    x, ctx_1024 = _rec_inputs()

    def _L0_attn_setup():
        import jax, jax.numpy as jnp
        import numpy as np
        key = jax.random.key(seed)
        k1, k2, k3 = jax.random.split(key, 3)
        B, S, D, N = (2, 512, 256, 16)
        H = D // N
        x = jax.random.normal(k1, (B, S, D), dtype=jnp.float32)
        W_qkv = jax.random.normal(k2, (N, D, 3 * H), dtype=jnp.float32) / np.sqrt(D).astype(np.float32)
        W_out = jax.random.normal(k3, (N, H, D), dtype=jnp.float32) / np.sqrt(D).astype(np.float32)
        return {'x': x, 'W_qkv': W_qkv, 'W_out': W_out}
    _L0_attn_all = _L0_attn_setup()
    _L0_attn_in = {k: v for k, v in _L0_attn_all.items() if k in ('W_qkv', 'W_out')}
    del _L0_attn_all

    def _L0_xattn_setup():
        import jax, jax.numpy as jnp
        import numpy as np
        B, S, DIM, NH = (2, 512, 256, 8)
        DH = DIM // NH
        GATE_SOFT_CAP = 15.0
        BACKEND_EPS = 5e-05
        NORM_EPS = 1e-06

        def _mlstm_parallel(q, k, v, i_pre, f_pre):
            log_fg = jax.nn.log_sigmoid(f_pre)
            lf_cs = jnp.cumsum(log_fg, axis=-1)
            lf = jnp.concatenate([jnp.zeros_like(lf_cs[..., :1]), lf_cs], axis=-1)
            log_d = lf[..., 1:, None] - lf[..., None, 1:] + i_pre[..., None, :]
            t_idx = jnp.arange(q.shape[2])
            mask = t_idx[:, None] >= t_idx[None, :]
            log_d = jnp.where(mask, log_d, -jnp.inf)
            m = jnp.max(log_d, axis=-1, keepdims=True)
            d_mat = jnp.exp(log_d - m)
            scores = jnp.einsum('bhtd,bhsd->bhts', q, k) * (1.0 / np.sqrt(DH))
            s_mat = scores * d_mat
            denom = jnp.maximum(jnp.abs(jnp.sum(s_mat, axis=-1, keepdims=True)), jnp.exp(-m)) + BACKEND_EPS
            return jnp.einsum('bhts,bhsd->bhtd', s_mat, v) / denom
        key = jax.random.key(seed)
        kq, kk, kv, kw = jax.random.split(key, 4)
        q = jax.random.normal(kq, (B, S, DIM), dtype=jnp.float32)
        k = jax.random.normal(kk, (B, S, DIM), dtype=jnp.float32)
        v = jax.random.normal(kv, (B, S, DIM), dtype=jnp.float32)
        ifgate_w = 0.02 * jax.random.normal(kw, (2 * NH, 3 * DIM), dtype=jnp.float32)
        ifgate_b = jnp.concatenate([jnp.full((NH,), -10.0, dtype=jnp.float32), jnp.linspace(3.0, 6.0, NH, dtype=jnp.float32)])
        outnorm_w = jnp.zeros((DIM,), dtype=jnp.float32)
        return {'q': q, 'k': k, 'v': v, 'ifgate_w': ifgate_w, 'ifgate_b': ifgate_b, 'outnorm_w': outnorm_w}
    _L0_xattn_all = _L0_xattn_setup()
    _L0_xattn_in = {k: v for k, v in _L0_xattn_all.items() if k in ('ifgate_w', 'ifgate_b', 'outnorm_w')}
    del _L0_xattn_all

    def _L0_ffn_setup():
        import jax, jax.numpy as jnp
        import numpy as np
        D_MODEL = 256
        N_EXPERTS = 8
        TOP_K = 2
        key = jax.random.key(seed)
        k1, k2, k3, k4 = jax.random.split(key, 4)
        B, S, D, E = (4, 512, D_MODEL, N_EXPERTS)
        dff = 4 * D
        lim = float(np.sqrt(6.0 / (D + dff)))
        return {'x': jax.random.normal(k1, (B, S, D), dtype=jnp.float32), 'router_w': jax.random.normal(k2, (D, E), dtype=jnp.float32) * (1.0 / np.sqrt(D)), 'router_b': jnp.zeros((E,), dtype=jnp.float32), 'expert_up': jax.random.uniform(k3, (E, dff, D), dtype=jnp.float32, minval=-lim, maxval=lim), 'expert_down': jax.random.uniform(k4, (E, D, dff), dtype=jnp.float32, minval=-lim, maxval=lim)}
    _L0_ffn_all = _L0_ffn_setup()
    _L0_ffn_in = {k: v for k, v in _L0_ffn_all.items() if k in ('router_w', 'router_b', 'expert_up', 'expert_down')}
    del _L0_ffn_all
    return {'x': x, 'ctx_1024': ctx_1024, 'L0_attn_W_qkv': _L0_attn_in['W_qkv'], 'L0_attn_W_out': _L0_attn_in['W_out'], 'L0_xattn_ifgate_w': _L0_xattn_in['ifgate_w'], 'L0_xattn_ifgate_b': _L0_xattn_in['ifgate_b'], 'L0_xattn_outnorm_w': _L0_xattn_in['outnorm_w'], 'L0_ffn_router_w': _L0_ffn_in['router_w'], 'L0_ffn_router_b': _L0_ffn_in['router_b'], 'L0_ffn_expert_up': _L0_ffn_in['expert_up'], 'L0_ffn_expert_down': _L0_ffn_in['expert_down']}

def reference(x, ctx_1024, L0_attn_W_qkv, L0_attn_W_out, L0_xattn_ifgate_w, L0_xattn_ifgate_b, L0_xattn_outnorm_w, L0_ffn_router_w, L0_ffn_router_b, L0_ffn_expert_up, L0_ffn_expert_down):
    import jax
    import jax.numpy as jnp

    def _L0_attn_ref(x, W_qkv, W_out):
        import jax, jax.numpy as jnp
        import numpy as np
        B, S, D = x.shape
        head_dim = W_qkv.shape[-1] // 3
        qkv = jnp.einsum('bsd,ndh->bnsh', x, W_qkv)
        q, k, v = jnp.split(qkv, 3, axis=-1)
        scale = jnp.asarray(1.0 / np.sqrt(head_dim), dtype=x.dtype)
        attn = jnp.einsum('bnqh,bnkh->bnqk', q, k) * scale
        mask = jnp.asarray(-10000000000.0, dtype=x.dtype) * (1.0 - jnp.tril(jnp.ones((S, S), dtype=x.dtype)))
        attn = jax.nn.softmax(attn + mask, axis=-1)
        out = jnp.einsum('bnqk,bnkh->bnqh', attn, v)
        out = out.reshape(B, -1, S)
        return jnp.einsum('bds,nhd->bsd', out, W_out)

    def _L0_xattn_ref(q, k, v, ifgate_w, ifgate_b, outnorm_w):
        import jax, jax.numpy as jnp
        import numpy as np
        B, S, DIM, NH = (2, 512, 256, 8)
        DH = DIM // NH
        GATE_SOFT_CAP = 15.0
        BACKEND_EPS = 5e-05
        NORM_EPS = 1e-06

        def _mlstm_parallel(q, k, v, i_pre, f_pre):
            log_fg = jax.nn.log_sigmoid(f_pre)
            lf_cs = jnp.cumsum(log_fg, axis=-1)
            lf = jnp.concatenate([jnp.zeros_like(lf_cs[..., :1]), lf_cs], axis=-1)
            log_d = lf[..., 1:, None] - lf[..., None, 1:] + i_pre[..., None, :]
            t_idx = jnp.arange(q.shape[2])
            mask = t_idx[:, None] >= t_idx[None, :]
            log_d = jnp.where(mask, log_d, -jnp.inf)
            m = jnp.max(log_d, axis=-1, keepdims=True)
            d_mat = jnp.exp(log_d - m)
            scores = jnp.einsum('bhtd,bhsd->bhts', q, k) * (1.0 / np.sqrt(DH))
            s_mat = scores * d_mat
            denom = jnp.maximum(jnp.abs(jnp.sum(s_mat, axis=-1, keepdims=True)), jnp.exp(-m)) + BACKEND_EPS
            return jnp.einsum('bhts,bhsd->bhtd', s_mat, v) / denom
        b, s, dim = q.shape
        gate_in = jnp.concatenate([q, k, v], axis=-1)
        pre = gate_in @ ifgate_w.T + ifgate_b
        pre = GATE_SOFT_CAP * jnp.tanh(pre / GATE_SOFT_CAP)
        i_pre = pre[..., :NH].transpose(0, 2, 1)
        f_pre = pre[..., NH:].transpose(0, 2, 1)
        qh = q.reshape(b, s, NH, DH).transpose(0, 2, 1, 3)
        kh = k.reshape(b, s, NH, DH).transpose(0, 2, 1, 3)
        vh = v.reshape(b, s, NH, DH).transpose(0, 2, 1, 3)
        h = _mlstm_parallel(qh, kh, vh, i_pre, f_pre)
        rrms = jax.lax.rsqrt(jnp.mean(h * h, axis=-1, keepdims=True) + NORM_EPS)
        gain = (1.0 + outnorm_w).reshape(1, NH, 1, DH)
        h = h * rrms * gain
        return h.transpose(0, 2, 1, 3).reshape(b, s, dim)

    def _L0_ffn_ref(x, router_w, router_b, expert_up, expert_down):
        import jax, jax.numpy as jnp
        import numpy as np
        D_MODEL = 256
        N_EXPERTS = 8
        TOP_K = 2
        B, S, D = x.shape
        E = expert_up.shape[0]
        x_flat = x.reshape(-1, D)
        logits = x_flat @ router_w + router_b
        probs = jax.nn.softmax(logits, axis=-1)
        top_w, top_idx = jax.lax.top_k(probs, TOP_K)
        comb = jnp.sum(top_w[..., None] * jax.nn.one_hot(top_idx, E, dtype=x.dtype), axis=1)
        output = jnp.zeros_like(x_flat)
        for e in range(E):
            h = jax.nn.gelu(x_flat @ expert_up[e].T, approximate=False)
            out_e = h @ expert_down[e].T
            output = output + comb[:, e:e + 1] * out_e
        return output.reshape(B, S, D)
    x = x + _L0_attn_ref(_layernorm(x, axis=-1), L0_attn_W_qkv, L0_attn_W_out)
    x = x + _L0_xattn_ref(_layernorm(x, axis=-1), ctx_1024, ctx_1024, L0_xattn_ifgate_w, L0_xattn_ifgate_b, L0_xattn_outnorm_w)
    x = x + _L0_ffn_ref(_layernorm(x, axis=-1), L0_ffn_router_w, L0_ffn_router_b, L0_ffn_expert_up, L0_ffn_expert_down)
    return x

_drawn_inputs = setup_inputs


def setup_inputs(seed=0):
    import zlib

    import numpy as np

    out = dict(_drawn_inputs(seed))
    spreads = {'L0_xattn_outnorm_w': (0.0, 0.1), 'L0_ffn_router_b': (0.0, 0.377)}
    factors = {}
    for name, (base, spread) in spreads.items():
        noise = np.random.default_rng([zlib.crc32(name.encode()), seed]).standard_normal(out[name].shape)
        drawn = base * np.exp(spread * noise) if base else spread * noise
        out[name] = jnp.asarray(drawn.astype(out[name].dtype))
    for name, factor in factors.items():
        out[name] = (out[name] * factor).astype(out[name].dtype)
    return out
```

```python
import concourse.bass as bass
from concourse import mybir
from contextlib import ExitStack

F32 = mybir.dt.float32
BF = mybir.dt.bfloat16
I32 = mybir.dt.int32
ALU = mybir.AluOpType
ACT = mybir.ActivationFunctionType
AX = mybir.AxisListType

B, S, D = 16, 256, 256
NT = B * 2
NH = 16
MH = 8
E = 8
TOK = B * S
NTILE = 71
SLOTS = NTILE * 128
ROW = 260
NEG = -1.0e30

C_ID, C_MASK, C_U, C_SEL, C_M0, C_M1, C_C17, C_TOK, C_EK, C_J, C_DUMP, C_END = (
    0, 128, 256, 384, 416, 417, 418, 419, 451, 459, 530, 531)


class Queue:

    def __init__(self, sem):
        self.sem, self.n, self.items, self.seen = sem, 0, [], {}

    def wait(self, *toks):
        for t in toks:
            if t is None or self.seen.get(id(t[0]), 0) >= t[1]:
                continue
            self.seen[id(t[0])] = t[1]
            self.items.append(lambda e, t=t: e.wait_ge(t[0], t[1]))

    def op(self, fn, sig=True):
        if sig:
            self.n += 1
            self.items.append(lambda e: fn(e).then_inc(self.sem, 1))
            return (self.sem, self.n)
        self.items.append(lambda e: fn(e))
        return None

    def raw(self, fn):
        self.items.append(fn)

    def dma(self, lane, fn):
        lane.n += 16
        self.items.append(lambda e: fn(e).then_inc(lane.sem, 16))
        return (lane.sem, lane.n)

    def now(self):
        return (self.sem, self.n)

    def run(self, e):
        for f in self.items:
            f(e)


class Lane:

    def __init__(self, sem):
        self.sem, self.n = sem, 0


def build(nc, x, ctx_in, wqkv, wout, wg, bg, gain, wr, br, wup, wdn, cst, out):
    xs = nc.dram_tensor("xs_scr", (SLOTS, ROW), F32, kind="Internal").ap()
    osc = nc.dram_tensor("o_scr", (B, D * S), F32, kind="Internal").ap()
    qsc = nc.dram_tensor("q_scr", (B, 128, 2048), BF, kind="Internal").ap()
    gsc = nc.dram_tensor("g_scr", (6, 128, 256), BF, kind="Internal").ap()

    st = ExitStack()
    with st:
        def sb(name, shape, dt, c=st):
            return c.enter_context(nc.sbuf_tensor(name, shape, dt))

        def sem(name):
            return st.enter_context(nc.semaphore(name))

        def lane(name):
            return Lane(sem(name))

        PE, DV, AC, PO, SP = (Queue(sem("s_" + n)) for n in ("pe", "dve", "act", "pool", "sp"))

        banks = [st.enter_context(nc.psum_tensor(f"bank{i}", [128, 512], F32)) for i in range(8)]

        XB = sb("XB", [128, NT, ROW], F32)
        WU = sb("WU", [128, E * 4096], BF)
        CF = sb("CF", [128, C_END], F32)
        idb = sb("idb", [128, 128], BF)
        Ub = sb("Ub", [128, 128], BF)
        onesb = sb("onesb", [128, 128], BF)
        onesf = sb("onesf", [128, 2], F32)
        mhalf = sb("mhalf", [128, 8], F32)
        WGf = sb("WGf", [128, 2, 56], F32)
        WGs = sb("WGs", [128, 2, 2, 40], BF)
        BG = sb("BG", [128, 24], F32)
        EM = sb("EM", [128, 2, 128], F32)
        GN = sb("GN", [128, 256], F32)
        stat = sb("stat", [128, 2, 2, 8], F32)
        STG = sb("STG", [128, 2, 512], F32)
        idf = CF[:, C_ID:C_ID + 128]
        m0 = CF[:, C_M0:C_M0 + 1]
        m1n = CF[:, C_M1:C_M1 + 1]
        c17 = CF[:, C_C17:C_C17 + 1]

        gates = banks[7]
        ringW = [banks[5], banks[6]]

        l_c = lane("l_c")
        l_x = [lane(f"l_x{i}") for i in range(4)]
        l_w = lane("l_w")
        t_c = SP.dma(l_c, lambda e: e.dma_start(CF[:, :], cst))
        xv = x.rearrange("b (t p) d -> p (b t) d", p=128)
        t_x = []

        def load_x(i):
            t_x.append(SP.dma(l_x[i], lambda e: e.dma_start(XB[:, 8 * i:8 * i + 8, 0:256], xv[:, 8 * i:8 * i + 8, :])))
        load_x(0)
        l_wg = lane("l_wg")
        SP.dma(l_wg, lambda e: e.dma_start(WGf[:, :, 0:48], wg))
        SP.dma(l_wg, lambda e: e.dma_start(WGf[:, :, 48:56], wr))
        SP.dma(l_wg, lambda e: e.dma_start(BG[:, 0:16], bg.rearrange("(a n) -> a n", a=1).broadcast_to([128, 16])))
        SP.dma(l_wg, lambda e: e.dma_start(BG[:, 16:24], br.rearrange("(a n) -> a n", a=1).broadcast_to([128, 8])))
        t_wg = SP.dma(l_wg, lambda e: e.dma_start(GN[:, :], gain.rearrange("(a n) -> a n", a=1).broadcast_to([128, 256])))

        ca = ExitStack()
        WQh = sb("WQh", [128, 2, 1280], BF, ca)
        WQl = sb("WQl", [128, 2, 1280], BF, ca)
        mkb = sb("mkb", [128, 128], BF, ca)
        xn = sb("xn", [128, 1, 2, 256], F32, ca)
        xTh = sb("xTh", [128, 2, 2, 256], BF, ca)
        xTl = sb("xTl", [128, 2, 2, 256], BF, ca)
        Qh = sb("Qh", [128, 2, 4, 256], BF, ca)
        Q1 = sb("Q1", [128, 3, 4, 256], BF, ca)
        Q2 = sb("Q2", [128, 2, 4, 256], BF, ca)
        K1 = sb("K1", [128, 3, 4, 256], BF, ca)
        Ym = sb("Ym", [128, 2, 256], BF, ca)
        K2 = sb("K2", [128, 3, 4, 256], BF, ca)
        Vp = sb("Vp", [128, 3, 2, NH * 17 + 15], F32, ca)
        Vv = Vp[:, :, :, 0:NH * 17].rearrange("p r t (n c) -> p r t n c", c=17)
        mx = sb("mx", [128, 2, 2, NH], F32, ca)
        Mp = sb("Mp", [128, 2, NH, 32], BF, ca)
        PT = sb("PT", [128, 2, 4, 2, 384], F32, ca)
        OTs = sb("OTs", [128, 4, 256], F32, ca)
        rc = sb("rc", [128, 2, NH], F32, ca)
        wsq = sb("wsq", [128, 2, NH], F32, ca)
        On = sb("On", [128, 2, NH, 16], F32, ca)
        Mm = sb("Mm", [128, 2, 2, 256], F32, ca)
        Cn = sb("Cn", [128, 1, 2, 256], F32, ca)
        WQf = PT[:, :, :, :, :].rearrange("p a j g c -> p (a j g c)")[:, 0:2560].rearrange("p (k c) -> p k c", k=2)
        WO = OTs[:, 0:2, :]
        wtmp = OTs[:, 2, :]
        SPL = sb("SPL", [128, 1, 2048], BF, ca)

        t_w = SP.dma(l_w, lambda e: e.dma_start(WQf, wqkv))
        l_wo = lane("l_wo")
        t_wo = SP.dma(l_wo, lambda e: e.dma_start(WO, wout.rearrange("(k p) d -> p k d", p=128)))

        t_half = PO.op(lambda e: e.memset(mhalf[:, :], -0.5))
        t_vz = PO.op(lambda e: e.memset(Vp[:, :, :, :], 0.0))
        t_mpz = PO.op(lambda e: e.memset(Mp[:, :, :, :], 0.0))
        PO.wait(t_vz)
        t_vz = PO.op(lambda e: e.memset(Vv[:, :, :, :, 16:17].rearrange("p r t n c -> p (r t) (n c)"), 1.0))
        PO.op(lambda e: e.memset(onesb[:, :], 1.0))
        t_ones = PO.op(lambda e: e.memset(onesf[:, :], 1.0))
        DV.wait(t_c)
        DV.op(lambda e: e.tensor_copy(idb[:, :], idf))
        DV.op(lambda e: e.tensor_copy(mkb[:, :], CF[:, C_MASK:C_MASK + 128]))
        t_cb = DV.op(lambda e: e.tensor_copy(Ub[:, :], CF[:, C_U:C_U + 128]))
        AC.wait(t_w)
        t_wh = AC.op(lambda e: e.activation(WQh[:, :, :], WQf, ACT.Copy))
        DV.wait(t_wh, t_w)
        t_wl = DV.op(lambda e: e.tensor_tensor(WQl[:, :, :], WQf, WQh[:, :, :], ALU.subtract))
        DV.wait(t_wg)
        t = DV.op(lambda e: e.tensor_tensor(WGf[:, :, 16:32], WGf[:, :, 16:32], WGf[:, :, 32:48], ALU.add))
        DV.wait(t)
        DV.op(lambda e: e.tensor_copy(WGs[:, :, 0, 0:32], WGf[:, :, 0:32]))
        t = DV.op(lambda e: e.tensor_copy(WGs[:, :, 0, 32:40], WGf[:, :, 48:56]))
        DV.wait(t)
        DV.op(lambda e: e.tensor_tensor(WGs[:, :, 1, 0:32], WGf[:, :, 0:32], WGs[:, :, 0, 0:32], ALU.subtract))
        DV.op(lambda e: e.tensor_tensor(WGs[:, :, 1, 32:40], WGf[:, :, 48:56], WGs[:, :, 0, 32:40], ALU.subtract))
        t_gn = DV.op(lambda e: e.tensor_scalar(GN[:, :], GN[:, :], 1.0, None, ALU.add))
        t_wgs = t_gn
        PO.op(lambda e: e.memset(wtmp, 1.0))
        t_w1 = PO.now()
        PE.wait(t_w1, t_wo)
        PE.op(lambda e: e.matmul(banks[0][:, 0:256], OTs[:, 2, 0:128], OTs[:, 0, :], start=True, stop=False), False)
        t_ws = PE.op(lambda e: e.matmul(banks[0][:, 0:256], OTs[:, 2, 0:128], OTs[:, 1, :], start=False, stop=True))
        DV.wait(t_ws)
        for tt in range(2):
            selv = CF[:, C_SEL + 16 * tt:C_SEL + 16 * tt + 16].rearrange("p (a s) -> p a s", a=1).broadcast_to([128, 16, 16])
            t = DV.op(lambda e, selv=selv: e.tensor_tensor(
                wtmp.rearrange("p (n s) -> p n s", s=16), banks[0][:, 0:256].rearrange("p (n s) -> p n s", s=16),
                selv, ALU.mult))
            DV.wait(t)
            t = DV.op(lambda e, tt=tt: e.tensor_reduce(wsq[:, tt, :], wtmp.rearrange("p (n s) -> p n s", s=16), AX.X, ALU.add))
            DV.wait(t)
        t_b0 = t
        t_wsq = t

        l_st = [lane("l_st0"), lane("l_st1")]
        stg_free = [None, None]
        chunk_n = [0]

        def chunk(dst, src, width, c):
            i = chunk_n[0] % 2
            chunk_n[0] += 1
            SP.wait(stg_free[i])
            tl = SP.dma(l_st[i], lambda e: e.dma_start(STG[:, i, :], src[:, 512 * c:512 * c + 512]))
            v = dst[:, 1024 * c:1024 * c + 1024].rearrange("p (a h w) -> p a h w", h=2, w=width)
            s = STG[:, i, :].rearrange("p (a w) -> p a w", w=width)
            return i, tl, v, s

        def split(c4):
            i, tl, v, s = c4
            PO.wait(tl)
            t = PO.op(lambda e: e.tensor_copy(v[:, :, 0, :], s))
            PO.wait(t)
            stg_free[i] = PO.op(lambda e: e.tensor_tensor(v[:, :, 1, :], s, v[:, :, 0, :], ALU.subtract))

        ringW_free = [t_b0, None]
        ringW_n = [0]

        def wbank(need_pe=True):
            i = ringW_n[0] % 2
            ringW_n[0] += 1
            PE.wait(ringW_free[i])
            return i, ringW[i]

        stat_n = [0]

        def layernorm(src, dst, eng, *toks):
            k = stat_n[0] % 2
            stat_n[0] += 1
            s6, mv = stat[:, k, 0, 0:6], stat[:, k, 1, 0:2]
            DV.wait(*toks, stat_free[k])
            t = DV.op(lambda e: e.bn_stats(s6, src))
            DV.wait(t)
            t = DV.op(lambda e: e.bn_aggr(mv, s6))
            DV.wait(t)
            t = DV.op(lambda e: e.tensor_scalar(stat[:, k, 1, 3:4], stat[:, k, 1, 1:2], 1e-5, None, ALU.add))
            PO.wait(t, t_half)
            t = PO.op(lambda e: e.tensor_tensor(stat[:, k, 1, 2:3], stat[:, k, 1, 3:4], mhalf[:, 0:1], ALU.pow))
            eng.wait(t, *toks)
            t = eng.op(lambda e: e.tensor_scalar(dst, src, stat[:, k, 1, 0:1], stat[:, k, 1, 2:3], ALU.subtract, ALU.mult))
            stat_free[k] = t
            return t
        stat_free = [None, None]

        def transpose_pair(src2, toks):
            i, bank = wbank()
            PE.wait(*toks, t_c)
            for tt in range(2):
                for dk in range(2):
                    t = PE.op(lambda e, tt=tt, dk=dk: e.transpose(
                        bank[:, 256 * dk + 128 * tt:256 * dk + 128 * tt + 128], src2[tt][:, 128 * dk:128 * dk + 128], idf),
                        tt == 1 and dk == 1)
            return i, bank, t

        def split_T(i, bank, t, hi, lo, *free):
            bv = bank[:, :].rearrange("p (k c) -> p k c", k=2)
            AC.wait(t, *free)
            th = AC.op(lambda e: e.activation(hi, bv, ACT.Copy))
            DV.wait(th)
            tl = DV.op(lambda e: e.tensor_tensor(lo, bv, hi, ALU.subtract))
            ringW_free[i] = tl
            return tl

        a = [dict() for _ in range(B)]

        ym_free = [None]

        def A1(b):
            r, r3 = b % 2, b % 3
            s = a[b]
            xt = [XB[:, 2 * b + tt, 0:256] for tt in range(2)]
            free = a[b - 1]["xT_done"] if b >= 1 else None
            PO.wait(free)
            tn = [layernorm(xt[tt], xn[:, 0, tt, :], PO, t_x[b // 4]) for tt in range(2)]
            tp = transpose_pair([xn[:, 0, 0, :], xn[:, 0, 1, :]], tn)
            s["xT_done"] = tp[2]
            tl = split_T(*tp, xTh[:, r, :, :], xTl[:, r, :, :], a[b - 2]["proj"] if b >= 2 else None)
            PE.wait(tl, t_wl)

            def proj(col, g2):
                i, bank = wbank()
                for gg in range(2):
                    c = col + 128 * (2 * g2 + gg)
                    n = 0
                    for dk in range(2):
                        for w, v in ((WQh, xTh), (WQh, xTl), (WQl, xTh)):
                            t = PE.op(lambda e, w=w, v=v, dk=dk, c=c, gg=gg, n=n: e.matmul(
                                bank[:, 256 * gg:256 * gg + 256], w[:, dk, c:c + 128], v[:, r, dk, :],
                                start=n == 0, stop=n == 5), n == 5 and gg == 1)
                            n += 1
                return i, bank, t

            tq1 = []
            for g2 in range(2):
                i, bank, t = proj(0, g2)
                bv = bank[:, :].rearrange("p (g c) -> p g c", g=2)
                gs = slice(2 * g2, 2 * g2 + 2)
                AC.wait(t, a[b - 2]["Q2"] if b >= 2 else None)
                th = AC.op(lambda e, bv=bv, gs=gs: e.activation(Qh[:, r, gs, :], bv, ACT.Copy))
                DV.wait(th, a[b - 3]["ST"] if b >= 3 else None)
                t = DV.op(lambda e, bv=bv, gs=gs: e.scalar_tensor_tensor(
                    Q1[:, r3, gs, :], Qh[:, r, gs, :], m1n, bv, ALU.mult, ALU.add))
                ringW_free[i] = t
            s["Q1"] = t
            for g2 in range(2):
                i, bank, t = proj(512, g2)
                bv = bank[:, :].rearrange("p (g c) -> p g c", g=2)
                gs = slice(2 * g2, 2 * g2 + 2)
                AC.wait(t, a[b - 3]["ST"] if b >= 3 else None)
                th = AC.op(lambda e, bv=bv, gs=gs: e.activation(K1[:, r3, gs, :], bv, ACT.Copy))
                DV.wait(th, ym_free[0])
                ty = DV.op(lambda e, gs=gs: e.tensor_scalar(Ym[:, :, :], K1[:, r3, gs, :], m0, c17, ALU.mult, ALU.subtract))
                DV.wait(ty)
                t = DV.op(lambda e, bv=bv, gs=gs: e.scalar_tensor_tensor(
                    K2[:, r3, gs, :], bv, m0, Ym[:, :, :], ALU.mult, ALU.subtract))
                ym_free[0] = t
                ringW_free[i] = t
            s["K1"], s["K2"] = th, t
            i, bank = wbank()
            for tt in range(2):
                n = 0
                for dk in range(2):
                    for w, v in ((WQh, xTh), (WQl, xTh), (WQh, xTl)):
                        t = PE.op(lambda e, w=w, v=v, dk=dk, tt=tt, n=n: e.matmul(
                            bank[:, 256 * tt:256 * tt + 256], v[:, r, dk, 128 * tt:128 * tt + 128], w[:, dk, 1024:1280],
                            start=n == 0, stop=n == 5), n == 5 and tt == 1)
                        n += 1
            s["proj"] = t
            AC.wait(t, t_vz, a[b - 3]["PV"] if b >= 3 else None)
            s["V"] = ringW_free[i] = AC.op(lambda e, bank=bank: e.activation(
                Vv[:, r3, :, :, 0:16], bank[:, :].rearrange("p (t n h) -> p t n h", t=2, h=16), ACT.Copy))

        mring, mring_free, mring_n = [banks[0], banks[1]], [t_b0, None], [0]
        sring, sring_free, sring_n = [banks[2], banks[3]], [None, None], [0]

        def take(ring, free, n):
            i = n[0] % 2
            n[0] += 1
            PE.wait(free[i])
            return i, ring[i]

        def run_jobs(*jobs):
            jobs = [j for j in jobs if j is not None]
            left = [list(j[0]) for j in jobs]
            toks = [None] * len(jobs)
            while any(left):
                for n, l in enumerate(left):
                    if l:
                        fn = l.pop(0)
                        toks[n] = PE.op(fn, not l)
            for j, t in zip(jobs, toks):
                j[1](t)

        def A2u(b, P, u, j):
            r, r3 = b % 2, b % 3
            s = a[b]
            PE.wait(s["Q1"], s["K1"], t_cb)
            DV.wait(a[b - 2]["mp"] if b >= 2 else None)
            i, bank = take(mring, mring_free, mring_n)
            w = 256 if u == 0 else 128
            q0 = 128 if u == 0 else 0
            tt = 1 - u
            bv = bank[:, 0:2 * w].rearrange("p (g c) -> p g c", g=2)
            pr = slice(32 * j, 32 * j + 32)
            ops = [lambda e: e.matmul(
                bv[:, :, w - 128:w], idb[:, :], mkb[:, :].rearrange("p (a c) -> p a c", a=1).broadcast_to([128, 2, 128]),
                start=True, stop=False, skip_group_check=True)]
            for gg in range(2):
                ops.append(lambda e, gg=gg: e.matmul(
                    bank[:, w * gg:w * gg + w], Q1[pr, r3, 2 * P + gg, q0:q0 + 128], K1[pr, r3, 2 * P + gg, 0:w],
                    start=False, stop=gg == 1, skip_group_check=True))

            def post(t):
                DV.wait(t)
                mring_free[i] = s["mx"] = DV.op(lambda e: e.tensor_reduce(
                    mx[:, r, tt, :].rearrange("p (g c) -> p g c", c=4)[:, 2 * P:2 * P + 2, j], bv, AX.X, ALU.max))
            return ops, post

        def A2e(b):
            r = b % 2
            s = a[b]
            DV.wait(s["mx"], t_mpz, a[b - 1]["mpT"] if b >= 1 else None)
            t = DV.op(lambda e: e.tensor_scalar(Mp[:, :, :, 16], mx[:, r, :, :], -1.0, None, ALU.mult))
            DV.wait(t)
            t = DV.op(lambda e: e.scalar_tensor_tensor(Mp[:, :, :, 17], mx[:, r, :, :], -1.0, Mp[:, :, :, 16], ALU.mult, ALU.subtract))
            s["mp"] = t
            i, bank = wbank()
            bb = bank[:, :].bitcast(BF)
            PE.wait(t)
            for g in range(4):
                for tt in range(2):
                    t = PE.op(lambda e, g=g, tt=tt: e.transpose(
                        bb[:, 256 * g + 128 * tt:256 * g + 128 * tt + 128],
                        Mp[:, tt, 4 * g:4 * g + 4, :].rearrange("p n c -> p (n c)"), idb[:, :]), g == 3 and tt == 1)
            s["mpT"] = t
            DV.wait(t, a[b - 2]["ST"] if b >= 2 else None)
            t = DV.op(lambda e: e.scalar_tensor_tensor(
                Q2[:, r, :, :].rearrange("p g c -> p (g c)"), Qh[:, r, :, :].rearrange("p g c -> p (g c)"), m0, bb, ALU.mult, ALU.add))
            ringW_free[i] = s["Q2"] = t

        pt_n = [0]
        pt_free = [None, None]
        otb = banks[4]
        ot_free = [None]

        def A3u(b, P, u, j):
            r, r3 = b % 2, b % 3
            s = a[b]
            p = P
            PE.wait(s["Q2"], s["K2"], s["Q1"])
            i, bank = take(sring, sring_free, sring_n)
            w = 256 if u == 0 else 128
            q0, k0 = 256 - w, 128 * u
            pr = slice(32 * j, 32 * j + 32)
            ops = []
            for gg in range(2):
                for n, (kk, qq, rq) in enumerate(((K1, Q1, r3), (K2, Q2, r))):
                    ops.append(lambda e, n=n, kk=kk, qq=qq, rq=rq, gg=gg: e.matmul(
                        bank[:, w * gg:w * gg + w], kk[pr, r3, 2 * P + gg, k0:k0 + 128], qq[pr, rq, 2 * P + gg, q0:256],
                        start=n == 0, stop=n == 1))

            def post(t):
                AC.wait(t, pt_free[p], t_wl)
                dst = PT[:, p, j, :, 0:256] if u == 0 else PT[:, p, j, :, 256:384]
                t1 = AC.op(lambda e: e.activation(dst, bank[:, 0:2 * w].rearrange("p (j c) -> p j c", c=w), ACT.Exp, scale=0.25))
                sring_free[i] = t1
                dg = dst[:, :, 0:128]
                PO.wait(t1)
                s["PT", P] = PO.op(lambda e: e.affine_select(
                    out=dg, in_=dg, pattern=[[0, 2], [1, 128]], compare_op=ALU.is_ge, fill=0.0, base=0, channel_multiplier=-1))
                s["ST"] = t
            return ops, post

        def A3v(b, g):
            r3 = b % 3
            s = a[b]
            p, gg = g // 2, g % 2
            if gg == 0:
                PE.wait(ot_free[0])
            PE.wait(s["PT", p], s["V"])
            for kt in range(2):
                for j in range(4):
                    c = 17 * (4 * g + j)
                    t = PE.op(lambda e, kt=kt, j=j, c=c: e.matmul(
                        otb[32 * j:32 * j + 32, 256 * gg + 128 * kt:256 * gg + 256], Vp[:, r3, kt, c:c + 32],
                        PT[:, p, j, gg, 0:256] if kt == 0 else PT[:, p, j, gg, 256:384], start=kt == 0, stop=kt == 1),
                        kt == 1 and j == 3)
            if gg == 1:
                pt_free[p] = t
                AC.wait(t, t_wsq, a[b - 1]["otT"] if b >= 1 else None)
                ot_free[0] = AC.op(lambda e: e.activation(
                    OTs[:, g - 1:g + 1, :], otb[:, :].rearrange("p (g c) -> p g c", g=2), ACT.Copy))
                s["OTs"] = ot_free[0]
            if g == 3:
                s["PV"] = t

        l_o = [lane("l_o0"), lane("l_o1")]
        l_m = [lane("l_m0"), lane("l_m1")]

        def A4(b):
            s = a[b]
            for tt in range(2):
                i, bank = wbank()
                PE.wait(s["OTs"])
                for g in range(4):
                    t = PE.op(lambda e, g=g, tt=tt, bank=bank: e.transpose(
                        bank[:, 128 * g:128 * g + 128], OTs[:, g, 128 * tt:128 * tt + 128], idf), g == 3)
                bv = bank[:, :].rearrange("p (n c) -> p n c", c=32)
                DV.wait(t, a[b - 1]["ost", tt] if b >= 1 else None)
                t2 = DV.op(lambda e, tt=tt, bv=bv: e.reciprocal(rc[:, tt, :], bv[:, :, 16]))
                DV.wait(t2, t_wsq)
                t2 = DV.op(lambda e, tt=tt: e.tensor_tensor(rc[:, tt, :], rc[:, tt, :], wsq[:, tt, :], ALU.mult))
                DV.wait(t2)
                t2 = DV.op(lambda e, tt=tt, bv=bv: e.tensor_tensor(
                    On[:, tt, :, :], bv[:, :, 0:16], rc[:, tt, :].rearrange("p (n a) -> p n a", a=1).broadcast_to([128, NH, 16]),
                    ALU.mult))
                ringW_free[i] = t2
            s["otT"] = t
            SP.wait(t2)
            r = b % 2
            for tt in range(2):
                to = SP.dma(l_o[tt], lambda e, tt=tt: e.dma_start(
                    osc[b, :].rearrange("(n q h) -> q n h", n=NH, h=16)[128 * tt:128 * tt + 128, :, :], On[:, tt, :, :]))
                s["ost", tt] = to
            pass

        def A4b(b):
            s = a[b]
            r = b % 2
            SP.wait(s["ost", 0], s["ost", 1], a[b - 2]["mT"] if b >= 2 else None)
            s["M"] = SP.dma(l_m[r], lambda e: e.dma_start(Mm[:, r, :, :], osc[b, :].rearrange("(k p s) -> p k s", p=128, s=256)))

        def A5(b):
            s = a[b]
            r = b % 2
            i, bank = wbank()
            PE.wait(s["M"])
            for dk in range(2):
                for tt in range(2):
                    t = PE.op(lambda e, dk=dk, tt=tt: e.transpose(
                        bank[:, 256 * tt + 128 * dk:256 * tt + 128 * dk + 128], Mm[:, r, dk, 128 * tt:128 * tt + 128], idf),
                        dk == 1 and tt == 1)
            s["mT"] = t
            DV.wait(t)
            xx = XB[:, 2 * b:2 * b + 2, 0:256]
            s["x1"] = ringW_free[i] = DV.op(lambda e: e.tensor_tensor(
                xx, bank[:, :].rearrange("p (t c) -> p t c", t=2), xx, ALU.add))

        l_cx = [lane("l_cx0")]
        l_sp = [lane("l_sp0"), lane("l_sp1")]

        def A6l(b):
            r = 0
            SP.wait(a[b - 1]["cT"] if b >= 1 else None)
            a[b]["cx"] = SP.dma(l_cx[r], lambda e: e.dma_start(Cn[:, r, :, :], ctx_in[b].rearrange("(t p) d -> p t d", p=128)))

        def A6(b):
            s = a[b]
            r = b % 2
            prev = a[b - 1] if b >= 1 else {}
            rn = b % 2
            PO.wait(prev.get("qT"))
            tn = [layernorm(XB[:, 2 * b + tt, 0:256], QN[:, tt, :], PO, s["x1"]) for tt in range(2)]
            v = SPL[:, 0, :].rearrange("p (s h k c) -> p s h k c", s=2, h=2, k=2)
            tp = transpose_pair([Cn[:, 0, 0, :], Cn[:, 0, 1, :]], [s["cx"]])
            s["cT"] = tp[2]
            fr = (a[b - 1]["spl"], a[b - 1]["gate"]) if b >= 1 else ()
            tc = split_T(*tp, v[:, 1, 0, :, :], v[:, 1, 1, :, :], *fr)
            tp = transpose_pair([QN[:, 0, :], QN[:, 1, :]], tn)
            s["qT"] = tp[2]
            tq = split_T(*tp, v[:, 0, 0, :, :], v[:, 0, 1, :, :], *fr)
            SP.wait(tc, tq)
            s["spl"] = SP.dma(l_sp[r], lambda e: e.dma_start(qsc[b], SPL[:, 0, :]))
            PE.wait(tc, tq, t_wgs)
            for tt in range(2):
                n = 0
                c = 16 * (2 * b + tt)
                for sx in range(2):
                    for dk in range(2):
                        for hx, hw in ((0, 0), (0, 1), (1, 0)):
                            t = PE.op(lambda e, sx=sx, dk=dk, hx=hx, hw=hw, tt=tt, n=n, c=c: e.matmul(
                                gates[:, c:c + 16], v[:, sx, hx, dk, 128 * tt:128 * tt + 128],
                                WGs[:, dk, hw, 16 * sx:16 * sx + 16], start=n == 0, stop=n == 11), n == 11 and tt == 1)
                            n += 1
            s["gate"] = t

        QN = sb("QN", [128, 2, 256], F32, ca)
        zfill = sb("zfill", [128, ROW], F32, ca)
        t_z = PO.op(lambda e: e.memset(zfill[:, :], 0.0))
        l_z = lane("l_z")
        for i in range(1, 4):
            load_x(i)
        SP.wait(t_z)
        t_zf = None
        t_zf = SP.dma(l_z, lambda e: e.dma_start(
            xs.rearrange("(n p) c -> p n c", p=128),
            zfill[:, :].rearrange("p (a c) -> p a c", a=1).broadcast_to([128, NTILE, ROW])))
        t_zf = SP.dma(l_z, lambda e: e.dma_start(out[TOK:TOK + 128, :], zfill[:, 0:256]))

        wchunk = [0]

        def prep(dst, src, width, n):
            cs = []
            for _ in range(n):
                if wchunk[0] < 32:
                    cs.append(chunk(dst, src, width, wchunk[0]))
                    wchunk[0] += 1
            return cs

        for i in range(B + 4):
            pend = prep(WU, wup, 128, 2) if i < B else []
            for P in range(2):
                for n in range(8):
                    u, j = n // 4, n % 4
                    run_jobs(A2u(i - 1, P, u, j) if 0 <= i - 1 < B else None,
                             A3u(i - 2, P, u, (j + 2) % 4) if 0 <= i - 2 < B else None)
                    if P == 1 and n in (2, 5) and 0 <= i - 2 < B:
                        A3v(i - 2, n // 3)
            if i < B:
                A1(i)
            if 0 <= i - 2 < B:
                A3v(i - 2, 2)
                A3v(i - 2, 3)
            if 0 <= i - 1 < B:
                A2e(i - 1)
            for c in pend:
                split(c)
            if 0 <= i - 3 < B:
                A5(i - 3)
                A6(i - 3)
            if 0 <= i - 2 < B:
                A4(i - 2)
                A4b(i - 2)
                A6l(i - 2)
        pend = []
        for c in pend:
            split(c)

        def barrier():
            toks = [q.now() for q in (PE, DV, AC, PO)]
            for q in (PE, DV, AC, PO, SP):
                q.wait(*toks)

        barrier()
        for q in (DV, AC, PE, PO):
            q.wait(*[a[b]["spl"] for b in (B - 2, B - 1)], *[a[b]["ost", k] for b in (B - 1,) for k in (0, 1)], t_zf)
        ca.close()

        WD = sb("WD", [128, E * 4096], BF)
        cg = ExitStack()
        G = sb("G", [128, NT, 16], F32, cg)
        gi = sb("gi", [128, 256], F32, cg)
        gf = sb("gf", [128, 256], F32, cg)
        zz = sb("zz", [128, 256], F32, cg)
        cs_ = sb("cs_", [128, 256], F32, cg)
        gg_ = sb("gg_", [128, 256], F32, cg)
        MM = sb("MM", [128, 256], F32, cg)
        r1 = sb("r1", [128, 2, 256], F32, cg)
        pp = sb("pp", [128, 6, 256], BF, cg)

        DV.op(lambda e: e.memset(zz[:, :], 0.0))
        t = DV.op(lambda e: e.tensor_tensor(
            G[:, :, :], gates[:, :].rearrange("p (t c) -> p t c", c=16),
            BG[:, 0:16].rearrange("p (a c) -> p a c", a=1).broadcast_to([128, NT, 16]), ALU.add))
        AC.wait(t)
        t = AC.op(lambda e: e.activation(G[:, :, :], G[:, :, :], ACT.Tanh, scale=1.0 / 15.0))
        PE.wait(t)
        Gv = G[:, :, :].rearrange("p (b t) (k h) -> p t k b h", t=2, h=8)
        GT = sb("GT", [128, 4, 128], F32, cg)
        DV.wait(t)
        for k in range(2):
            for tt in range(2):
                t = DV.op(lambda e, k=k, tt=tt: e.tensor_scalar(
                    GT[:, 2 * k + tt, :].rearrange("p (b h) -> p b h", h=8), Gv[:, tt, k, :, :], 15.0, None, ALU.mult))
        PE.wait(t)
        for k in range(4):
            t = PE.op(lambda e, k=k: e.transpose(banks[0][:, 128 * k:128 * k + 128], GT[:, k, :], idf), k == 3)
        DV.wait(t)
        t = DV.op(lambda e: e.tensor_copy(gi[:, :], banks[0][:, 0:256]))
        AC.wait(t)
        t = AC.op(lambda e: e.activation(gf[:, :], banks[0][:, 256:512], ACT.Exp, scale=-1.0))
        AC.wait(t)
        t = AC.op(lambda e: e.activation(gf[:, :], gf[:, :], ACT.Ln, bias=1.0))
        DV.wait(t)
        t = DV.op(lambda e: e.tensor_tensor_scan(cs_[:, :], gf[:, :], zz[:, :], 0.0, ALU.add, ALU.add))
        DV.wait(t)
        t = DV.op(lambda e: e.tensor_tensor(gg_[:, :], gi[:, :], cs_[:, :], ALU.add))
        DV.wait(t)
        t = DV.op(lambda e: e.tensor_tensor_scan(MM[:, :], gg_[:, :], gg_[:, :], NEG, ALU.max, ALU.max))
        DV.wait(t)
        t = DV.op(lambda e: e.tensor_tensor(cs_[:, :], cs_[:, :], MM[:, :], ALU.subtract))
        AC.wait(t)
        t_em = AC.op(lambda e: e.activation(cs_[:, :], cs_[:, :], ACT.Exp))
        PE.wait(t_em)
        for tt in range(2):
            t_em = PE.op(lambda e, tt=tt: e.transpose(banks[1][:, 128 * tt:128 * tt + 128], cs_[:, 128 * tt:128 * tt + 128], idf), tt == 1)
        DV.op(lambda e: e.tensor_scalar(MM[:, :], MM[:, :], -1.0, None, ALU.mult))
        DV.wait(DV.now())
        for k, src in enumerate((gg_, MM)):
            DV.op(lambda e, k=k, src=src: e.tensor_copy(pp[:, 3 * k, :], src[:, :]))
            DV.wait(DV.now())
            DV.op(lambda e, k=k, src=src: e.tensor_tensor(r1[:, 0, :], src[:, :], pp[:, 3 * k, :], ALU.subtract))
            DV.wait(DV.now())
            DV.op(lambda e, k=k: e.tensor_copy(pp[:, 3 * k + 1, :], r1[:, 0, :]))
            DV.wait(DV.now())
            DV.op(lambda e, k=k: e.tensor_tensor(r1[:, 1, :], r1[:, 0, :], pp[:, 3 * k + 1, :], ALU.subtract))
            DV.wait(DV.now())
            DV.op(lambda e, k=k: e.tensor_copy(pp[:, 3 * k + 2, :], r1[:, 1, :]))
            DV.wait(DV.now())
        t = DV.now()
        l_g = lane("l_g")
        SP.wait(t)
        t_g = SP.dma(l_g, lambda e: e.dma_start(gsc.rearrange("k p c -> p k c"), pp[:, :, :]))
        DV.wait(t_em)
        t_em = DV.op(lambda e: e.tensor_copy(EM[:, :, :], banks[1][:, 0:256].rearrange("p (t c) -> p t c", t=2)))
        barrier()
        for q in (PE, DV, AC, PO, SP):
            q.wait(t_g)
        cg.close()

        cb = ExitStack()
        QC = sb("QC", [128, 2, 2048], BF, cb)
        LH = WD[0:6, 24576:28672].rearrange("p (r h c) -> p r h c", r=2, h=8)
        RH = WD[0:6, 28672:32768].rearrange("p (r h c) -> p r h c", r=2, h=8)
        CX = sb("CX", [128, 2, 2, 256], F32, cb)
        Es = sb("Es", [128, 2, 512], F32, cb)
        SD = sb("SD", [128, 6, 512], F32, cb)
        dsel = sb("dsel", [128, 2, 32], F32, cb)
        OB = sb("OB", [128, 768], F32, cb)
        sq = sb("sq", [128, 256], F32, cb)
        sm = sb("sm", [128, 5, 8], F32, cb)
        hh = sb("hh", [128, 256], F32, cb)
        x3T = sb("x3T", [128, 2, 2, 256], BF, cb)

        PO.op(lambda e: e.memset(WD[0:6, 24576:28672], 1.0))
        t_lr = PO.op(lambda e: e.memset(WD[0:6, 28672:32768], 1.0))
        PO.op(lambda e: e.memset(dsel[:, :, :], 0.0))
        PO.wait(PO.now())
        PO.op(lambda e: e.memset(dsel[:, 0, 0:1], 1.0))
        t_ds = PO.op(lambda e: e.memset(dsel[:, 1, 1:2], 1.0))

        l_qc = [lane(f"l_qc{k}") for k in range(2)]
        l_lh = [lane(f"l_lh{k}") for k in range(2)]
        l_rh = [lane(f"l_rh{k}") for k in range(2)]
        l_cb = [lane(f"l_cb{k}") for k in range(2)]
        bb_ = [dict() for _ in range(B)]

        def B1(b):
            r = b % 2
            s = bb_[b]
            p = bb_[b - 2] if b >= 2 else {}
            SP.wait(p.get("S"), p.get("PV"), t_g)
            s["qc"] = SP.dma(l_qc[r], lambda e: e.dma_start(QC[:, r, :], qsc[b]))
            s["cx"] = SP.dma(l_cb[r], lambda e: e.dma_start(CX[:, r, :, :], ctx_in[b].rearrange("(t p) d -> p t d", p=128)))

        def B1g(b):
            s = bb_[b]
            r = b % 2
            SP.wait(bb_[b - 2]["D"] if b >= 2 else None, t_lr, t_g)
            s["lh"] = SP.dma(l_lh[r], lambda e: e.dma_start(LH[0:3, r, :, :], gsc[0:3, 8 * b:8 * b + 8, :]))
            s["rh"] = SP.dma(l_rh[r], lambda e: e.dma_start(RH[3:6, r, :, :], gsc[3:6, 8 * b:8 * b + 8, :]))

        sdb, sdb_free = [(banks[0], banks[1]), (banks[2], banks[3])], [None, None]
        es_free, sd_free = [None, None], [None] * 6
        un = [0]
        ob, den, tb = banks[4], banks[5], banks[6]
        lgb = banks[7]
        ob_free, den_free, tb_free = [None], [None], [None]

        def B2u(b, st, j):
            r = b % 2
            s = bb_[b]
            k2, k6 = un[0] % 2, un[0] % 6
            un[0] += 1
            sbk, dbk = sdb[k2]
            w = 256 if st == 0 else 128
            t0, s0 = 256 - w, 128 * st
            v = QC[:, r, :].rearrange("p (s h k c) -> p s h k c", s=2, h=2, k=2)
            PE.wait(sdb_free[k2], s["qc"], s["lh"], s["rh"])
            pr = slice(32 * j, 32 * j + 32)
            dops, sops = [], []
            for dk in range(2):
                dops.append(lambda e, dk=dk: e.matmul(
                    dbk[:, w * dk:w * dk + w], LH[0:6, r, 4 * dk + j, s0:s0 + 128], RH[0:6, r, 4 * dk + j, t0:256],
                    start=True, stop=True))
                for n, (hc, hq) in enumerate(((0, 0), (0, 1), (1, 0))):
                    sops.append(lambda e, dk=dk, n=n, hc=hc, hq=hq: e.matmul(
                        sbk[:, w * dk:w * dk + w], v[pr, 1, hc, dk, s0:s0 + 128], v[pr, 0, hq, dk, t0:256],
                        start=n == 0, stop=n == 2))

            def dpost(t):
                s["D"] = t
                AC.wait(t, es_free[k2])
                s["te"] = AC.op(lambda e: e.activation(Es[:, k2, 0:2 * w], dbk[:, 0:2 * w], ACT.Exp))

            def spost(t):
                s["S"] = t
                DV.wait(s["te"], t, sd_free[k6])
                t1 = DV.op(lambda e: e.tensor_tensor(SD[:, k6, 0:2 * w], sbk[:, 0:2 * w], Es[:, k2, 0:2 * w], ALU.mult))
                sdb_free[k2] = es_free[k2] = t1
                PO.wait(t1)
                dg = SD[:, k6, 0:2 * w].rearrange("p (j c) -> p j c", c=w)[:, :, 0:128]
                s["SD", st, j] = (k6, PO.op(lambda e: e.affine_select(
                    out=dg, in_=dg, pattern=[[0, 2], [1, 128]], compare_op=ALU.is_ge, fill=0.0, base=0, channel_multiplier=-1)))
            run_jobs((dops, dpost), (sops, spost))

        def B2v(b, st):
            r = b % 2
            s = bb_[b]
            if st == 0:
                PE.wait(ob_free[0], den_free[0], t_ds, s["cx"])
            w = 256 if st == 0 else 128
            o0 = 256 - w
            sl = [s["SD", st, j][0] for j in range(4)]
            PE.wait(*[s["SD", st, j][1] for j in range(4)])
            for dk in range(2):
                for j in range(4):
                    PE.op(lambda e, j=j, dk=dk: e.matmul(
                        ob[32 * j:32 * j + 32, 256 * dk + o0:256 * dk + 256], CX[:, r, st, 128 * dk + 32 * j:128 * dk + 32 * j + 32],
                        SD[:, sl[j], w * dk:w * dk + w], start=st == 0 and dk == 0, stop=st == 1 and dk == 1,
                        skip_group_check=True), False)
            for dk in range(2):
                for j in range(4):
                    t = PE.op(lambda e, j=j, dk=dk: e.matmul(
                        den[32 * j:32 * j + 32, o0:256], dsel[:, dk, :], SD[:, sl[j], w * dk:w * dk + w],
                        start=dk == 0 and st == 0, stop=dk == 1 and st == 1,
                        skip_group_check=True), dk == 1 and j == 3)
            for j in range(4):
                sd_free[sl[j]] = t
            s["PV"] = t

        l_x2 = [lane(f"l_x2{k}") for k in range(2)]
        ISQ = float(1.0 / (32.0 ** 0.5))

        def B3(b):
            s = bb_[b]
            r = b % 2
            prev = bb_[b - 1] if b >= 1 else {}
            AC.wait(s["PV"], prev.get("obT"))
            ob_free[0] = AC.op(lambda e: e.activation(OB[:, 0:512], ob[:, :], ACT.Copy))
            den_free[0] = t = AC.op(lambda e: e.activation(OB[:, 512:768], den[:, 0:256], ACT.Copy))
            s["ob"] = t

        def B4(b):
            s = bb_[b]
            r = b % 2
            def half(tt):
                PE.wait(s["ob"], tb_free[0])
                for k in range(2):
                    PE.op(lambda e, k=k: e.transpose(tb[:, 128 * k:128 * k + 128], OB[:, 256 * k + 128 * tt:256 * k + 128 * tt + 128], idf), False)
                t = PE.op(lambda e: e.transpose(tb[:, 256:384], OB[:, 512 + 128 * tt:640 + 128 * tt], idf))
                DV.wait(t)
                o = tb[:, 0:256]
                dv = tb[:, 256:384].rearrange("p (j c) -> p c j", c=32)[:, 0:2, :]
                em = EM[:, tt, 8 * b:8 * b + 8].rearrange("p (k j) -> p k j", k=2)
                smv = [sm[:, k, :].rearrange("p (k j) -> p k j", k=2) for k in range(5)]
                DV.wait(DV.now())
                t = DV.op(lambda e: e.tensor_scalar(smv[4], dv, ISQ, None, ALU.mult))
                DV.wait(t)
                t_dv = t = DV.op(lambda e: e.scalar_tensor_tensor(smv[0], dv, -ISQ, smv[4], ALU.mult, ALU.max))
                DV.wait(t, t_em)
                t = DV.op(lambda e, em=em: e.tensor_tensor(smv[1], smv[0], em, ALU.max))
                DV.wait(t)
                t = DV.op(lambda e: e.tensor_scalar(sm[:, 0, :], sm[:, 1, :], 5e-5, None, ALU.add))
                DV.wait(t)
                t = DV.op(lambda e: e.tensor_tensor(sm[:, 1, :], sm[:, 0, :], sm[:, 0, :], ALU.mult))
                AC.wait(t_dv)
                t_h = AC.op(lambda e, o=o: e.activation(hh[:, :], o, ACT.Copy, scale=ISQ))
                DV.wait(t_h, t)
                t = DV.op(lambda e: e.tensor_tensor(sq[:, :], hh[:, :], hh[:, :], ALU.mult))
                tb_free[0] = t
                DV.wait(t)
                t = DV.op(lambda e: e.tensor_reduce(sm[:, 2, :], sq[:, :].rearrange("p (h c) -> p h c", c=32), AX.X, ALU.add))
                DV.wait(t)
                t = DV.op(lambda e: e.tensor_scalar(sm[:, 1, :], sm[:, 1, :], 32e-6, None, ALU.mult))
                DV.wait(t)
                t = DV.op(lambda e: e.tensor_tensor(sm[:, 3, :], sm[:, 2, :], sm[:, 1, :], ALU.add))
                DV.wait(t)
                t = DV.op(lambda e: e.tensor_scalar(sm[:, 4, :], sm[:, 3, :], 1.0 / 32.0, None, ALU.mult))
                PO.wait(t)
                t = PO.op(lambda e: e.tensor_tensor(sm[:, 3, :], sm[:, 4, :], mhalf[:, :], ALU.pow))
                DV.wait(t)
                t = DV.op(lambda e: e.tensor_tensor(
                    hh[:, :].rearrange("p (h c) -> p h c", c=32), hh[:, :].rearrange("p (h c) -> p h c", c=32),
                    sm[:, 3, :].rearrange("p (h a) -> p h a", a=1).broadcast_to([128, 8, 32]), ALU.mult))
                PO.wait(t, t_gn)
                t = PO.op(lambda e: e.tensor_tensor(hh[:, :], hh[:, :], GN[:, :], ALU.mult))
                PO.wait(t)
                xx = XB[:, 2 * b + tt, 0:256]
                t = PO.op(lambda e, xx=xx: e.tensor_tensor(xx, xx, hh[:, :], ALU.add))
                AC.wait(t)
                DV.wait(t)
                return t
            x2t = [half(tt) for tt in range(2)]
            SP.wait(*x2t)
            ov = out[0:TOK, :].rearrange("(t p) d -> p t d", p=128)
            s["x2o"] = SP.dma(l_x2[r], lambda e: e.dma_start(ov[:, 2 * b:2 * b + 2, :], XB[:, 2 * b:2 * b + 2, 0:256]))
            s["x2"] = x2t[-1]

        def B5(b):
            s = bb_[b]
            r = b % 2
            PO.wait(s["x2o"])
            tn = [layernorm(XB[:, 2 * b + tt, 0:256], XB[:, 2 * b + tt, 0:256], PO, s["x2"]) for tt in range(2)]
            PE.wait(*tn, tb_free[0])
            for tt in range(2):
                for dk in range(2):
                    t = PE.op(lambda e, tt=tt, dk=dk: e.transpose(
                        tb[:, 256 * dk + 128 * tt:256 * dk + 128 * tt + 128], XB[:, 2 * b + tt, 128 * dk:128 * dk + 128], idf),
                        tt == 1 and dk == 1)
            bv = tb[:, :].rearrange("p (k c) -> p k c", k=2)
            AC.wait(t, bb_[b - 1]["lg"] if b >= 1 else None)
            th = AC.op(lambda e: e.activation(x3T[:, 0, :, :], bv, ACT.Copy))
            DV.wait(th)
            tl = DV.op(lambda e: e.tensor_tensor(x3T[:, 1, :, :], bv, x3T[:, 0, :, :], ALU.subtract))
            tb_free[0] = tl
            PE.wait(tl)
            for tt in range(2):
                n = 0
                c = 8 * (2 * b + tt)
                for dk in range(2):
                    for hx, hw in ((0, 0), (0, 1), (1, 0)):
                        t = PE.op(lambda e, dk=dk, hx=hx, hw=hw, tt=tt, n=n, c=c: e.matmul(
                            lgb[:, c:c + 8], x3T[:, hx, dk, 128 * tt:128 * tt + 128], WGs[:, dk, hw, 32:40],
                            start=n == 0, stop=n == 5), n == 5 and tt == 1)
                        n += 1
            s["lg"] = t

        wchunk[0] = 0
        pend = []
        B1(0)
        B1g(0)
        B1(1)
        B1g(1)
        todo = []
        for i in range(B + 2):
            pend = prep(WD, wdn, 256, 2) if i < B and wchunk[0] < 24 else []
            for n in range(8):
                if i < B:
                    B2u(i, n // 4, n % 4)
                if n in (0, 4) and todo:
                    B2v(*todo[0])
                    if todo[0][1] == 1:
                        B3(todo[0][0])
                    todo.pop(0)
                if n == 3 and i < B:
                    todo.append((i, 0))
                if n == 7 and i < B:
                    todo.append((i, 1))
                if n == 1:
                    for c in pend:
                        split(c)
                if n == 2 and 1 <= i < B - 1:
                    B1(i + 1)
                    B1g(i + 1)
                if n == 3 and 0 <= i - 1 < B:
                    B4(i - 1)
                if n == 6 and 0 <= i - 2 < B:
                    B5(i - 2)
        pend = []
        for c in pend:
            split(c)

        barrier()
        cb.close()

        for _ in range(4):
            for c in prep(WD, wdn, 256, 2):
                split(c)
        cr = ExitStack()
        TE = sb("TE", [128, NTILE], F32)
        TEi = sb("TEi", [128, NTILE], I32)
        names = ("lg_", "pr", "eq", "ky", "o1", "o2", "mk", "tot", "cum", "pf")
        T = {n: sb("c_" + n, [128, NT, E], F32, cr) for n in names}
        mkbt = sb("mkbt", [128, E, NT], BF, cr)
        m32 = {n: sb("c_" + n, [128, NT], F32, cr) for n in ("mx1", "sm", "k1", "w2t", "s1", "s2")}
        sl1 = sb("sl1", [128, NT], I32, cr)
        sl2 = sb("sl2", [128, NT], I32, cr)
        t8 = sb("t8", [128, 8, E], F32, cr)
        t8i = sb("t8i", [128, E], I32, cr)
        te8 = sb("te8", [128, NTILE, E], F32, cr)

        def dv(fn):
            t = DV.op(fn)
            DV.wait(t)
            return t

        def bc(x):
            return x[:, :].rearrange("p (t a) -> p t a", a=1).broadcast_to([128, NT, E])

        def cb8(x):
            return x.rearrange("p (a c) -> p a c", a=1).broadcast_to([128, NT, E])

        ek = cb8(CF[:, C_EK:C_EK + 8])
        dv(lambda e: e.tensor_tensor(T["lg_"][:, :, :], lgb[:, 0:256].rearrange("p (t c) -> p t c", c=8), cb8(BG[:, 16:24]), ALU.add))
        dv(lambda e: e.tensor_reduce(m32["mx1"][:, :], T["lg_"][:, :, :], AX.X, ALU.max))
        t = dv(lambda e: e.tensor_tensor(T["lg_"][:, :, :], T["lg_"][:, :, :], bc(m32["mx1"]), ALU.subtract))
        AC.wait(t)
        t = AC.op(lambda e: e.activation(T["pr"][:, :, :], T["lg_"][:, :, :], ACT.Exp))
        DV.wait(t)
        dv(lambda e: e.tensor_reduce(m32["sm"][:, :], T["pr"][:, :, :], AX.X, ALU.add))
        dv(lambda e: e.reciprocal(m32["sm"][:, :], m32["sm"][:, :]))
        dv(lambda e: e.tensor_tensor(T["pr"][:, :, :], T["pr"][:, :, :], bc(m32["sm"]), ALU.mult))

        def pick(src, wt, oh):
            dv(lambda e: e.tensor_reduce(wt, src, AX.X, ALU.max))
            dv(lambda e: e.tensor_tensor(T["eq"][:, :, :], src, wt.rearrange("p (t a) -> p t a", a=1).broadcast_to([128, NT, E]), ALU.is_equal))
            dv(lambda e: e.tensor_tensor(T["ky"][:, :, :], T["eq"][:, :, :], ek, ALU.mult))
            dv(lambda e: e.tensor_reduce(m32["k1"][:, :], T["ky"][:, :, :], AX.X, ALU.max))
            dv(lambda e: e.tensor_tensor(oh, T["ky"][:, :, :], bc(m32["k1"]), ALU.is_equal))

        pick(T["pr"][:, :, :], m32["mx1"][:, :], T["o1"][:, :, :])
        dv(lambda e: e.tensor_scalar(XB[:, :, 259], m32["k1"][:, :], -1.0, 8.0, ALU.mult, ALU.add))
        dv(lambda e: e.scalar_tensor_tensor(T["mk"][:, :, :], T["o1"][:, :, :], -2.0, T["pr"][:, :, :], ALU.mult, ALU.add))
        pick(T["mk"][:, :, :], m32["w2t"][:, :], T["o2"][:, :, :])
        dv(lambda e: e.tensor_copy(XB[:, :, 257], m32["w2t"][:, :]))
        dv(lambda e: e.tensor_tensor(XB[:, :, 258], m32["mx1"][:, :], m32["w2t"][:, :], ALU.subtract))
        dv(lambda e: e.tensor_copy(XB[:, :, 256], CF[:, C_TOK:C_TOK + 32]))
        t = dv(lambda e: e.tensor_tensor(mkbt[:, :, :].rearrange("p c t -> p t c"), T["o1"][:, :, :], T["o2"][:, :, :], ALU.add))
        PE.wait(t, t_cb, t_ones)
        mf = mkbt[:, :, :].rearrange("p c t -> p (c t)")
        PE.op(lambda e: e.matmul(banks[0][:, 0:256], Ub[:, :], mf, start=True, stop=True), False)
        t = PE.op(lambda e: e.matmul(banks[1][:, 0:256], onesb[:, :], mf, start=True, stop=True))
        DV.wait(t)
        cum = T["cum"][:, :, :].rearrange("p t c -> p (t c)")
        tot = T["tot"][:, :, :].rearrange("p t c -> p (t c)")
        pf = T["pf"][:, :, :].rearrange("p t c -> p (t c)")
        dv(lambda e: e.tensor_copy(tot, banks[1][:, 0:256]))
        dv(lambda e: e.memset(pf, 0.0))
        dv(lambda e: e.tensor_tensor_scan(cum, tot, pf, 0.0, ALU.add, ALU.add))
        dv(lambda e: e.tensor_tensor(tot, cum, tot, ALU.subtract))
        ec = tot.rearrange("p (c t) -> p c t", t=NT)
        ic = cum.rearrange("p (c t) -> p c t", t=NT)
        e0 = t8[:, 0, :]
        dv(lambda e: e.tensor_copy(e0, ec[:, :, 0]))
        dv(lambda e: e.tensor_tensor(t8[:, 1, :], ic[:, :, NT - 1], e0, ALU.subtract))
        dv(lambda e: e.tensor_scalar(t8i[:, :], t8[:, 1, :], 63.5, 1.0 / 128.0, ALU.add, ALU.mult))
        dv(lambda e: e.tensor_copy(t8[:, 2, :], t8i[:, :]))
        dv(lambda e: e.memset(t8[:, 3, :], 0.0))
        dv(lambda e: e.tensor_tensor_scan(t8[:, 4, :], t8[:, 2, :], t8[:, 3, :], 0.0, ALU.add, ALU.add))
        dv(lambda e: e.tensor_tensor(t8[:, 5, :], t8[:, 4, :], t8[:, 2, :], ALU.subtract))
        dv(lambda e: e.scalar_tensor_tensor(t8[:, 6, :], t8[:, 5, :], 128.0, e0, ALU.mult, ALU.subtract))
        dv(lambda e: e.tensor_tensor(
            te8[:, :, :], t8[:, 4, :].rearrange("p (a c) -> p a c", a=1).broadcast_to([128, NTILE, E]),
            CF[:, C_J:C_J + NTILE].rearrange("p (j a) -> p j a", a=1).broadcast_to([128, NTILE, E]), ALU.is_le))
        dv(lambda e: e.tensor_reduce(TE[:, :], te8[:, :, :], AX.X, ALU.add))
        dv(lambda e: e.tensor_scalar(TE[:, :], TE[:, :], 7.0, None, ALU.min))
        t_te = dv(lambda e: e.tensor_copy(TEi[:, :], TE[:, :]))
        dv(lambda e: e.tensor_tensor(
            ec, ec, t8[:, 6, :].rearrange("p (c a) -> p c a", a=1).broadcast_to([128, E, NT]), ALU.add))
        dv(lambda e: e.tensor_tensor(tot, banks[0][:, 0:256], tot, ALU.add))
        ect = tot.rearrange("p (c t) -> p t c", t=NT)
        for o, sx, si in ((T["o1"], "s1", sl1), (T["o2"], "s2", sl2)):
            dv(lambda e, o=o: e.tensor_tensor(o[:, :, :], o[:, :, :], ect, ALU.mult))
            dv(lambda e, o=o, sx=sx: e.tensor_reduce(m32[sx][:, :], o[:, :, :], AX.X, ALU.add))
            t = dv(lambda e, sx=sx, si=si: e.tensor_copy(si[:, :], m32[sx][:, :]))
        NS = 4
        l_sc = [lane(f"l_sc{k}") for k in range(NS)]
        PO.wait(t, t_zf, *[bb_[b]["x2o"] for b in (B - 2, B - 1)])
        n = 0
        t_sc = [None] * NS
        for tl in range(NT):
            for si in (sl1, sl2):
                k = n % NS
                n += 1
                PO.wait(t_sc[k])
                t_sc[k] = PO.dma(l_sc[k], lambda e, tl=tl, si=si: e.indirect_dma_start(
                    out=xs, out_offset=bass.IndirectOffsetOnAxis(ap=si[:, tl:tl + 1], axis=0),
                    in_=XB[:, tl, :], in_offset=None, bounds_check=SLOTS - 1, oob_is_err=True))
        for q in (PE, DV, AC, PO, SP):
            q.wait(*t_sc)
        barrier()
        cr.close()

        NX = 3
        XS = sb("XS", [128, NX, ROW], F32)
        XTs = sb("XTs", [128, 2, 2, 2, 128], BF)
        Hf = sb("Hf", [128, 2, 1024], F32)
        Hh = sb("Hh", [128, 2, 1024], BF)
        Hl = sb("Hl", [128, 2, 1024], BF)
        Yf = sb("Yf", [128, 2, 256], F32)
        yt = sb("yt", [128, 2, 256], F32)
        ix = sb("ix", [128, 3, 5], F32)
        ixi = sb("ixi", [128, 3, 1], I32)
        l_xs = [lane(f"l_xs{k}") for k in range(NX)]
        l_y = [lane(f"l_y{k}") for k in range(2)]
        f = [dict() for _ in range(NTILE)]
        xtb = [banks[0], banks[1]]
        upb = [(banks[2], banks[3]), (banks[4], banks[5])]
        yb = [banks[6], banks[7]]

        def F0(j):
            SP.wait(*(f[j - NX][k] for k in ("T", "w")) if j >= NX else ())
            f[j]["x"] = SP.dma(l_xs[j % NX], lambda e: e.dma_start(XS[:, j % NX, :], xs[128 * j:128 * j + 128, :]))

        def F1(j):
            s = f[j]
            r, rx = j % 2, j % NX
            p = f[j - 2] if j >= 2 else {}
            PE.wait(s["x"], p.get("xl"))
            for dk in range(2):
                t = PE.op(lambda e, dk=dk: e.transpose(xtb[r][:, 128 * dk:128 * dk + 128], XS[:, rx, 128 * dk:128 * dk + 128], idf), dk == 1)
            s["T"] = t
            bv = xtb[r][:, 0:256].rearrange("p (k c) -> p k c", k=2)
            AC.wait(t, p.get("up"))
            th = AC.op(lambda e: e.activation(XTs[:, r, 0, :, :], bv, ACT.Copy))
            DV.wait(th)
            s["xl"] = DV.op(lambda e: e.tensor_tensor(XTs[:, r, 1, :, :], bv, XTs[:, r, 0, :, :], ALU.subtract))
            q = j % 3
            old = f[j - 3] if j >= 3 else {"y": None, "y1": None, "sc": None}
            PO.wait(s["x"], old["y"], old["y1"], old["sc"])
            v = XS[:, rx, 256:257]
            PO.op(lambda e: e.tensor_scalar(ix[:, q, 0:1], v, 0.0, CF[:, C_DUMP:C_DUMP + 1], ALU.is_equal, ALU.mult))
            t = PO.op(lambda e: e.tensor_scalar(ix[:, q, 2:3], XS[:, rx, 259:260], TE[:, j:j + 1], XS[:, rx, 258:259], ALU.is_equal, ALU.mult))
            PO.op(lambda e: e.tensor_scalar(ix[:, q, 1:2], v, -1.0, None, ALU.add))
            PO.wait(PO.now())
            PO.op(lambda e: e.tensor_tensor(ix[:, q, 4:5], ix[:, q, 0:1], ix[:, q, 1:2], ALU.add))
            PO.wait(PO.now())
            PO.op(lambda e: e.tensor_copy(ixi[:, q, 0:1], ix[:, q, 4:5]))
            s["w"] = PO.op(lambda e: e.tensor_tensor(ix[:, q, 3:4], ix[:, q, 2:3], XS[:, rx, 257:258], ALU.add))

        def F2(j):
            s = f[j]
            r = j % 2
            p = f[j - 2] if j >= 2 else {}
            PE.wait(s["xl"], t_te, p.get("h"))
            reg = {}
            PE.raw(lambda e: reg.__setitem__("e", e.value_load(TEi[0:1, j:j + 1], min_val=0, max_val=7)))
            s["reg"] = reg
            for fm in range(8):
                bank = upb[r][fm // 4]
                n = 0
                for dk in range(2):
                    for hw, hx in ((0, 0), (0, 1), (1, 0)):
                        off = 512 * fm + 256 * dk + 128 * hw
                        t = PE.op(lambda e, off=off, hx=hx, dk=dk, n=n, bank=bank, fm=fm: e.matmul(
                            bank[:, 128 * (fm % 4):128 * (fm % 4) + 128], WU[:, bass.ds(reg["e"] * 4096 + off, 128)],
                            XTs[:, r, hx, dk, :], start=n == 0, stop=n == 5), n == 5 and fm % 4 == 3)
                        n += 1
                if fm % 4 == 3:
                    k = fm // 4
                    AC.wait(t, p.get("hl"))
                    th = AC.op(lambda e, bank=bank, k=k: e.activation(Hf[:, r, 512 * k:512 * k + 512], bank[:, :], ACT.Gelu))
                    s["h"] = th
                    hs = slice(512 * k, 512 * k + 512)
                    DV.wait(th, p.get("dn"))
                    t2 = DV.op(lambda e, hs=hs: e.tensor_copy(Hh[:, r, hs], Hf[:, r, hs]))
                    DV.wait(t2)
                    s["hl"] = DV.op(lambda e, hs=hs: e.tensor_tensor(Hl[:, r, hs], Hf[:, r, hs], Hh[:, r, hs], ALU.subtract))
            s["up"] = t

        def F3(j):
            s = f[j]
            r, q = j % 2, j % 3
            p = f[j - 2] if j >= 2 else {}
            PE.wait(s["hl"], p.get("y"), p.get("y1"))
            reg = s["reg"]
            for fk in range(8):
                hsl = slice(128 * fk, 128 * fk + 128)
                PE.op(lambda e, fk=fk, hsl=hsl: e.matmul(
                    yb[r][:, 0:512], Hh[:, r, hsl], WD[:, bass.ds(reg["e"] * 4096 + 512 * fk, 512)], start=fk == 0, stop=False,
                    skip_group_check=True), False)
                t = PE.op(lambda e, fk=fk, hsl=hsl: e.matmul(
                    yb[r][:, 0:256], Hl[:, r, hsl], WD[:, bass.ds(reg["e"] * 4096 + 512 * fk, 256)], start=False, stop=fk == 7,
                    skip_group_check=True), fk == 7)
            s["dn"] = t
            AC.wait(t, s["w"], p.get("y"))
            t1 = AC.op(lambda e: e.activation(yt[:, r, :], yb[r][:, 256:512], ACT.Copy, scale=ix[:, q, 3:4]))
            s["y1"] = t1
            DV.wait(t1, s["w"], p.get("sc"))
            s["y"] = t2 = DV.op(lambda e: e.scalar_tensor_tensor(
                Yf[:, r, :], yb[r][:, 0:256], ix[:, q, 3:4], yt[:, r, :], ALU.mult, ALU.add))
            PO.wait(t2, s["w"], f[j - 1]["sc"] if j else None)
            s["sc"] = PO.dma(l_y[r], lambda e: e.indirect_dma_start(
                out=out, out_offset=bass.IndirectOffsetOnAxis(ap=ixi[:, q, 0:1], axis=0), in_=Yf[:, r, :], in_offset=None,
                bounds_check=TOK + 127, oob_is_err=True, compute_op=ALU.add))

        F0(0)
        F0(1)
        F1(0)
        for j in range(NTILE + 1):
            if j < NTILE:
                F2(j)
            if j + 1 < NTILE:
                if j + 2 < NTILE:
                    F0(j + 2)
                F1(j + 1)
            if j >= 1:
                F3(j - 1)
        SP.wait(f[NTILE - 1]["sc"], f[NTILE - 2]["sc"], t_zf)
        PO.wait(f[NTILE - 1]["sc"], f[NTILE - 2]["sc"])

        with nc.Block() as block:
            @block.sync
            def _(e):
                SP.run(e)

            @block.gpsimd
            def _(e):
                PO.run(e)

            @block.scalar
            def _(e):
                AC.run(e)

            @block.vector
            def _(e):
                DV.run(e)

            @block.tensor
            def _(e):
                PE.run(e)


_INS = ["x", "ctx", "wqkv", "wout", "wg", "bg", "gain", "wr", "br", "wup", "wdn", "cst"]


def constants():
    import numpy as np
    c = np.zeros((128, C_END), np.float32)
    p = np.arange(128)
    c[:, C_ID:C_ID + 128] = np.eye(128)
    c[:, C_MASK:C_MASK + 128] = np.where(p[None, :] > p[:, None], NEG, 0.0)
    c[:, C_U:C_U + 128] = p[:, None] < p[None, :]
    for tt in range(2):
        for s in range(16):
            c[:, C_SEL + 16 * tt + s] = s == 8 * tt + p // 16
    c[:, C_M0] = p % 32 < 16
    c[:, C_M1] = -1.0 * (p % 32 >= 16)
    c[:, C_C17] = (p % 32 == 16) | (p % 32 == 17)
    c[:, C_TOK:C_TOK + 32] = 128 * np.arange(32)[None, :] + p[:, None] + 1
    c[:, C_EK:C_EK + 8] = 8 - np.arange(8)
    c[:, C_J:C_J + NTILE] = np.arange(NTILE)
    c[:, C_DUMP] = TOK + p + 1
    return c


def layout(inputs):
    import numpy as np
    i = {k: np.asarray(v) for k, v in inputs.items()}
    w = i["L0_attn_W_qkv"].reshape(4, 4, D, 3, 16)
    q = w[:, :, :, 0, :].transpose(2, 0, 1, 3)
    k = w[:, :, :, 1, :].transpose(2, 0, 1, 3)
    v = w[:, :, :, 2, :].transpose(2, 0, 1, 3).reshape(D, 256)
    q2 = np.concatenate([q, q], axis=3).reshape(D, 512)
    k2 = np.concatenate([k, k], axis=3).reshape(D, 512)
    wq = np.concatenate([q2, k2, v], axis=1).reshape(2, 128, 1280).transpose(1, 0, 2)
    ig = i["L0_xattn_ifgate_w"].reshape(16, 3, 2, 128)
    wg = ig.transpose(3, 2, 1, 0).reshape(128, 2, 48)
    wr = i["L0_ffn_router_w"].reshape(2, 128, 8).transpose(1, 0, 2)
    wup = i["L0_ffn_expert_up"].reshape(8, 8, 128, 2, 128).transpose(4, 0, 1, 3, 2).reshape(128, 16384)
    wdn = i["L0_ffn_expert_down"].reshape(8, 256, 8, 128).transpose(3, 0, 2, 1).reshape(128, 16384)
    arrays = {"x": i["x"], "ctx": i["ctx_1024"], "wqkv": wq, "wout": i["L0_attn_W_out"].reshape(256, 256), "wg": wg,
              "bg": i["L0_xattn_ifgate_b"], "gain": i["L0_xattn_outnorm_w"], "wr": wr, "br": i["L0_ffn_router_b"],
              "wup": wup, "wdn": wdn, "cst": constants()}
    return {n: np.ascontiguousarray(a) for n, a in arrays.items()}


def kernel(**inputs):
    import concourse.bacc as _bacc
    from concourse import mybir as _mybir
    from concourse.bass_utils import run_bass_kernel_spmd as _run

    arrays = layout(inputs)
    nc = _bacc.Bacc("TRN2", target_bir_lowering=False, num_devices=1)
    args = [nc.dram_tensor(n + "_in", arrays[n].shape, F32, kind="ExternalInput").ap() for n in _INS]
    out = nc.dram_tensor("out_d", (TOK + 128, D), F32, kind="ExternalOutput").ap()
    build(nc, *args, out)
    r = _run(nc, [{n + "_in": arrays[n] for n in _INS}], core_ids=[0])
    return r.results[0]["out_d"][:TOK].reshape(B, S, D)
```

```python
import concourse.bass as bass
from concourse import mybir
from contextlib import ExitStack

F32 = mybir.dt.float32
BF = mybir.dt.bfloat16
I32 = mybir.dt.int32
ALU = mybir.AluOpType
ACT = mybir.ActivationFunctionType
AX = mybir.AxisListType

B, S, D = 16, 256, 256
NT = B * 2
NH = 16
MH = 8
E = 8
TOK = B * S
NTILE = 71
SLOTS = NTILE * 128
ROW = 260
NEG = -1.0e30
KF1 = 3
LAG = 9

C_ID, C_MASK, C_U, C_SEL, C_M0, C_M1, C_C17, C_TOK, C_EK, C_J, C_DUMP, C_SL, C_END = (
    0, 128, 256, 384, 416, 417, 418, 419, 451, 459, 530, 531, 535)


class Queue:

    def __init__(self, sem):
        self.sem, self.n, self.items, self.seen = sem, 0, [], {}

    def wait(self, *toks):
        for t in toks:
            if t is None or self.seen.get(id(t[0]), 0) >= t[1]:
                continue
            self.seen[id(t[0])] = t[1]
            self.items.append(lambda e, t=t: e.wait_ge(t[0], t[1]))

    def op(self, fn, sig=True):
        if sig:
            self.n += 1
            self.items.append(lambda e: fn(e).then_inc(self.sem, 1))
            return (self.sem, self.n)
        self.items.append(lambda e: fn(e))
        return None

    def raw(self, fn):
        self.items.append(fn)

    def dma(self, lane, fn):
        lane.n += 16
        self.items.append(lambda e: fn(e).then_inc(lane.sem, 16))
        return (lane.sem, lane.n)

    def now(self):
        return (self.sem, self.n)

    def run(self, e):
        for f in self.items:
            f(e)


class Lane:

    def __init__(self, sem):
        self.sem, self.n = sem, 0


def build(nc, x, ctx_in, wqkv, wout, wg, bg, gain, wr, br, wup, wdn, cst, out):
    xs = nc.dram_tensor("xs_scr", (SLOTS, ROW), F32, kind="Internal").ap()
    osc = nc.dram_tensor("o_scr", (B, D * S), F32, kind="Internal").ap()
    qsc = nc.dram_tensor("q_scr", (B, 128, 2048), BF, kind="Internal").ap()
    gsc = nc.dram_tensor("g_scr", (6, 128, 256), BF, kind="Internal").ap()

    st = ExitStack()
    with st:
        def sb(name, shape, dt, c=st):
            return c.enter_context(nc.sbuf_tensor(name, shape, dt))

        def sem(name):
            return st.enter_context(nc.semaphore(name))

        def lane(name):
            return Lane(sem(name))

        PE, DV, AC, PO, SP = (Queue(sem("s_" + n)) for n in ("pe", "dve", "act", "pool", "sp"))

        banks = [st.enter_context(nc.psum_tensor(f"bank{i}", [128, 512], F32)) for i in range(8)]

        XB = sb("XB", [128, NT, ROW], F32)
        WU = sb("WU", [128, E * 4096], BF)
        CF = sb("CF", [128, C_END], F32)
        idb = sb("idb", [128, 128], BF)
        Ub = sb("Ub", [128, 128], BF)
        onesb = sb("onesb", [128, 128], BF)
        onesf = sb("onesf", [128, 2], F32)
        mhalf = sb("mhalf", [128, 8], F32)
        WGf = sb("WGf", [128, 2, 56], F32)
        WGs = sb("WGs", [128, 2, 2, 40], BF)
        BG = sb("BG", [128, 24], F32)
        EM = sb("EM", [128, 2, 128], F32)
        GN = sb("GN", [128, 256], F32)
        stat = sb("stat", [128, 2, 2, 8], F32)
        LS = sb("LS", [128, 2, 2, 4], F32)
        STG = sb("STG", [128, 2, 512], F32)
        idf = CF[:, C_ID:C_ID + 128]
        m0 = CF[:, C_M0:C_M0 + 1]
        m1n = CF[:, C_M1:C_M1 + 1]
        c17 = CF[:, C_C17:C_C17 + 1]

        gates = banks[7]
        ringW = [banks[k] for k in (5, 6, 0, 1, 2, 3)]

        l_c = lane("l_c")
        l_x = [lane(f"l_x{i}") for i in range(4)]
        l_w = lane("l_w")
        t_c = SP.dma(l_c, lambda e: e.dma_start(CF[:, :], cst))
        xv = x.rearrange("b (t p) d -> p (b t) d", p=128)
        t_x = []

        def load_x(i):
            t_x.append(SP.dma(l_x[i], lambda e: e.dma_start(XB[:, 8 * i:8 * i + 8, 0:256], xv[:, 8 * i:8 * i + 8, :])))
        load_x(0)
        l_wg = lane("l_wg")
        SP.dma(l_wg, lambda e: e.dma_start(WGf[:, :, 0:48], wg))
        SP.dma(l_wg, lambda e: e.dma_start(WGf[:, :, 48:56], wr))
        SP.dma(l_wg, lambda e: e.dma_start(BG[:, 0:16], bg.rearrange("(a n) -> a n", a=1).broadcast_to([128, 16])))
        SP.dma(l_wg, lambda e: e.dma_start(BG[:, 16:24], br.rearrange("(a n) -> a n", a=1).broadcast_to([128, 8])))
        t_wg = SP.dma(l_wg, lambda e: e.dma_start(GN[:, :], gain.rearrange("(a n) -> a n", a=1).broadcast_to([128, 256])))

        ca = ExitStack()
        WQh = sb("WQh", [128, 2, 1280], BF, ca)
        WQl = sb("WQl", [128, 2, 1280], BF, ca)
        mkb = sb("mkb", [128, 128], BF, ca)
        xn = sb("xn", [128, 2, 256], F32, ca)
        xTh = sb("xTh", [128, 2, 2, 256], BF, ca)
        xTl = sb("xTl", [128, 2, 2, 256], BF, ca)
        Qh = sb("Qh", [128, 2, 4, 256], BF, ca)
        Q1 = sb("Q1", [128, 2, 4, 256], BF, ca)
        Q2 = sb("Q2", [128, 2, 512], BF, ca)
        QM1 = sb("QM1", [128, 2, 4, 512], BF, ca)
        QM2 = sb("QM2", [128, 2, 512], BF, ca)
        K1 = sb("K1", [128, 2, 4, 256], BF, ca)
        K2 = sb("K2", [128, 2, 4, 256], BF, ca)
        Ym = sb("Ym", [128, 2, 256], BF, ca)
        Vp = sb("Vp", [128, 2, 2, NH * 17 + 15], F32, ca)
        Vv = Vp[:, :, :, 0:NH * 17].rearrange("p r t (n c) -> p r t n c", c=17)
        mx = sb("mx", [128, 2, 2, 8], F32, ca)
        Mp = sb("Mp", [128, 2, 8, 32], BF, ca)
        PT = sb("PT", [128, 2, 4, 2, 384], F32, ca)
        OTs = sb("OTs", [128, 4, 256], F32, ca)
        rc = sb("rc", [128, 2, NH], F32, ca)
        wsq = sb("wsq", [128, 2, NH], F32, ca)
        On = sb("On", [128, 2, NH, 16], F32, ca)
        Mm = sb("Mm", [128, 2, 2, 256], F32, ca)
        Cn = sb("Cn", [128, 1, 2, 256], F32, ca)
        WQf = PT[:, :, :, :, :].rearrange("p a j g c -> p (a j g c)")[:, 0:2560].rearrange("p (k c) -> p k c", k=2)
        WO = OTs[:, 0:2, :]
        wtmp = OTs[:, 2, :]
        SPL = sb("SPL", [128, 1, 2048], BF, ca)

        t_w = SP.dma(l_w, lambda e: e.dma_start(WQf, wqkv))
        l_wo = lane("l_wo")
        t_wo = SP.dma(l_wo, lambda e: e.dma_start(WO, wout.rearrange("(k p) d -> p k d", p=128)))

        t_half = PO.op(lambda e: e.memset(mhalf[:, :], -0.5))
        t_vz = PO.op(lambda e: e.memset(Vp[:, :, :, :], 0.0))
        t_mpz = PO.op(lambda e: e.memset(Mp[:, :, :, :], 0.0))
        PO.wait(t_vz)
        t_vz = PO.op(lambda e: e.memset(Vv[:, :, :, :, 16:17].rearrange("p r t n c -> p (r t) (n c)"), 1.0))
        PO.op(lambda e: e.memset(onesb[:, :], 1.0))
        t_ones = PO.op(lambda e: e.memset(onesf[:, :], 1.0))
        DV.wait(t_c)
        DV.op(lambda e: e.tensor_copy(idb[:, :], idf))
        DV.op(lambda e: e.tensor_copy(mkb[:, :], CF[:, C_MASK:C_MASK + 128]))
        t_cb = DV.op(lambda e: e.tensor_copy(Ub[:, :], CF[:, C_U:C_U + 128]))
        AC.wait(t_w)
        t_wh = AC.op(lambda e: e.activation(WQh[:, :, :], WQf, ACT.Copy))
        DV.wait(t_wh, t_w)
        t_wl = DV.op(lambda e: e.tensor_tensor(WQl[:, :, :], WQf, WQh[:, :, :], ALU.subtract))
        DV.wait(t_wg)
        t = DV.op(lambda e: e.tensor_tensor(WGf[:, :, 16:32], WGf[:, :, 16:32], WGf[:, :, 32:48], ALU.add))
        DV.wait(t)
        DV.op(lambda e: e.tensor_copy(WGs[:, :, 0, 0:32], WGf[:, :, 0:32]))
        t = DV.op(lambda e: e.tensor_copy(WGs[:, :, 0, 32:40], WGf[:, :, 48:56]))
        DV.wait(t)
        DV.op(lambda e: e.tensor_tensor(WGs[:, :, 1, 0:32], WGf[:, :, 0:32], WGs[:, :, 0, 0:32], ALU.subtract))
        DV.op(lambda e: e.tensor_tensor(WGs[:, :, 1, 32:40], WGf[:, :, 48:56], WGs[:, :, 0, 32:40], ALU.subtract))
        t_gn = DV.op(lambda e: e.tensor_scalar(GN[:, :], GN[:, :], 1.0, None, ALU.add))
        t_wgs = t_gn
        PO.op(lambda e: e.memset(wtmp, 1.0))
        t_w1 = PO.now()
        PE.wait(t_w1, t_wo)
        PE.op(lambda e: e.matmul(banks[0][:, 0:256], OTs[:, 2, 0:128], OTs[:, 0, :], start=True, stop=False), False)
        t_ws = PE.op(lambda e: e.matmul(banks[0][:, 0:256], OTs[:, 2, 0:128], OTs[:, 1, :], start=False, stop=True))
        DV.wait(t_ws)
        for tt in range(2):
            selv = CF[:, C_SEL + 16 * tt:C_SEL + 16 * tt + 16].rearrange("p (a s) -> p a s", a=1).broadcast_to([128, 16, 16])
            t = DV.op(lambda e, selv=selv: e.tensor_tensor(
                wtmp.rearrange("p (n s) -> p n s", s=16), banks[0][:, 0:256].rearrange("p (n s) -> p n s", s=16),
                selv, ALU.mult))
            DV.wait(t)
            t = DV.op(lambda e, tt=tt: e.tensor_reduce(wsq[:, tt, :], wtmp.rearrange("p (n s) -> p n s", s=16), AX.X, ALU.add))
            DV.wait(t)
        t_b0 = t
        t_wsq = t

        l_st = [lane("l_st0"), lane("l_st1")]
        stg_free = [None, None]
        chunk_n = [0]

        def chunk(dst, src, width, c):
            i = chunk_n[0] % 2
            chunk_n[0] += 1
            SP.wait(stg_free[i])
            tl = SP.dma(l_st[i], lambda e: e.dma_start(STG[:, i, :], src[:, 512 * c:512 * c + 512]))
            v = dst[:, 1024 * c:1024 * c + 1024].rearrange("p (a h w) -> p a h w", h=2, w=width)
            s = STG[:, i, :].rearrange("p (a w) -> p a w", w=width)
            return i, tl, v, s

        def split(c4):
            i, tl, v, s = c4
            PO.wait(tl)
            t = PO.op(lambda e: e.tensor_copy(v[:, :, 0, :], s))
            PO.wait(t)
            stg_free[i] = PO.op(lambda e: e.tensor_tensor(v[:, :, 1, :], s, v[:, :, 0, :], ALU.subtract))

        def splitb(c4):
            i, tl, v, s = c4
            AC.wait(tl)
            t = AC.op(lambda e: e.activation(v[:, :, 0, :], s, ACT.Copy))
            DV.wait(t)
            stg_free[i] = DV.op(lambda e: e.tensor_tensor(v[:, :, 1, :], s, v[:, :, 0, :], ALU.subtract))

        ringW_free = [t_b0] * 6
        ringW_n = [0]

        def wbank(need_pe=True):
            i = ringW_n[0] % 6
            ringW_n[0] += 1
            PE.wait(ringW_free[i])
            return i, ringW[i]

        stat_n = [0]
        stat_free = [None, None]

        def ln_stats(src, *toks):
            k = stat_n[0] % 2
            stat_n[0] += 1
            mv = LS[:, k, :, :]
            DV.wait(*toks, stat_free[k])
            for tt in range(2):
                t = DV.op(lambda e, tt=tt: e.bn_stats(stat[:, k, tt, 0:6], src[:, tt, :]))
            DV.wait(t)
            for tt in range(2):
                t = DV.op(lambda e, tt=tt: e.bn_aggr(mv[:, tt, 0:2], stat[:, k, tt, 0:6]))
            DV.wait(t)
            t = DV.op(lambda e: e.tensor_scalar(mv[:, :, 2], mv[:, :, 1], 1e-5, None, ALU.add))
            PO.wait(t, t_half)
            return k, PO.op(lambda e: e.tensor_tensor(mv[:, :, 3], mv[:, :, 2], mhalf[:, 0:2], ALU.pow))

        def ln_apply(kt, src, dst, *toks):
            k, t = kt
            DV.wait(t, *toks)
            for tt in range(2):
                t = DV.op(lambda e, tt=tt: e.tensor_scalar(
                    dst[:, tt, :], src[:, tt, :], LS[:, k, tt, 0:1], LS[:, k, tt, 3:4], ALU.subtract, ALU.mult))
            stat_free[k] = t
            return t

        def transpose_pair(src2, toks):
            i, bank = wbank()
            PE.wait(*toks, t_c)
            for tt in range(2):
                for dk in range(2):
                    t = PE.op(lambda e, tt=tt, dk=dk: e.transpose(
                        bank[:, 256 * dk + 128 * tt:256 * dk + 128 * tt + 128], src2[tt][:, 128 * dk:128 * dk + 128], idf),
                        tt == 1 and dk == 1)
            return i, bank, t

        def split_T(i, bank, t, hi, lo, *free):
            bv = bank[:, :].rearrange("p (k c) -> p k c", k=2)
            AC.wait(t, *free)
            th = AC.op(lambda e: e.activation(hi, bv, ACT.Copy))
            DV.wait(th)
            tl = DV.op(lambda e: e.tensor_tensor(lo, bv, hi, ALU.subtract))
            ringW_free[i] = tl
            return tl

        a = [dict() for _ in range(B)]

        def got(b, key):
            return a[b].get(key) if 0 <= b < B else None

        def A0s(b):
            xx = XB[:, 2 * b:2 * b + 2, 0:256]
            a[b]["ls"] = ln_stats(xx, t_x[b // 4])

        def A0n(b):
            s = a[b]
            xx = XB[:, 2 * b:2 * b + 2, 0:256]
            s["xn"] = ln_apply(s["ls"], xx, xn, got(b - 1, "xT_done"), t_x[b // 4])

        def A0(b):
            r = b % 2
            s = a[b]
            tp = transpose_pair([xn[:, 0, :], xn[:, 1, :]], [s["xn"]])
            s["xT_done"] = tp[2]
            s["xTl"] = split_T(*tp, xTh[:, r, :, :], xTl[:, r, :, :], got(b - 2, "Vproj"))

        def A1(b, which, g2):
            r = b % 2
            s = a[b]
            PE.wait(s["xTl"], t_wl)
            i, bank = wbank()
            col = 0 if which == "q" else 512
            for gg in range(2):
                c = col + 128 * (2 * g2 + gg)
                n = 0
                for dk in range(2):
                    for w, v in ((WQh, xTh), (WQh, xTl), (WQl, xTh)):
                        t = PE.op(lambda e, w=w, v=v, dk=dk, c=c, gg=gg, n=n: e.matmul(
                            bank[:, 256 * gg:256 * gg + 256], w[:, dk, c:c + 128], v[:, r, dk, :],
                            start=n == 0, stop=n == 5), n == 5 and gg == 1)
                        n += 1
            bv = bank[:, :].rearrange("p (g c) -> p g c", g=2)
            gs = slice(2 * g2, 2 * g2 + 2)
            if which == "q":
                AC.wait(t, got(b - 2, "Q2"))
                th = AC.op(lambda e: e.activation(Qh[:, r, gs, :], bv, ACT.Copy))
                DV.wait(th, got(b - 2, "QM1"))
                s["Q1", g2] = ringW_free[i] = DV.op(lambda e: e.scalar_tensor_tensor(
                    Q1[:, r, gs, :], Qh[:, r, gs, :], m1n, bv, ALU.mult, ALU.add))
                return
            AC.wait(t, got(b - 2, "ST"))
            s["K1", g2] = th = AC.op(lambda e: e.activation(K1[:, r, gs, :], bv, ACT.Copy))
            DV.wait(th, ym_free[0])
            ty = DV.op(lambda e: e.tensor_scalar(Ym[:, :, :], K1[:, r, gs, :], m0, c17, ALU.mult, ALU.subtract))
            DV.wait(ty, got(b - 2, "ST"))
            s["K2", g2] = ym_free[0] = ringW_free[i] = DV.op(lambda e: e.scalar_tensor_tensor(
                K2[:, r, gs, :], bv, m0, Ym[:, :, :], ALU.mult, ALU.subtract))

        ym_free = [None]

        def A1v(b):
            r = b % 2
            s = a[b]
            i, bank = wbank()
            for tt in range(2):
                n = 0
                for dk in range(2):
                    for w, v in ((WQh, xTh), (WQl, xTh), (WQh, xTl)):
                        t = PE.op(lambda e, w=w, v=v, dk=dk, tt=tt, n=n: e.matmul(
                            bank[:, 256 * tt:256 * tt + 256], v[:, r, dk, 128 * tt:128 * tt + 128], w[:, dk, 1024:1280],
                            start=n == 0, stop=n == 5), n == 5 and tt == 1)
                        n += 1
            s["Vproj"] = t
            AC.wait(t, t_vz, got(b - 2, "PV"))
            s["V"] = ringW_free[i] = AC.op(lambda e: e.activation(
                Vv[:, r, :, :, 0:16], bank[:, :].rearrange("p (t n h) -> p t n h", t=2, h=16), ACT.Copy))

        qm1_free, qm2_free, q2_free, mp_free = [None, None], [None, None], [None, None], [None]

        def QM(b, P, j):
            r = b % 2
            h = P
            s = a[b]
            DV.wait(s["Q1", P], qm1_free[h] if j == 0 else None)
            s["QM1"] = s["QM1", P, j] = DV.op(lambda e: e.tensor_scalar(
                QM1[:, h, j, :], Q1[:, r, 2 * P:2 * P + 2, :].rearrange("p g c -> p (g c)"),
                CF[:, C_SL + j:C_SL + j + 1], None, ALU.mult))

        def QN2(b, P, j):
            s = a[b]
            h = P
            AC.wait(s["Q2"], qm2_free[j % 2])
            s["QM2", j % 2] = q2_free[h] = AC.op(lambda e: e.activation(
                QM2[:, j % 2, :], Q2[:, h, :], ACT.Copy, scale=CF[:, C_SL + j:C_SL + j + 1]))

        def A2(b, P, j):
            r = b % 2
            s = a[b]
            PE.wait(s["QM1", P, j], s["K1", P], t_cb)
            DV.wait(mp_free[0])
            for u in range(2):
                i, bank = wbank()
                w = 256 if u == 0 else 128
                q0 = 128 if u == 0 else 0
                tt = 1 - u
                bv = bank[:, 0:2 * w].rearrange("p (g c) -> p g c", g=2)
                PE.op(lambda e, bv=bv, w=w: e.matmul(
                    bv[:, :, w - 128:w], idb[:, :], mkb[:, :].rearrange("p (a c) -> p a c", a=1).broadcast_to([128, 2, 128]),
                    start=True, stop=False, skip_group_check=True), False)
                for gg in range(2):
                    t = PE.op(lambda e, gg=gg, w=w, q0=q0, bank=bank: e.matmul(
                        bank[:, w * gg:w * gg + w], QM1[:, P, j, 256 * gg + q0:256 * gg + q0 + 128], K1[:, r, 2 * P + gg, 0:w],
                        start=False, stop=gg == 1, skip_group_check=True), gg == 1)
                DV.wait(t)
                ringW_free[i] = s["mx"] = DV.op(lambda e, bv=bv, tt=tt: e.tensor_reduce(
                    mx[:, P, tt, :].rearrange("p (g c) -> p g c", c=4)[:, :, j], bv, AX.X, ALU.max))

        def A2e(b, P):
            s = a[b]
            DV.wait(s["mx"], t_mpz, mp_free[0])
            t = DV.op(lambda e: e.tensor_scalar(Mp[:, :, :, 16], mx[:, P, :, :], -1.0, None, ALU.mult))
            DV.wait(t)
            s["mp"] = DV.op(lambda e: e.scalar_tensor_tensor(
                Mp[:, :, :, 17], mx[:, P, :, :], -1.0, Mp[:, :, :, 16], ALU.mult, ALU.subtract))

        def A2t(b, P):
            r = b % 2
            s = a[b]
            i, bank = wbank()
            bb = bank[:, :].bitcast(BF)
            PE.wait(s["mp"])
            for g in range(2):
                for tt in range(2):
                    t = PE.op(lambda e, g=g, tt=tt: e.transpose(
                        bb[:, 256 * g + 128 * tt:256 * g + 128 * tt + 128],
                        Mp[:, tt, 4 * g:4 * g + 4, :].rearrange("p n c -> p (n c)"), idb[:, :]), g == 1 and tt == 1)
            mp_free[0] = t
            DV.wait(t, q2_free[P])
            ringW_free[i] = s["Q2"] = DV.op(lambda e: e.scalar_tensor_tensor(
                Q2[:, P, :], Qh[:, r, 2 * P:2 * P + 2, :].rearrange("p g c -> p (g c)"), m0, bb[:, 0:512], ALU.mult, ALU.add))

        pt_free = [None, None]
        otb = banks[4]
        ot_free = [None]

        def A3(b, P, j):
            r = b % 2
            s = a[b]
            PE.wait(s["QM2", j % 2], s["K2", P])
            for u in range(2):
                i, bank = wbank()
                w = 256 if u == 0 else 128
                q0, k0 = 256 - w, 128 * u
                for gg in range(2):
                    PE.op(lambda e, gg=gg, w=w, q0=q0, k0=k0, bank=bank: e.matmul(
                        bank[:, w * gg:w * gg + w], K1[:, r, 2 * P + gg, k0:k0 + 128], QM1[:, P, j, 256 * gg + q0:256 * gg + 256],
                        start=True, stop=False), False)
                    t = PE.op(lambda e, gg=gg, w=w, q0=q0, k0=k0, bank=bank: e.matmul(
                        bank[:, w * gg:w * gg + w], K2[:, r, 2 * P + gg, k0:k0 + 128],
                        QM2[:, j % 2, 256 * gg + q0:256 * gg + 256], start=False, stop=True), gg == 1)
                AC.wait(t, pt_free[P], t_wl)
                dst = PT[:, P, j, :, 0:256] if u == 0 else PT[:, P, j, :, 256:384]
                t1 = AC.op(lambda e, dst=dst, bank=bank, w=w: e.activation(
                    dst, bank[:, 0:2 * w].rearrange("p (j c) -> p j c", c=w), ACT.Exp, scale=0.25))
                ringW_free[i] = t1
                dg = dst[:, :, 0:128]
                PO.wait(t1)
                s["PT", P] = PO.op(lambda e, dg=dg: e.affine_select(
                    out=dg, in_=dg, pattern=[[0, 2], [1, 128]], compare_op=ALU.is_ge, fill=0.0, base=0, channel_multiplier=-1))
            qm2_free[j % 2] = t
            if j == 3:
                qm1_free[P] = s["ST"] = t

        def A3v(b, g):
            r = b % 2
            s = a[b]
            p, gg = g // 2, g % 2
            if gg == 0:
                PE.wait(ot_free[0])
            PE.wait(s["PT", p], s["V"])
            for kt in range(2):
                for j in range(4):
                    c = 17 * (4 * g + j)
                    t = PE.op(lambda e, kt=kt, j=j, c=c: e.matmul(
                        otb[32 * j:32 * j + 32, 256 * gg + 128 * kt:256 * gg + 256], Vp[:, r, kt, c:c + 32],
                        PT[:, p, j, gg, 0:256] if kt == 0 else PT[:, p, j, gg, 256:384], start=kt == 0, stop=kt == 1),
                        kt == 1 and j == 3)
            if gg == 1:
                pt_free[p] = t
                AC.wait(t, t_wsq, got(b - 1, "otT"))
                ot_free[0] = AC.op(lambda e: e.activation(
                    OTs[:, g - 1:g + 1, :], otb[:, :].rearrange("p (g c) -> p g c", g=2), ACT.Copy))
                s["OTs"] = ot_free[0]
            if g == 3:
                s["PV"] = t

        l_o = [lane("l_o0"), lane("l_o1")]
        l_m = [lane("l_m0"), lane("l_m1")]

        def A4(b, tt):
            s = a[b]
            for tt in (tt,):
                i, bank = wbank()
                PE.wait(s["OTs"])
                for g in range(4):
                    t = PE.op(lambda e, g=g, tt=tt, bank=bank: e.transpose(
                        bank[:, 128 * g:128 * g + 128], OTs[:, g, 128 * tt:128 * tt + 128], idf), g == 3)
                bv = bank[:, :].rearrange("p (n c) -> p n c", c=32)
                DV.wait(t, a[b - 1]["ost", tt] if b >= 1 else None)
                t2 = DV.op(lambda e, tt=tt, bv=bv: e.reciprocal(rc[:, tt, :], bv[:, :, 16]))
                DV.wait(t2, t_wsq)
                t2 = DV.op(lambda e, tt=tt: e.tensor_tensor(rc[:, tt, :], rc[:, tt, :], wsq[:, tt, :], ALU.mult))
                DV.wait(t2)
                t2 = DV.op(lambda e, tt=tt, bv=bv: e.tensor_tensor(
                    On[:, tt, :, :], bv[:, :, 0:16], rc[:, tt, :].rearrange("p (n a) -> p n a", a=1).broadcast_to([128, NH, 16]),
                    ALU.mult))
                ringW_free[i] = t2
            s["otT"] = t
            s["On"] = t2
            SP.wait(t2)
            for tt in (tt,):
                to = SP.dma(l_o[tt], lambda e, tt=tt: e.dma_start(
                    osc[b, :].rearrange("(n q h) -> q n h", n=NH, h=16)[128 * tt:128 * tt + 128, :, :], On[:, tt, :, :]))
                s["ost", tt] = to

        def A4b(b):
            s = a[b]
            r = b % 2
            SP.wait(s["ost", 0], s["ost", 1], a[b - 2]["mT"] if b >= 2 else None)
            s["M"] = SP.dma(l_m[r], lambda e: e.dma_start(Mm[:, r, :, :], osc[b, :].rearrange("(k p s) -> p k s", p=128, s=256)))

        def A5(b):
            s = a[b]
            r = b % 2
            i, bank = wbank()
            PE.wait(s["M"])
            for dk in range(2):
                for tt in range(2):
                    t = PE.op(lambda e, dk=dk, tt=tt: e.transpose(
                        bank[:, 256 * tt + 128 * dk:256 * tt + 128 * dk + 128], Mm[:, r, dk, 128 * tt:128 * tt + 128], idf),
                        dk == 1 and tt == 1)
            s["mT"] = t
            DV.wait(t)
            xx = XB[:, 2 * b:2 * b + 2, 0:256]
            s["x1"] = ringW_free[i] = DV.op(lambda e: e.tensor_tensor(
                xx, bank[:, :].rearrange("p (t c) -> p t c", t=2), xx, ALU.add))

        def A6s(b):
            a[b]["ls1"] = ln_stats(XB[:, 2 * b:2 * b + 2, 0:256], a[b]["x1"])

        def A6n(b):
            s = a[b]
            s["qn"] = ln_apply(s["ls1"], XB[:, 2 * b:2 * b + 2, 0:256], QN, got(b - 1, "qT"))

        l_cx = [lane("l_cx0")]
        l_sp = [lane("l_sp0"), lane("l_sp1")]

        def A6l(b):
            r = 0
            SP.wait(a[b - 1]["cT"] if b >= 1 else None)
            a[b]["cx"] = SP.dma(l_cx[r], lambda e: e.dma_start(Cn[:, r, :, :], ctx_in[b].rearrange("(t p) d -> p t d", p=128)))

        def A6c(b):
            s = a[b]
            v = SPL[:, 0, :].rearrange("p (s h k c) -> p s h k c", s=2, h=2, k=2)
            tp = transpose_pair([Cn[:, 0, 0, :], Cn[:, 0, 1, :]], [s["cx"]])
            s["cT"] = tp[2]
            s["tc"] = split_T(*tp, v[:, 1, 0, :, :], v[:, 1, 1, :, :], got(b - 1, "spl"), got(b - 1, "gate"))

        def A6q(b):
            s = a[b]
            v = SPL[:, 0, :].rearrange("p (s h k c) -> p s h k c", s=2, h=2, k=2)
            tp = transpose_pair([QN[:, 0, :], QN[:, 1, :]], [s["qn"]])
            s["qT"] = tp[2]
            s["tq"] = split_T(*tp, v[:, 0, 0, :, :], v[:, 0, 1, :, :], got(b - 1, "spl"), got(b - 1, "gate"))
            SP.wait(s["tc"], s["tq"])
            s["spl"] = SP.dma(l_sp[b % 2], lambda e: e.dma_start(qsc[b], SPL[:, 0, :]))

        def A6g(b):
            s = a[b]
            v = SPL[:, 0, :].rearrange("p (s h k c) -> p s h k c", s=2, h=2, k=2)
            PE.wait(s["tc"], s["tq"], t_wgs)
            for tt in range(2):
                n = 0
                c = 16 * (2 * b + tt)
                for sx in range(2):
                    for dk in range(2):
                        for hx, hw in ((0, 0), (0, 1), (1, 0)):
                            t = PE.op(lambda e, sx=sx, dk=dk, hx=hx, hw=hw, tt=tt, n=n, c=c: e.matmul(
                                gates[:, c:c + 16], v[:, sx, hx, dk, 128 * tt:128 * tt + 128],
                                WGs[:, dk, hw, 16 * sx:16 * sx + 16], start=n == 0, stop=n == 11), n == 11 and tt == 1)
                            n += 1
            s["gate"] = t

        QN = sb("QN", [128, 2, 256], F32, ca)
        zfill = sb("zfill", [128, ROW], F32, ca)
        t_z = PO.op(lambda e: e.memset(zfill[:, :], 0.0))
        l_z = lane("l_z")
        for i in range(1, 4):
            load_x(i)
        SP.wait(t_z)
        t_zf = None
        t_zf = SP.dma(l_z, lambda e: e.dma_start(
            xs.rearrange("(n p) c -> p n c", p=128),
            zfill[:, :].rearrange("p (a c) -> p a c", a=1).broadcast_to([128, NTILE, ROW])))
        t_zf = SP.dma(l_z, lambda e: e.dma_start(out[TOK:TOK + 128, :], zfill[:, 0:256]))

        wchunk = [0]

        def prep(dst, src, width, n):
            cs = []
            for _ in range(n):
                if wchunk[0] < 32:
                    cs.append(chunk(dst, src, width, wchunk[0]))
                    wchunk[0] += 1
            return cs

        def ok(b):
            return 0 <= b < B

        for h in range(-4, 2 * B + 5):
            i, P = h // 2, h % 2
            b3, P3 = (h - 1) // 2, (h - 1) % 2
            bv_ = (h - 2) // 2
            nb, nP = (h + 1) // 2, (h + 1) % 2
            pend = prep(WU, wup, 128, 1) if h >= 0 else []
            for j in range(4):
                if ok(i) and j < 3:
                    QM(i, P, j + 1)
                if ok(b3) and j < 3:
                    QN2(b3, P3, j + 1)
                if ok(i):
                    A2(i, P, j)
                if ok(b3):
                    A3(b3, P3, j)
                if j in (1, 2) and ok(bv_):
                    A3v(bv_, 2 * P + j - 1)
                if j == 0 and P == 0:
                    if ok(i + 2):
                        A0s(i + 2)
                    if ok(i - 3):
                        A6g(i - 3)
                if j == 1 and P == 1 and ok(i - 2):
                    A6s(i - 2)
                if j == 2:
                    for c in pend:
                        split(c)
                if j == 3:
                    if P == 0 and ok(i + 2):
                        A0n(i + 2)
                    if P == 1 and ok(i - 2):
                        A6n(i - 2)
            if ok(i):
                A2e(i, P)
            if P == 0:
                if ok(i + 1):
                    A1(i + 1, "k", 0)
                    A1(i + 1, "k", 1)
                if ok(i - 2):
                    A5(i - 2)
                if ok(i):
                    A2t(i, P)
            else:
                if ok(i + 2):
                    A0(i + 2)
                if ok(i + 1):
                    A1v(i + 1)
                if ok(i):
                    A2t(i, P)
            if ok(nb):
                QM(nb, nP, 0)
            if ok(i):
                QN2(i, P, 0)
            if P == 0:
                if ok(i + 1):
                    A1(i + 1, "q", 0)
                    A1(i + 1, "q", 1)
            else:
                if ok(i - 2):
                    A6c(i - 2)
                if ok(i - 1):
                    A4(i - 1, 0)
                if ok(i - 2):
                    A6q(i - 2)
                if ok(i - 1):
                    A4(i - 1, 1)
                    A4b(i - 1)
                if ok(i - 1):
                    A6l(i - 1)

        def barrier():
            toks = [q.now() for q in (PE, DV, AC, PO)]
            for q in (PE, DV, AC, PO, SP):
                q.wait(*toks)

        barrier()
        for q in (DV, AC, PE, PO):
            q.wait(*[a[b]["spl"] for b in (B - 2, B - 1)], *[a[b]["ost", k] for b in (B - 1,) for k in (0, 1)], t_zf)
        ca.close()

        WD = sb("WD", [128, E * 4096], BF)
        cg = ExitStack()
        G = sb("G", [128, NT, 16], F32, cg)
        gi = sb("gi", [128, 256], F32, cg)
        gf = sb("gf", [128, 256], F32, cg)
        zz = sb("zz", [128, 256], F32, cg)
        cs_ = sb("cs_", [128, 256], F32, cg)
        gg_ = sb("gg_", [128, 256], F32, cg)
        MM = sb("MM", [128, 256], F32, cg)
        r1 = sb("r1", [128, 2, 256], F32, cg)
        pp = sb("pp", [128, 6, 256], BF, cg)

        DV.op(lambda e: e.memset(zz[:, :], 0.0))
        t = DV.op(lambda e: e.tensor_tensor(
            G[:, :, :], gates[:, :].rearrange("p (t c) -> p t c", c=16),
            BG[:, 0:16].rearrange("p (a c) -> p a c", a=1).broadcast_to([128, NT, 16]), ALU.add))
        AC.wait(t)
        t = AC.op(lambda e: e.activation(G[:, :, :], G[:, :, :], ACT.Tanh, scale=1.0 / 15.0))
        PE.wait(t)
        Gv = G[:, :, :].rearrange("p (b t) (k h) -> p t k b h", t=2, h=8)
        GT = sb("GT", [128, 4, 128], F32, cg)
        DV.wait(t)
        for k in range(2):
            for tt in range(2):
                t = DV.op(lambda e, k=k, tt=tt: e.tensor_scalar(
                    GT[:, 2 * k + tt, :].rearrange("p (b h) -> p b h", h=8), Gv[:, tt, k, :, :], 15.0, None, ALU.mult))
        PE.wait(t)
        for k in range(4):
            t = PE.op(lambda e, k=k: e.transpose(banks[0][:, 128 * k:128 * k + 128], GT[:, k, :], idf), k == 3)
        DV.wait(t)
        t = DV.op(lambda e: e.tensor_copy(gi[:, :], banks[0][:, 0:256]))
        AC.wait(t)
        t = AC.op(lambda e: e.activation(gf[:, :], banks[0][:, 256:512], ACT.Exp, scale=-1.0))
        AC.wait(t)
        t = AC.op(lambda e: e.activation(gf[:, :], gf[:, :], ACT.Ln, bias=1.0))
        DV.wait(t)
        t = DV.op(lambda e: e.tensor_tensor_scan(cs_[:, :], gf[:, :], zz[:, :], 0.0, ALU.add, ALU.add))
        DV.wait(t)
        t = DV.op(lambda e: e.tensor_tensor(gg_[:, :], gi[:, :], cs_[:, :], ALU.add))
        DV.wait(t)
        t = DV.op(lambda e: e.tensor_tensor_scan(MM[:, :], gg_[:, :], gg_[:, :], NEG, ALU.max, ALU.max))
        DV.wait(t)
        t = DV.op(lambda e: e.tensor_tensor(cs_[:, :], cs_[:, :], MM[:, :], ALU.subtract))
        AC.wait(t)
        t_em = AC.op(lambda e: e.activation(cs_[:, :], cs_[:, :], ACT.Exp))
        PE.wait(t_em)
        for tt in range(2):
            t_em = PE.op(lambda e, tt=tt: e.transpose(banks[1][:, 128 * tt:128 * tt + 128], cs_[:, 128 * tt:128 * tt + 128], idf), tt == 1)
        DV.op(lambda e: e.tensor_scalar(MM[:, :], MM[:, :], -1.0, None, ALU.mult))
        DV.wait(DV.now())
        for k, src in enumerate((gg_, MM)):
            DV.op(lambda e, k=k, src=src: e.tensor_copy(pp[:, 3 * k, :], src[:, :]))
            DV.wait(DV.now())
            DV.op(lambda e, k=k, src=src: e.tensor_tensor(r1[:, 0, :], src[:, :], pp[:, 3 * k, :], ALU.subtract))
            DV.wait(DV.now())
            DV.op(lambda e, k=k: e.tensor_copy(pp[:, 3 * k + 1, :], r1[:, 0, :]))
            DV.wait(DV.now())
            DV.op(lambda e, k=k: e.tensor_tensor(r1[:, 1, :], r1[:, 0, :], pp[:, 3 * k + 1, :], ALU.subtract))
            DV.wait(DV.now())
            DV.op(lambda e, k=k: e.tensor_copy(pp[:, 3 * k + 2, :], r1[:, 1, :]))
            DV.wait(DV.now())
        t = DV.now()
        l_g = lane("l_g")
        SP.wait(t)
        t_g = SP.dma(l_g, lambda e: e.dma_start(gsc.rearrange("k p c -> p k c"), pp[:, :, :]))
        DV.wait(t_em)
        t_em = DV.op(lambda e: e.tensor_copy(EM[:, :, :], banks[1][:, 0:256].rearrange("p (t c) -> p t c", t=2)))
        barrier()
        for q in (PE, DV, AC, PO, SP):
            q.wait(t_g)
        cg.close()

        cb = ExitStack()
        QC = sb("QC", [128, 2, 1024], BF, cb)
        LH = WD[:, 24576:28672].rearrange("p (r h c) -> p r h c", r=2, h=8)
        RH = WD[:, 28672:32768].rearrange("p (r h c) -> p r h c", r=2, h=8)
        CX = sb("CX", [128, 2, 2, 256], F32, cb)
        SD = sb("SD", [128, 6, 512], F32, cb)
        dsel = CF[:, C_MASK:C_MASK + 64].rearrange("p (k c) -> p k c", k=2)
        OB = sb("OB", [128, 768], F32, cb)
        QB = sb("QB", [128, 4, 1024], BF, cb)
        sq = sb("sq", [128, 2, 256], F32, cb)
        sm = sb("sm", [128, 5, 2, 8], F32, cb)
        hh = sb("hh", [128, 2, 256], F32, cb)
        x3T = sb("x3T", [128, 2, 2, 256], BF, cb)

        t = DV.op(lambda e: e.memset(WD[:, 24576:32768], 0.0))
        DV.wait(t)
        t_qz = DV.op(lambda e: e.memset(QB[:, :, :], 0.0))
        t_lr = DV.op(lambda e: e.memset(WD[0:6, 24576:32768], 1.0))
        PO.op(lambda e: e.memset(dsel[:, :, :], 0.0))
        PO.wait(PO.now())
        PO.op(lambda e: e.memset(dsel[:, 0, 0:1], 1.0))
        t_ds = PO.op(lambda e: e.memset(dsel[:, 1, 1:2], 1.0))

        l_qc = [lane(f"l_qc{k}") for k in range(2)]
        l_lh = [lane(f"l_lh{k}") for k in range(2)]
        l_rh = [lane(f"l_rh{k}") for k in range(2)]
        l_cb = [lane(f"l_cb{k}") for k in range(2)]
        bb_ = [dict() for _ in range(B)]

        def B1(b):
            r = b % 2
            s = bb_[b]
            p = bb_[b - 2] if b >= 2 else {}
            SP.wait(p.get("S"), p.get("PV"), t_g)
            s["qc"] = SP.dma(l_qc[r], lambda e: e.dma_start(QC[:, r, :], qsc[b, :, 1024:2048]))
            s["cx"] = SP.dma(l_cb[r], lambda e: e.dma_start(CX[:, r, :, :], ctx_in[b].rearrange("(t p) d -> p t d", p=128)))

        def B1g(b):
            s = bb_[b]
            r = b % 2
            SP.wait(bb_[b - 2]["D"] if b >= 2 else None, t_lr, t_g)
            s["lh"] = SP.dma(l_lh[r], lambda e: e.dma_start(LH[0:3, r, :, :], gsc[0:3, 8 * b:8 * b + 8, :]))
            s["rh"] = SP.dma(l_rh[r], lambda e: e.dma_start(RH[3:6, r, :, :], gsc[3:6, 8 * b:8 * b + 8, :]))

        sdb, sdb_free = [(banks[0], banks[1]), (banks[2], banks[3])], [None, None]
        sd_free = [None] * 6
        un = [0]
        ob, den, tb = banks[4], banks[5], banks[6]
        lgb = banks[7]
        ob_free, den_free, tb_free = [None], [None], [None]

        qb_free = [None] * 4
        l_qb = [lane(f"l_qb{k}") for k in range(4)]

        def BQ(b, j):
            s = bb_[b]
            SP.wait(t_qz, qb_free[j])
            s["QB", j] = SP.dma(l_qb[j], lambda e: e.dma_start(
                QB[32 * j:32 * j + 32, j, :], qsc[b, 32 * j:32 * j + 32, 0:1024]))

        def B2u(b, st, j):
            r = b % 2
            s = bb_[b]
            k2, k6 = un[0] % 2, un[0] % 6
            un[0] += 1
            sbk, dbk = sdb[k2]
            w = 256 if st == 0 else 128
            t0, s0 = 256 - w, 128 * st
            v = QC[:, r, :].rearrange("p (h k c) -> p h k c", h=2, k=2)
            q = QB[:, j, :].rearrange("p (h k c) -> p h k c", h=2, k=2)
            PE.wait(sdb_free[k2], s["lh"], s["rh"], s["qc"])
            for dk in range(2):
                t = PE.op(lambda e, dk=dk: e.matmul(
                    dbk[:, w * dk:w * dk + w], LH[:, r, 4 * dk + j, s0:s0 + 128], RH[:, r, 4 * dk + j, t0:256],
                    start=True, stop=True), dk == 1)
            s["D"] = t
            AC.wait(t, sd_free[k6])
            te = AC.op(lambda e: e.activation(SD[:, k6, 0:2 * w], dbk[:, 0:2 * w], ACT.Exp))
            PE.wait(s["QB", j])
            for dk in range(2):
                for n, (hc, hq) in enumerate(((0, 0), (0, 1), (1, 0))):
                    t = PE.op(lambda e, dk=dk, n=n, hc=hc, hq=hq: e.matmul(
                        sbk[:, w * dk:w * dk + w], v[:, hc, dk, s0:s0 + 128], q[:, hq, dk, t0:256],
                        start=n == 0, stop=n == 2), dk == 1 and n == 2)
            s["S"] = t
            if st == 1:
                qb_free[j] = t
            DV.wait(te, t)
            t1 = DV.op(lambda e: e.tensor_tensor(SD[:, k6, 0:2 * w], sbk[:, 0:2 * w], SD[:, k6, 0:2 * w], ALU.mult))
            sdb_free[k2] = t1
            PO.wait(t1)
            dg = SD[:, k6, 0:2 * w].rearrange("p (j c) -> p j c", c=w)[:, :, 0:128]
            s["SD", st, j] = (k6, PO.op(lambda e: e.affine_select(
                out=dg, in_=dg, pattern=[[0, 2], [1, 128]], compare_op=ALU.is_ge, fill=0.0, base=0, channel_multiplier=-1)))

        def B2v(b, st):
            r = b % 2
            s = bb_[b]
            if st == 0:
                PE.wait(ob_free[0], den_free[0], t_ds, s["cx"])
            w = 256 if st == 0 else 128
            o0 = 256 - w
            sl = [s["SD", st, j][0] for j in range(4)]
            PE.wait(*[s["SD", st, j][1] for j in range(4)])
            for dk in range(2):
                for j in range(4):
                    PE.op(lambda e, j=j, dk=dk: e.matmul(
                        ob[32 * j:32 * j + 32, 256 * dk + o0:256 * dk + 256], CX[:, r, st, 128 * dk + 32 * j:128 * dk + 32 * j + 32],
                        SD[:, sl[j], w * dk:w * dk + w], start=st == 0 and dk == 0, stop=st == 1 and dk == 1,
                        skip_group_check=True), False)
            for dk in range(2):
                for j in range(4):
                    t = PE.op(lambda e, j=j, dk=dk: e.matmul(
                        den[32 * j:32 * j + 32, o0:256], dsel[:, dk, :], SD[:, sl[j], w * dk:w * dk + w],
                        start=dk == 0 and st == 0, stop=dk == 1 and st == 1,
                        skip_group_check=True), dk == 1 and j == 3)
            for j in range(4):
                sd_free[sl[j]] = t
            s["PV"] = t

        l_x2 = [lane(f"l_x2{k}") for k in range(2)]
        ISQ = float(1.0 / (32.0 ** 0.5))

        def B3(b):
            s = bb_[b]
            r = b % 2
            prev = bb_[b - 1] if b >= 1 else {}
            AC.wait(s["PV"], prev.get("obT"))
            ob_free[0] = AC.op(lambda e: e.activation(OB[:, 0:512], ob[:, :], ACT.Copy))
            den_free[0] = t = AC.op(lambda e: e.activation(OB[:, 512:768], den[:, 0:256], ACT.Copy))
            s["ob"] = t

        ISQ32 = float(1.0 / 32.0)
        hh_free = [None]

        def B4(b):
            s = bb_[b]
            r = b % 2
            PE.wait(s["ob"], tb_free[0])
            for tt in range(2):
                for k in range(2):
                    PE.op(lambda e, k=k, tt=tt: e.transpose(
                        tb[:, 256 * tt + 128 * k:256 * tt + 128 * k + 128], OB[:, 256 * k + 128 * tt:256 * k + 128 * tt + 128], idf), False)
            PE.wait(sm_free[0])
            for tt in range(2):
                t = PE.op(lambda e, tt=tt: e.transpose(
                    lgb[:, 256 + 128 * tt:384 + 128 * tt], OB[:, 512 + 128 * tt:640 + 128 * tt], idf), tt == 1)
            s["obT"] = t
            AC.wait(t, hh_free[0])
            t_s = AC.op(lambda e: e.activation(sq[:, :, :], tb[:, :].rearrange("p (t c) -> p t c", t=2), ACT.Square, scale=ISQ32))
            t_h = AC.op(lambda e: e.activation(hh[:, :, :], tb[:, :].rearrange("p (t c) -> p t c", t=2), ACT.Copy, scale=ISQ))
            tb_free[0] = t_h
            em = EM[:, :, 8 * b:8 * b + 8].rearrange("p t (k j) -> p t k j", k=2)
            v4 = [sm[:, k, :, :].rearrange("p t (k j) -> p t k j", k=2) for k in range(5)]

            def dsum(tt):
                return lgb[:, 256 + 128 * tt:384 + 128 * tt].rearrange("p (j c) -> p c j", c=32)[:, 0:2, :]

            DV.wait(t, hh_free[0])
            for tt in range(2):
                t = DV.op(lambda e, tt=tt: e.tensor_scalar(v4[4][:, tt], dsum(tt), ISQ, None, ALU.mult))
            DV.wait(t, t_em)
            for tt in range(2):
                t = DV.op(lambda e, tt=tt: e.scalar_tensor_tensor(v4[0][:, tt], dsum(tt), -ISQ, v4[4][:, tt], ALU.mult, ALU.max))
            sm_free[0] = t
            DV.wait(t)
            t = DV.op(lambda e: e.tensor_tensor(sm[:, 1, :, :], sm[:, 0, :, :], EM[:, :, 8 * b:8 * b + 8], ALU.max))
            DV.wait(t)
            t = DV.op(lambda e: e.tensor_scalar(sm[:, 0, :, :], sm[:, 1, :, :], 5e-5, None, ALU.add))
            DV.wait(t)
            DV.op(lambda e: e.tensor_tensor(sm[:, 1, :, :], sm[:, 0, :, :], sm[:, 0, :, :], ALU.mult))
            DV.wait(t_s)
            t = DV.op(lambda e: e.tensor_reduce(sm[:, 2, :, :], sq[:, :, :].rearrange("p t (h c) -> p t h c", c=32), AX.X, ALU.add))
            DV.wait(t)
            t = DV.op(lambda e: e.scalar_tensor_tensor(sm[:, 3, :, :], sm[:, 1, :, :], 1e-6, sm[:, 2, :, :], ALU.mult, ALU.add))
            s["ms"] = t
            s["hh"] = t_h

        def B4p(b):
            s = bb_[b]
            PO.wait(s["ms"])
            s["rs"] = PO.op(lambda e: e.tensor_tensor(
                sm[:, 4, :, :], sm[:, 3, :, :], mhalf[:, :].rearrange("p (a c) -> p a c", a=1).broadcast_to([128, 2, 8]), ALU.pow))

        def B4x(b):
            s = bb_[b]
            r = b % 2
            DV.wait(s["rs"], s["hh"])
            hv = hh[:, :, :].rearrange("p t (h c) -> p (t h) c", c=32)
            t = DV.op(lambda e: e.tensor_tensor(
                hv, hv, sm[:, 4, :, :].rearrange("p t (h a) -> p (t h) a", a=1).broadcast_to([128, 16, 32]), ALU.mult))
            DV.wait(t, t_gn)
            t = DV.op(lambda e: e.tensor_tensor(
                hh[:, :, :], hh[:, :, :], GN[:, :].rearrange("p (a c) -> p a c", a=1).broadcast_to([128, 2, 256]), ALU.mult))
            DV.wait(t)
            xx = XB[:, 2 * b:2 * b + 2, 0:256]
            hh_free[0] = s["x2"] = t = DV.op(lambda e: e.tensor_tensor(xx, xx, hh[:, :, :], ALU.add))

        def B4o(b):
            s = bb_[b]
            r = b % 2
            SP.wait(s["x2"])
            ov = out[0:TOK, :].rearrange("(t p) d -> p t d", p=128)
            s["x2o"] = SP.dma(l_x2[r], lambda e: e.dma_start(ov[:, 2 * b:2 * b + 2, :], XB[:, 2 * b:2 * b + 2, 0:256]))

        sm_free = [None]

        def B5s(b):
            bb_[b]["ls"] = ln_stats(XB[:, 2 * b:2 * b + 2, 0:256], bb_[b]["x2"])

        def B5n(b):
            xx = XB[:, 2 * b:2 * b + 2, 0:256]
            bb_[b]["x3"] = ln_apply(bb_[b]["ls"], xx, xx, bb_[b]["x2o"])

        def B5(b):
            s = bb_[b]
            PE.wait(s["x3"], tb_free[0])
            for tt in range(2):
                for dk in range(2):
                    t = PE.op(lambda e, tt=tt, dk=dk: e.transpose(
                        tb[:, 256 * dk + 128 * tt:256 * dk + 128 * tt + 128], XB[:, 2 * b + tt, 128 * dk:128 * dk + 128], idf),
                        tt == 1 and dk == 1)
            bv = tb[:, :].rearrange("p (k c) -> p k c", k=2)
            AC.wait(t, bb_[b - 1]["lg"] if b >= 1 else None)
            th = AC.op(lambda e: e.activation(x3T[:, 0, :, :], bv, ACT.Copy))
            DV.wait(th)
            tl = DV.op(lambda e: e.tensor_tensor(x3T[:, 1, :, :], bv, x3T[:, 0, :, :], ALU.subtract))
            tb_free[0] = tl
            s["x3T"] = tl

        def B6(b):
            s = bb_[b]
            PE.wait(s["x3T"], sm_free[0])
            for tt in range(2):
                n = 0
                c = 8 * (2 * b + tt)
                for dk in range(2):
                    for hx, hw in ((0, 0), (0, 1), (1, 0)):
                        t = PE.op(lambda e, dk=dk, hx=hx, hw=hw, tt=tt, n=n, c=c: e.matmul(
                            lgb[:, c:c + 8], x3T[:, hx, dk, 128 * tt:128 * tt + 128], WGs[:, dk, hw, 32:40],
                            start=n == 0, stop=n == 5), n == 5 and tt == 1)
                        n += 1
            s["lg"] = t

        wchunk[0] = 0
        pend = []
        B1(0)
        B1g(0)
        B1(1)
        B1g(1)
        todo = []
        for j in range(4):
            BQ(0, j)
        for i in range(B + 4):
            pend = prep(WD, wdn, 256, 2) if i < B and wchunk[0] < 24 else []
            for n in range(8):
                if i < B:
                    B2u(i, n // 4, n % 4)
                if n >= 4 and i + 1 < B:
                    BQ(i + 1, n - 4)
                if n in (1, 5) and todo:
                    B2v(*todo[0])
                    if todo[0][1] == 1:
                        B3(todo[0][0])
                    todo.pop(0)
                if n == 3 and i < B:
                    todo.append((i, 0))
                if n == 7 and i < B:
                    todo.append((i, 1))
                if n in (0, 6) and pend:
                    splitb(pend.pop(0))
                if n == 1 and 1 <= i < B - 1:
                    B1(i + 1)
                    B1g(i + 1)
                if n == 2 and 0 <= i - 1 < B:
                    B4(i - 1)
                if n == 4 and 0 <= i - 1 < B:
                    B4p(i - 1)
                if n == 7 and 0 <= i - 1 < B:
                    B4x(i - 1)
                if n == 0 and 0 <= i - 2 < B:
                    B4o(i - 2)
                if n == 3 and 0 <= i - 2 < B:
                    B5s(i - 2)
                if n == 5 and 0 <= i - 2 < B:
                    B5n(i - 2)
                if n == 0 and 0 <= i - 3 < B:
                    B5(i - 3)
                if n == 1 and 0 <= i - 3 < B:
                    B6(i - 3)

        barrier()
        cb.close()

        for _ in range(4):
            for c in prep(WD, wdn, 256, 2):
                split(c)
        cr = ExitStack()
        TE = sb("TE", [128, NTILE], F32)
        TEi = sb("TEi", [128, NTILE], I32)
        names = ("lg_", "pr", "eq", "ky", "o1", "o2", "mk", "tot", "cum", "pf")
        T = {n: sb("c_" + n, [128, NT, E], F32, cr) for n in names}
        mkbt = sb("mkbt", [128, E, NT], BF, cr)
        m32 = {n: sb("c_" + n, [128, NT], F32, cr) for n in ("mx1", "sm", "k1", "w2t", "s1", "s2")}
        sl1 = sb("sl1", [128, NT], I32, cr)
        sl2 = sb("sl2", [128, NT], I32, cr)
        t8 = sb("t8", [128, 8, E], F32, cr)
        t8i = sb("t8i", [128, E], I32, cr)
        te8 = sb("te8", [128, NTILE, E], F32, cr)

        def dv(fn):
            t = DV.op(fn)
            DV.wait(t)
            return t

        def bc(x):
            return x[:, :].rearrange("p (t a) -> p t a", a=1).broadcast_to([128, NT, E])

        def cb8(x):
            return x.rearrange("p (a c) -> p a c", a=1).broadcast_to([128, NT, E])

        ek = cb8(CF[:, C_EK:C_EK + 8])
        dv(lambda e: e.tensor_tensor(T["lg_"][:, :, :], lgb[:, 0:256].rearrange("p (t c) -> p t c", c=8), cb8(BG[:, 16:24]), ALU.add))
        dv(lambda e: e.tensor_reduce(m32["mx1"][:, :], T["lg_"][:, :, :], AX.X, ALU.max))
        t = dv(lambda e: e.tensor_tensor(T["lg_"][:, :, :], T["lg_"][:, :, :], bc(m32["mx1"]), ALU.subtract))
        AC.wait(t)
        t = AC.op(lambda e: e.activation(T["pr"][:, :, :], T["lg_"][:, :, :], ACT.Exp))
        DV.wait(t)
        dv(lambda e: e.tensor_reduce(m32["sm"][:, :], T["pr"][:, :, :], AX.X, ALU.add))
        dv(lambda e: e.reciprocal(m32["sm"][:, :], m32["sm"][:, :]))
        dv(lambda e: e.tensor_tensor(T["pr"][:, :, :], T["pr"][:, :, :], bc(m32["sm"]), ALU.mult))

        def pick(src, wt, oh):
            dv(lambda e: e.tensor_reduce(wt, src, AX.X, ALU.max))
            dv(lambda e: e.tensor_tensor(T["eq"][:, :, :], src, wt.rearrange("p (t a) -> p t a", a=1).broadcast_to([128, NT, E]), ALU.is_equal))
            dv(lambda e: e.tensor_tensor(T["ky"][:, :, :], T["eq"][:, :, :], ek, ALU.mult))
            dv(lambda e: e.tensor_reduce(m32["k1"][:, :], T["ky"][:, :, :], AX.X, ALU.max))
            dv(lambda e: e.tensor_tensor(oh, T["ky"][:, :, :], bc(m32["k1"]), ALU.is_equal))

        pick(T["pr"][:, :, :], m32["mx1"][:, :], T["o1"][:, :, :])
        dv(lambda e: e.tensor_scalar(XB[:, :, 259], m32["k1"][:, :], -1.0, 8.0, ALU.mult, ALU.add))
        dv(lambda e: e.scalar_tensor_tensor(T["mk"][:, :, :], T["o1"][:, :, :], -2.0, T["pr"][:, :, :], ALU.mult, ALU.add))
        pick(T["mk"][:, :, :], m32["w2t"][:, :], T["o2"][:, :, :])
        dv(lambda e: e.tensor_copy(XB[:, :, 257], m32["w2t"][:, :]))
        dv(lambda e: e.tensor_tensor(XB[:, :, 258], m32["mx1"][:, :], m32["w2t"][:, :], ALU.subtract))
        dv(lambda e: e.tensor_copy(XB[:, :, 256], CF[:, C_TOK:C_TOK + 32]))
        t = dv(lambda e: e.tensor_tensor(mkbt[:, :, :].rearrange("p c t -> p t c"), T["o1"][:, :, :], T["o2"][:, :, :], ALU.add))
        PE.wait(t, t_cb, t_ones)
        mf = mkbt[:, :, :].rearrange("p c t -> p (c t)")
        PE.op(lambda e: e.matmul(banks[0][:, 0:256], Ub[:, :], mf, start=True, stop=True), False)
        t = PE.op(lambda e: e.matmul(banks[1][:, 0:256], onesb[:, :], mf, start=True, stop=True))
        DV.wait(t)
        cum = T["cum"][:, :, :].rearrange("p t c -> p (t c)")
        tot = T["tot"][:, :, :].rearrange("p t c -> p (t c)")
        pf = T["pf"][:, :, :].rearrange("p t c -> p (t c)")
        dv(lambda e: e.tensor_copy(tot, banks[1][:, 0:256]))
        dv(lambda e: e.memset(pf, 0.0))
        dv(lambda e: e.tensor_tensor_scan(cum, tot, pf, 0.0, ALU.add, ALU.add))
        dv(lambda e: e.tensor_tensor(tot, cum, tot, ALU.subtract))
        ec = tot.rearrange("p (c t) -> p c t", t=NT)
        ic = cum.rearrange("p (c t) -> p c t", t=NT)
        e0 = t8[:, 0, :]
        dv(lambda e: e.tensor_copy(e0, ec[:, :, 0]))
        dv(lambda e: e.tensor_tensor(t8[:, 1, :], ic[:, :, NT - 1], e0, ALU.subtract))
        dv(lambda e: e.tensor_scalar(t8i[:, :], t8[:, 1, :], 63.5, 1.0 / 128.0, ALU.add, ALU.mult))
        dv(lambda e: e.tensor_copy(t8[:, 2, :], t8i[:, :]))
        dv(lambda e: e.memset(t8[:, 3, :], 0.0))
        dv(lambda e: e.tensor_tensor_scan(t8[:, 4, :], t8[:, 2, :], t8[:, 3, :], 0.0, ALU.add, ALU.add))
        dv(lambda e: e.tensor_tensor(t8[:, 5, :], t8[:, 4, :], t8[:, 2, :], ALU.subtract))
        dv(lambda e: e.scalar_tensor_tensor(t8[:, 6, :], t8[:, 5, :], 128.0, e0, ALU.mult, ALU.subtract))
        dv(lambda e: e.tensor_tensor(
            te8[:, :, :], t8[:, 4, :].rearrange("p (a c) -> p a c", a=1).broadcast_to([128, NTILE, E]),
            CF[:, C_J:C_J + NTILE].rearrange("p (j a) -> p j a", a=1).broadcast_to([128, NTILE, E]), ALU.is_le))
        dv(lambda e: e.tensor_reduce(TE[:, :], te8[:, :, :], AX.X, ALU.add))
        dv(lambda e: e.tensor_scalar(TE[:, :], TE[:, :], 7.0, None, ALU.min))
        t_te = dv(lambda e: e.tensor_copy(TEi[:, :], TE[:, :]))
        dv(lambda e: e.tensor_tensor(
            ec, ec, t8[:, 6, :].rearrange("p (c a) -> p c a", a=1).broadcast_to([128, E, NT]), ALU.add))
        dv(lambda e: e.tensor_tensor(tot, banks[0][:, 0:256], tot, ALU.add))
        ect = tot.rearrange("p (c t) -> p t c", t=NT)
        for o, sx, si in ((T["o1"], "s1", sl1), (T["o2"], "s2", sl2)):
            dv(lambda e, o=o: e.tensor_tensor(o[:, :, :], o[:, :, :], ect, ALU.mult))
            dv(lambda e, o=o, sx=sx: e.tensor_reduce(m32[sx][:, :], o[:, :, :], AX.X, ALU.add))
            t = dv(lambda e, sx=sx, si=si: e.tensor_copy(si[:, :], m32[sx][:, :]))
        NS = 4
        l_sc = [lane(f"l_sc{k}") for k in range(NS)]
        PO.wait(t, t_zf, *[bb_[b]["x2o"] for b in (B - 2, B - 1)])
        n = 0
        t_sc = [None] * NS
        for tl in range(NT):
            for si in (sl1, sl2):
                k = n % NS
                n += 1
                PO.wait(t_sc[k])
                t_sc[k] = PO.dma(l_sc[k], lambda e, tl=tl, si=si: e.indirect_dma_start(
                    out=xs, out_offset=bass.IndirectOffsetOnAxis(ap=si[:, tl:tl + 1], axis=0),
                    in_=XB[:, tl, :], in_offset=None, bounds_check=SLOTS - 1, oob_is_err=True))
        for q in (PE, DV, AC, PO, SP):
            q.wait(*t_sc)
        barrier()
        cr.close()

        NX = 3
        XS = sb("XS", [128, NX, ROW], F32)
        XTs = sb("XTs", [128, 2, 2, 2, 128], BF)
        Hf = sb("Hf", [128, 2, 1024], F32)
        Hh = sb("Hh", [128, 2, 1024], BF)
        Hl = sb("Hl", [128, 2, 1024], BF)
        Yf = sb("Yf", [128, 2, 256], F32)
        yt = sb("yt", [128, 2, 256], F32)
        ix = sb("ix", [128, 3, 5], F32)
        ixi = sb("ixi", [128, 3, 1], I32)
        l_xs = [lane(f"l_xs{k}") for k in range(NX)]
        l_y = [lane(f"l_y{k}") for k in range(2)]
        f = [dict() for _ in range(NTILE)]
        xtb = [banks[0], banks[1]]
        upb = [(banks[2], banks[3]), (banks[4], banks[5])]
        yb = [banks[6], banks[7]]

        def F0(j):
            SP.wait(*(f[j - NX][k] for k in ("T", "w")) if j >= NX else ())
            f[j]["x"] = SP.dma(l_xs[j % NX], lambda e: e.dma_start(XS[:, j % NX, :], xs[128 * j:128 * j + 128, :]))

        def F1(j):
            s = f[j]
            r, rx = j % 2, j % NX
            p = f[j - 2] if j >= 2 else {}
            PE.wait(s["x"], p.get("xl"))
            for dk in range(2):
                t = PE.op(lambda e, dk=dk: e.transpose(xtb[r][:, 128 * dk:128 * dk + 128], XS[:, rx, 128 * dk:128 * dk + 128], idf), dk == 1)
            s["T"] = t
            bv = xtb[r][:, 0:256].rearrange("p (k c) -> p k c", k=2)
            AC.wait(t, p.get("up"))
            th = AC.op(lambda e: e.activation(XTs[:, r, 0, :, :], bv, ACT.Copy))
            DV.wait(th)
            s["xl"] = DV.op(lambda e: e.tensor_tensor(XTs[:, r, 1, :, :], bv, XTs[:, r, 0, :, :], ALU.subtract))
            q = j % 3
            old = f[j - 3] if j >= 3 else {"y": None, "y1": None, "sc": None}
            PO.wait(s["x"], old["y"], old["y1"], old["sc"])
            v = XS[:, rx, 256:257]
            PO.op(lambda e: e.tensor_scalar(ix[:, q, 0:1], v, 0.0, CF[:, C_DUMP:C_DUMP + 1], ALU.is_equal, ALU.mult))
            t = PO.op(lambda e: e.tensor_scalar(ix[:, q, 2:3], XS[:, rx, 259:260], TE[:, j:j + 1], XS[:, rx, 258:259], ALU.is_equal, ALU.mult))
            PO.op(lambda e: e.tensor_scalar(ix[:, q, 1:2], v, -1.0, None, ALU.add))
            PO.wait(PO.now())
            PO.op(lambda e: e.tensor_tensor(ix[:, q, 4:5], ix[:, q, 0:1], ix[:, q, 1:2], ALU.add))
            PO.wait(PO.now())
            PO.op(lambda e: e.tensor_copy(ixi[:, q, 0:1], ix[:, q, 4:5]))
            s["w"] = PO.op(lambda e: e.tensor_tensor(ix[:, q, 3:4], ix[:, q, 2:3], XS[:, rx, 257:258], ALU.add))

        def F2(j, fm):
            s = f[j]
            r = j % 2
            p = f[j - 2] if j >= 2 else {}
            if fm == 0:
                PE.wait(s["xl"], t_te)
                reg = s["reg"] = {}
                PE.raw(lambda e: reg.__setitem__("e", e.value_load(TEi[0:1, j:j + 1], min_val=0, max_val=7)))
            reg = s["reg"]
            k = fm // 4
            bank = upb[r][k]
            if fm % 4 == 0:
                PE.wait(p.get(("h", k)))
            n = 0
            for dk in range(2):
                for hw, hx in ((0, 0), (0, 1), (1, 0)):
                    off = 512 * fm + 256 * dk + 128 * hw
                    t = PE.op(lambda e, off=off, hx=hx, dk=dk, n=n: e.matmul(
                        bank[:, 128 * (fm % 4):128 * (fm % 4) + 128], WU[:, bass.ds(reg["e"] * 4096 + off, 128)],
                        XTs[:, r, hx, dk, :], start=n == 0, stop=n == 5), n == 5 and fm % 4 == 3)
                    n += 1
            if fm % 4 == 3:
                hs = slice(512 * k, 512 * k + 512)
                AC.wait(t, p.get(("hl", k)))
                s["h", k] = th = AC.op(lambda e: e.activation(Hf[:, r, hs], bank[:, :], ACT.Gelu))
                DV.wait(th, p.get("dn"))
                t2 = DV.op(lambda e: e.tensor_copy(Hh[:, r, hs], Hf[:, r, hs]))
                DV.wait(t2)
                s["hl", k] = DV.op(lambda e: e.tensor_tensor(Hl[:, r, hs], Hf[:, r, hs], Hh[:, r, hs], ALU.subtract))
                s["up"] = t

        def F3(j, fk):
            s = f[j]
            r, q = j % 2, j % 3
            p = f[j - 2] if j >= 2 else {}
            PE.wait(s["hl", fk // 4], *((p.get("y"), p.get("y1")) if fk == 0 else ()))
            reg = s["reg"]
            hsl = slice(128 * fk, 128 * fk + 128)
            PE.op(lambda e: e.matmul(
                yb[r][:, 0:512], Hh[:, r, hsl], WD[:, bass.ds(reg["e"] * 4096 + 512 * fk, 512)], start=fk == 0, stop=False,
                skip_group_check=True), False)
            t = PE.op(lambda e: e.matmul(
                yb[r][:, 0:256], Hl[:, r, hsl], WD[:, bass.ds(reg["e"] * 4096 + 512 * fk, 256)], start=False, stop=fk == 7,
                skip_group_check=True), fk == 7)
            if fk < 7:
                return
            s["dn"] = t
            AC.wait(t, s["w"], p.get("y"))
            t1 = AC.op(lambda e: e.activation(yt[:, r, :], yb[r][:, 256:512], ACT.Copy, scale=ix[:, q, 3:4]))
            s["y1"] = t1
            DV.wait(t1, s["w"], p.get("sc"))
            s["y"] = t2 = DV.op(lambda e: e.scalar_tensor_tensor(
                Yf[:, r, :], yb[r][:, 0:256], ix[:, q, 3:4], yt[:, r, :], ALU.mult, ALU.add))
            PO.wait(t2, s["w"], f[j - 1]["sc"] if j else None)
            s["sc"] = PO.dma(l_y[r], lambda e: e.indirect_dma_start(
                out=out, out_offset=bass.IndirectOffsetOnAxis(ap=ixi[:, q, 0:1], axis=0), in_=Yf[:, r, :], in_offset=None,
                bounds_check=TOK + 127, oob_is_err=True, compute_op=ALU.add))

        F0(0)
        F0(1)
        F1(0)
        for g in range(8 * NTILE + LAG):
            j, k = divmod(g, 8)
            if j < NTILE:
                F2(j, k)
            if g >= LAG:
                F3(*divmod(g - LAG, 8))
            if k == 0 and j + 2 < NTILE:
                F0(j + 2)
            if k == KF1 and j + 1 < NTILE:
                F1(j + 1)
        SP.wait(f[NTILE - 1]["sc"], f[NTILE - 2]["sc"], t_zf)
        PO.wait(f[NTILE - 1]["sc"], f[NTILE - 2]["sc"])

        with nc.Block() as block:
            @block.sync
            def _(e):
                SP.run(e)

            @block.gpsimd
            def _(e):
                PO.run(e)

            @block.scalar
            def _(e):
                AC.run(e)

            @block.vector
            def _(e):
                DV.run(e)

            @block.tensor
            def _(e):
                PE.run(e)


_INS = ["x", "ctx", "wqkv", "wout", "wg", "bg", "gain", "wr", "br", "wup", "wdn", "cst"]


def constants():
    import numpy as np
    c = np.zeros((128, C_END), np.float32)
    p = np.arange(128)
    c[:, C_ID:C_ID + 128] = np.eye(128)
    c[:, C_MASK:C_MASK + 128] = np.where(p[None, :] > p[:, None], NEG, 0.0)
    c[:, C_U:C_U + 128] = p[:, None] < p[None, :]
    for tt in range(2):
        for s in range(16):
            c[:, C_SEL + 16 * tt + s] = s == 8 * tt + p // 16
    c[:, C_M0] = p % 32 < 16
    c[:, C_M1] = -1.0 * (p % 32 >= 16)
    c[:, C_C17] = (p % 32 == 16) | (p % 32 == 17)
    c[:, C_TOK:C_TOK + 32] = 128 * np.arange(32)[None, :] + p[:, None] + 1
    c[:, C_EK:C_EK + 8] = 8 - np.arange(8)
    c[:, C_J:C_J + NTILE] = np.arange(NTILE)
    c[:, C_DUMP] = TOK + p + 1
    for j in range(4):
        c[:, C_SL + j] = p // 32 == j
    return c


def layout(inputs):
    import numpy as np
    i = {k: np.asarray(v) for k, v in inputs.items()}
    w = i["L0_attn_W_qkv"].reshape(4, 4, D, 3, 16)
    q = w[:, :, :, 0, :].transpose(2, 0, 1, 3)
    k = w[:, :, :, 1, :].transpose(2, 0, 1, 3)
    v = w[:, :, :, 2, :].transpose(2, 0, 1, 3).reshape(D, 256)
    q2 = np.concatenate([q, q], axis=3).reshape(D, 512)
    k2 = np.concatenate([k, k], axis=3).reshape(D, 512)
    wq = np.concatenate([q2, k2, v], axis=1).reshape(2, 128, 1280).transpose(1, 0, 2)
    ig = i["L0_xattn_ifgate_w"].reshape(16, 3, 2, 128)
    wg = ig.transpose(3, 2, 1, 0).reshape(128, 2, 48)
    wr = i["L0_ffn_router_w"].reshape(2, 128, 8).transpose(1, 0, 2)
    wup = i["L0_ffn_expert_up"].reshape(8, 8, 128, 2, 128).transpose(4, 0, 1, 3, 2).reshape(128, 16384)
    wdn = i["L0_ffn_expert_down"].reshape(8, 256, 8, 128).transpose(3, 0, 2, 1).reshape(128, 16384)
    arrays = {"x": i["x"], "ctx": i["ctx_1024"], "wqkv": wq, "wout": i["L0_attn_W_out"].reshape(256, 256), "wg": wg,
              "bg": i["L0_xattn_ifgate_b"], "gain": i["L0_xattn_outnorm_w"], "wr": wr, "br": i["L0_ffn_router_b"],
              "wup": wup, "wdn": wdn, "cst": constants()}
    return {n: np.ascontiguousarray(a) for n, a in arrays.items()}


def kernel(**inputs):
    import concourse.bacc as _bacc
    from concourse import mybir as _mybir
    from concourse.bass_utils import run_bass_kernel_spmd as _run

    arrays = layout(inputs)
    nc = _bacc.Bacc("TRN2", target_bir_lowering=False, num_devices=1)
    args = [nc.dram_tensor(n + "_in", arrays[n].shape, F32, kind="ExternalInput").ap() for n in _INS]
    out = nc.dram_tensor("out_d", (TOK + 128, D), F32, kind="ExternalOutput").ap()
    build(nc, *args, out)
    r = _run(nc, [{n + "_in": arrays[n] for n in _INS}], core_ids=[0])
    return r.results[0]["out_d"][:TOK].reshape(B, S, D)
```

```python
import concourse.bass as bass
from concourse import mybir
from contextlib import ExitStack

F32 = mybir.dt.float32
BF = mybir.dt.bfloat16
I32 = mybir.dt.int32
ALU = mybir.AluOpType
ACT = mybir.ActivationFunctionType
AX = mybir.AxisListType

B, S, D = 16, 256, 256
NT = B * 2
NH = 16
MH = 8
E = 8
TOK = B * S
NTILE = 71
REG = TOK + 128
XROWS = E * REG + (NTILE - TOK * 2 // 128) * 128
ROW = 260
NEG = -1.0e30
KF1 = 3
LAG = 9

C_ID, C_MASK, C_U, C_SEL, C_M0, C_M1, C_C17, C_TOK, C_EK, C_J, C_DUMP, C_SL, C_RB, C_END = (
    0, 128, 256, 384, 416, 417, 418, 419, 451, 459, 530, 531, 535, 543)


class Queue:

    def __init__(self, sem):
        self.sem, self.n, self.items, self.seen = sem, 0, [], {}

    def wait(self, *toks):
        for t in toks:
            if t is None or self.seen.get(id(t[0]), 0) >= t[1]:
                continue
            self.seen[id(t[0])] = t[1]
            self.items.append(lambda e, t=t: e.wait_ge(t[0], t[1]))

    def op(self, fn, sig=True):
        if sig:
            self.n += 1
            self.items.append(lambda e: fn(e).then_inc(self.sem, 1))
            return (self.sem, self.n)
        self.items.append(lambda e: fn(e))
        return None

    def raw(self, fn):
        self.items.append(fn)

    def dma(self, lane, fn):
        lane.n += 16
        self.items.append(lambda e: fn(e).then_inc(lane.sem, 16))
        return (lane.sem, lane.n)

    def now(self):
        return (self.sem, self.n)

    def run(self, e):
        for f in self.items:
            f(e)


class Lane:

    def __init__(self, sem):
        self.sem, self.n = sem, 0


def build(nc, x, ctx_in, wqkv, wout, wg, bg, gain, wr, br, wup, wdn, cst, out):
    xs = nc.dram_tensor("xs_scr", (XROWS, ROW), F32, kind="Internal").ap()
    osc = nc.dram_tensor("o_scr", (B, D * S), F32, kind="Internal").ap()
    qsc = nc.dram_tensor("q_scr", (B, 128, 2048), BF, kind="Internal").ap()
    gsc = nc.dram_tensor("g_scr", (6, 128, 256), BF, kind="Internal").ap()

    st = ExitStack()
    with st:
        def sb(name, shape, dt, c=st):
            return c.enter_context(nc.sbuf_tensor(name, shape, dt))

        def sem(name):
            return st.enter_context(nc.semaphore(name))

        def lane(name):
            return Lane(sem(name))

        PE, DV, AC, PO, SP = (Queue(sem("s_" + n)) for n in ("pe", "dve", "act", "pool", "sp"))

        banks = [st.enter_context(nc.psum_tensor(f"bank{i}", [128, 512], F32)) for i in range(8)]

        XB = sb("XB", [128, NT, ROW], F32)
        WU = sb("WU", [128, E * 4096], BF)
        CF = sb("CF", [128, C_END], F32)
        idb = sb("idb", [128, 128], BF)
        Ub = sb("Ub", [128, 128], BF)
        onesb = sb("onesb", [128, 128], BF)
        onesf = sb("onesf", [128, 2], F32)
        mhalf = sb("mhalf", [128, 8], F32)
        WGf = sb("WGf", [128, 2, 56], F32)
        WGs = sb("WGs", [128, 2, 2, 40], BF)
        BG = sb("BG", [128, 24], F32)
        EM = sb("EM", [128, 2, 128], F32)
        GN = sb("GN", [128, 256], F32)
        stat = sb("stat", [128, 2, 2, 8], F32)
        LS = sb("LS", [128, 2, 2, 4], F32)
        STG = sb("STG", [128, 2, 512], F32)
        idf = CF[:, C_ID:C_ID + 128]
        m0 = CF[:, C_M0:C_M0 + 1]
        m1n = CF[:, C_M1:C_M1 + 1]
        c17 = CF[:, C_C17:C_C17 + 1]

        gates = banks[7]
        ringW = [banks[k] for k in (5, 6, 0, 1, 2, 3)]

        l_c = lane("l_c")
        l_x = []
        l_w = lane("l_w")
        t_c = SP.dma(l_c, lambda e: e.dma_start(CF[:, :], cst))
        xv = x.rearrange("b (t p) d -> p (b t) d", p=128)
        t_x = []

        def load_x(t0, t1):
            i = len(l_x)
            l_x.append(lane(f"l_x{i}"))
            t_x.extend([SP.dma(l_x[i], lambda e: e.dma_start(XB[:, t0:t1, 0:256], xv[:, t0:t1, :]))] * ((t1 - t0) // 2))
        ca = ExitStack()
        WQh = sb("WQh", [128, 2, 1280], BF, ca)
        WQl = sb("WQl", [128, 2, 1280], BF, ca)
        mkb = sb("mkb", [128, 128], BF, ca)
        xn = sb("xn", [128, 2, 256], F32, ca)
        xTh = sb("xTh", [128, 2, 2, 256], BF, ca)
        xTl = sb("xTl", [128, 2, 2, 256], BF, ca)
        Qh = sb("Qh", [128, 2, 4, 256], BF, ca)
        Q1 = sb("Q1", [128, 2, 4, 256], BF, ca)
        Q2 = sb("Q2", [128, 2, 512], BF, ca)
        QM1 = sb("QM1", [128, 2, 4, 512], BF, ca)
        QM2 = sb("QM2", [128, 2, 512], BF, ca)
        K1 = sb("K1", [128, 2, 4, 256], BF, ca)
        K2 = sb("K2", [128, 2, 4, 256], BF, ca)
        Ym = sb("Ym", [128, 2, 256], BF, ca)
        Vp = sb("Vp", [128, 2, 2, NH * 17 + 15], F32, ca)
        Vv = Vp[:, :, :, 0:NH * 17].rearrange("p r t (n c) -> p r t n c", c=17)
        mx = sb("mx", [128, 2, 2, 8], F32, ca)
        Mp = sb("Mp", [128, 2, 8, 32], BF, ca)
        PT = sb("PT", [128, 2, 4, 2, 384], F32, ca)
        OTs = sb("OTs", [128, 4, 256], F32, ca)
        rc = sb("rc", [128, 2, NH], F32, ca)
        wsq = sb("wsq", [128, 2, NH], F32, ca)
        On = sb("On", [128, 2, NH, 16], F32, ca)
        Mm = sb("Mm", [128, 2, 2, 256], F32, ca)
        Cn = sb("Cn", [128, 1, 2, 256], F32, ca)
        WQf = PT[:, :, :, :, :].rearrange("p a j g c -> p (a j g c)")[:, 0:2560].rearrange("p (k c) -> p k c", k=2)
        WO = OTs[:, 0:2, :]
        wtmp = OTs[:, 2, :]
        SPL = sb("SPL", [128, 1, 2048], BF, ca)

        load_x(0, 2)
        t_w = SP.dma(l_w, lambda e: e.dma_start(WQf, wqkv))
        load_x(2, 8)
        l_wo = lane("l_wo")
        t_wo = SP.dma(l_wo, lambda e: e.dma_start(WO, wout.rearrange("(k p) d -> p k d", p=128)))

        l_wg = lane("l_wg")
        SP.dma(l_wg, lambda e: e.dma_start(WGf[:, :, 0:48], wg))
        SP.dma(l_wg, lambda e: e.dma_start(WGf[:, :, 48:56], wr))
        SP.dma(l_wg, lambda e: e.dma_start(BG[:, 0:16], bg.rearrange("(a n) -> a n", a=1).broadcast_to([128, 16])))
        SP.dma(l_wg, lambda e: e.dma_start(BG[:, 16:24], br.rearrange("(a n) -> a n", a=1).broadcast_to([128, 8])))
        t_wg = SP.dma(l_wg, lambda e: e.dma_start(GN[:, :], gain.rearrange("(a n) -> a n", a=1).broadcast_to([128, 256])))
        load_x(8, 16)
        load_x(16, 32)

        t_half = PO.op(lambda e: e.memset(mhalf[:, :], -0.5))
        t_vz = PO.op(lambda e: e.memset(Vp[:, :, :, :], 0.0))
        t_mpz = PO.op(lambda e: e.memset(Mp[:, :, :, :], 0.0))
        PO.wait(t_vz)
        t_vz = PO.op(lambda e: e.memset(Vv[:, :, :, :, 16:17].rearrange("p r t n c -> p (r t) (n c)"), 1.0))
        PO.op(lambda e: e.memset(onesb[:, :], 1.0))
        t_ones = PO.op(lambda e: e.memset(onesf[:, :], 1.0))
        DV.wait(t_c)
        DV.op(lambda e: e.tensor_copy(idb[:, :], idf))
        DV.op(lambda e: e.tensor_copy(mkb[:, :], CF[:, C_MASK:C_MASK + 128]))
        t_cb = DV.op(lambda e: e.tensor_copy(Ub[:, :], CF[:, C_U:C_U + 128]))
        l_st = [lane("l_st0"), lane("l_st1")]
        stg_free = [None, None]
        chunk_n = [0]

        def chunk(dst, src, width, c):
            i = chunk_n[0] % 2
            chunk_n[0] += 1
            SP.wait(stg_free[i])
            tl = SP.dma(l_st[i], lambda e: e.dma_start(STG[:, i, :], src[:, 512 * c:512 * c + 512]))
            v = dst[:, 1024 * c:1024 * c + 1024].rearrange("p (a h w) -> p a h w", h=2, w=width)
            s = STG[:, i, :].rearrange("p (a w) -> p a w", w=width)
            return i, tl, v, s

        def split(c4):
            i, tl, v, s = c4
            PO.wait(tl)
            t = PO.op(lambda e: e.tensor_copy(v[:, :, 0, :], s))
            PO.wait(t)
            stg_free[i] = PO.op(lambda e: e.tensor_tensor(v[:, :, 1, :], s, v[:, :, 0, :], ALU.subtract))

        def splitb(c4):
            i, tl, v, s = c4
            AC.wait(tl)
            t = AC.op(lambda e: e.activation(v[:, :, 0, :], s, ACT.Copy))
            DV.wait(t)
            stg_free[i] = DV.op(lambda e: e.tensor_tensor(v[:, :, 1, :], s, v[:, :, 0, :], ALU.subtract))

        ringW_free = [None] * 6
        t_wl = t_wsq = t_gn = t_wgs = None
        ringW_n = [0]

        def wbank(need_pe=True):
            i = ringW_n[0] % 6
            ringW_n[0] += 1
            PE.wait(ringW_free[i])
            return i, ringW[i]

        stat_n = [0]
        stat_free = [None, None]

        def ln_stats(src, *toks):
            k = stat_n[0] % 2
            stat_n[0] += 1
            mv = LS[:, k, :, :]
            DV.wait(*toks, stat_free[k])
            for tt in range(2):
                t = DV.op(lambda e, tt=tt: e.bn_stats(stat[:, k, tt, 0:6], src[:, tt, :]))
            DV.wait(t)
            for tt in range(2):
                t = DV.op(lambda e, tt=tt: e.bn_aggr(mv[:, tt, 0:2], stat[:, k, tt, 0:6]))
            DV.wait(t)
            t = DV.op(lambda e: e.tensor_scalar(mv[:, :, 2], mv[:, :, 1], 1e-5, None, ALU.add))
            PO.wait(t, t_half)
            return k, PO.op(lambda e: e.tensor_tensor(mv[:, :, 3], mv[:, :, 2], mhalf[:, 0:2], ALU.pow))

        def ln_apply(kt, src, dst, *toks):
            k, t = kt
            DV.wait(t, *toks)
            for tt in range(2):
                t = DV.op(lambda e, tt=tt: e.tensor_scalar(
                    dst[:, tt, :], src[:, tt, :], LS[:, k, tt, 0:1], LS[:, k, tt, 3:4], ALU.subtract, ALU.mult))
            stat_free[k] = t
            return t

        def transpose_pair(src2, toks):
            i, bank = wbank()
            PE.wait(*toks, t_c)
            for tt in range(2):
                for dk in range(2):
                    t = PE.op(lambda e, tt=tt, dk=dk: e.transpose(
                        bank[:, 256 * dk + 128 * tt:256 * dk + 128 * tt + 128], src2[tt][:, 128 * dk:128 * dk + 128], idf),
                        tt == 1 and dk == 1)
            return i, bank, t

        def split_T(i, bank, t, hi, lo, *free):
            bv = bank[:, :].rearrange("p (k c) -> p k c", k=2)
            AC.wait(t, *free)
            th = AC.op(lambda e: e.activation(hi, bv, ACT.Copy))
            DV.wait(th)
            tl = DV.op(lambda e: e.tensor_tensor(lo, bv, hi, ALU.subtract))
            ringW_free[i] = tl
            return tl

        a = [dict() for _ in range(B)]

        def got(b, key):
            return a[b].get(key) if 0 <= b < B else None

        def A0s(b):
            xx = XB[:, 2 * b:2 * b + 2, 0:256]
            a[b]["ls"] = ln_stats(xx, t_x[b])

        def A0n(b):
            s = a[b]
            xx = XB[:, 2 * b:2 * b + 2, 0:256]
            s["xn"] = ln_apply(s["ls"], xx, xn, got(b - 1, "xT_done"), t_x[b])

        def A0(b):
            r = b % 2
            s = a[b]
            tp = transpose_pair([xn[:, 0, :], xn[:, 1, :]], [s["xn"]])
            s["xT_done"] = tp[2]
            s["xTl"] = split_T(*tp, xTh[:, r, :, :], xTl[:, r, :, :], got(b - 2, "Vproj"))

        def A1(b, which, g2):
            r = b % 2
            s = a[b]
            PE.wait(s["xTl"], t_wl)
            i, bank = wbank()
            col = 0 if which == "q" else 512
            for gg in range(2):
                c = col + 128 * (2 * g2 + gg)
                n = 0
                for dk in range(2):
                    for w, v in ((WQh, xTh), (WQh, xTl), (WQl, xTh)):
                        t = PE.op(lambda e, w=w, v=v, dk=dk, c=c, gg=gg, n=n: e.matmul(
                            bank[:, 256 * gg:256 * gg + 256], w[:, dk, c:c + 128], v[:, r, dk, :],
                            start=n == 0, stop=n == 5), n == 5 and gg == 1)
                        n += 1
            bv = bank[:, :].rearrange("p (g c) -> p g c", g=2)
            gs = slice(2 * g2, 2 * g2 + 2)
            if which == "q":
                AC.wait(t, got(b - 2, "Q2"))
                th = AC.op(lambda e: e.activation(Qh[:, r, gs, :], bv, ACT.Copy))
                DV.wait(th, got(b - 2, "QM1"))
                s["Q1", g2] = ringW_free[i] = DV.op(lambda e: e.scalar_tensor_tensor(
                    Q1[:, r, gs, :], Qh[:, r, gs, :], m1n, bv, ALU.mult, ALU.add))
                return
            AC.wait(t, got(b - 2, "ST"))
            s["K1", g2] = th = AC.op(lambda e: e.activation(K1[:, r, gs, :], bv, ACT.Copy))
            DV.wait(th, ym_free[0])
            ty = DV.op(lambda e: e.tensor_scalar(Ym[:, :, :], K1[:, r, gs, :], m0, c17, ALU.mult, ALU.subtract))
            DV.wait(ty, got(b - 2, "ST"))
            s["K2", g2] = ym_free[0] = ringW_free[i] = DV.op(lambda e: e.scalar_tensor_tensor(
                K2[:, r, gs, :], bv, m0, Ym[:, :, :], ALU.mult, ALU.subtract))

        ym_free = [None]

        def A1v(b):
            r = b % 2
            s = a[b]
            i, bank = wbank()
            for tt in range(2):
                n = 0
                for dk in range(2):
                    for w, v in ((WQh, xTh), (WQl, xTh), (WQh, xTl)):
                        t = PE.op(lambda e, w=w, v=v, dk=dk, tt=tt, n=n: e.matmul(
                            bank[:, 256 * tt:256 * tt + 256], v[:, r, dk, 128 * tt:128 * tt + 128], w[:, dk, 1024:1280],
                            start=n == 0, stop=n == 5), n == 5 and tt == 1)
                        n += 1
            s["Vproj"] = t
            AC.wait(t, t_vz, got(b - 2, "PV"))
            s["V"] = ringW_free[i] = AC.op(lambda e: e.activation(
                Vv[:, r, :, :, 0:16], bank[:, :].rearrange("p (t n h) -> p t n h", t=2, h=16), ACT.Copy))

        qm1_free, qm2_free, q2_free, mp_free = [None, None], [None, None], [None, None], [None]

        def QM(b, P, j):
            r = b % 2
            h = P
            s = a[b]
            DV.wait(s["Q1", P], qm1_free[h] if j == 0 else None)
            s["QM1"] = s["QM1", P, j] = DV.op(lambda e: e.tensor_scalar(
                QM1[:, h, j, :], Q1[:, r, 2 * P:2 * P + 2, :].rearrange("p g c -> p (g c)"),
                CF[:, C_SL + j:C_SL + j + 1], None, ALU.mult))

        def QN2(b, P, j):
            s = a[b]
            h = P
            AC.wait(s["Q2"], qm2_free[j % 2])
            s["QM2", j % 2] = q2_free[h] = AC.op(lambda e: e.activation(
                QM2[:, j % 2, :], Q2[:, h, :], ACT.Copy, scale=CF[:, C_SL + j:C_SL + j + 1]))

        def A2(b, P, j):
            r = b % 2
            s = a[b]
            PE.wait(s["QM1", P, j], s["K1", P], t_cb)
            DV.wait(mp_free[0])
            for u in range(2):
                i, bank = wbank()
                w = 256 if u == 0 else 128
                q0 = 128 if u == 0 else 0
                tt = 1 - u
                bv = bank[:, 0:2 * w].rearrange("p (g c) -> p g c", g=2)
                PE.op(lambda e, bv=bv, w=w: e.matmul(
                    bv[:, :, w - 128:w], idb[:, :], mkb[:, :].rearrange("p (a c) -> p a c", a=1).broadcast_to([128, 2, 128]),
                    start=True, stop=False, skip_group_check=True), False)
                for gg in range(2):
                    t = PE.op(lambda e, gg=gg, w=w, q0=q0, bank=bank: e.matmul(
                        bank[:, w * gg:w * gg + w], QM1[:, P, j, 256 * gg + q0:256 * gg + q0 + 128], K1[:, r, 2 * P + gg, 0:w],
                        start=False, stop=gg == 1, skip_group_check=True), gg == 1)
                DV.wait(t)
                ringW_free[i] = s["mx"] = DV.op(lambda e, bv=bv, tt=tt: e.tensor_reduce(
                    mx[:, P, tt, :].rearrange("p (g c) -> p g c", c=4)[:, :, j], bv, AX.X, ALU.max))

        def A2e(b, P):
            s = a[b]
            DV.wait(s["mx"], t_mpz, mp_free[0])
            t = DV.op(lambda e: e.tensor_scalar(Mp[:, :, :, 16], mx[:, P, :, :], -1.0, None, ALU.mult))
            DV.wait(t)
            s["mp"] = DV.op(lambda e: e.scalar_tensor_tensor(
                Mp[:, :, :, 17], mx[:, P, :, :], -1.0, Mp[:, :, :, 16], ALU.mult, ALU.subtract))

        def A2t(b, P):
            r = b % 2
            s = a[b]
            i, bank = wbank()
            bb = bank[:, :].bitcast(BF)
            PE.wait(s["mp"])
            for g in range(2):
                for tt in range(2):
                    t = PE.op(lambda e, g=g, tt=tt: e.transpose(
                        bb[:, 256 * g + 128 * tt:256 * g + 128 * tt + 128],
                        Mp[:, tt, 4 * g:4 * g + 4, :].rearrange("p n c -> p (n c)"), idb[:, :]), g == 1 and tt == 1)
            mp_free[0] = t
            DV.wait(t, q2_free[P])
            ringW_free[i] = s["Q2"] = DV.op(lambda e: e.scalar_tensor_tensor(
                Q2[:, P, :], Qh[:, r, 2 * P:2 * P + 2, :].rearrange("p g c -> p (g c)"), m0, bb[:, 0:512], ALU.mult, ALU.add))

        pt_free = [None, None]
        otb = banks[4]
        ot_free = [None]

        def A3(b, P, j):
            r = b % 2
            s = a[b]
            PE.wait(s["QM2", j % 2], s["K2", P])
            for u in range(2):
                i, bank = wbank()
                w = 256 if u == 0 else 128
                q0, k0 = 256 - w, 128 * u
                for gg in range(2):
                    PE.op(lambda e, gg=gg, w=w, q0=q0, k0=k0, bank=bank: e.matmul(
                        bank[:, w * gg:w * gg + w], K1[:, r, 2 * P + gg, k0:k0 + 128], QM1[:, P, j, 256 * gg + q0:256 * gg + 256],
                        start=True, stop=False), False)
                    t = PE.op(lambda e, gg=gg, w=w, q0=q0, k0=k0, bank=bank: e.matmul(
                        bank[:, w * gg:w * gg + w], K2[:, r, 2 * P + gg, k0:k0 + 128],
                        QM2[:, j % 2, 256 * gg + q0:256 * gg + 256], start=False, stop=True), gg == 1)
                AC.wait(t, pt_free[P], t_wl)
                dst = PT[:, P, j, :, 0:256] if u == 0 else PT[:, P, j, :, 256:384]
                t1 = AC.op(lambda e, dst=dst, bank=bank, w=w: e.activation(
                    dst, bank[:, 0:2 * w].rearrange("p (j c) -> p j c", c=w), ACT.Exp, scale=0.25))
                ringW_free[i] = t1
                dg = dst[:, :, 0:128]
                PO.wait(t1)
                s["PT", P] = PO.op(lambda e, dg=dg: e.affine_select(
                    out=dg, in_=dg, pattern=[[0, 2], [1, 128]], compare_op=ALU.is_ge, fill=0.0, base=0, channel_multiplier=-1))
            qm2_free[j % 2] = t
            if j == 3:
                qm1_free[P] = s["ST"] = t

        def A3v(b, g):
            r = b % 2
            s = a[b]
            p, gg = g // 2, g % 2
            if gg == 0:
                PE.wait(ot_free[0])
            PE.wait(s["PT", p], s["V"])
            for kt in range(2):
                for j in range(4):
                    c = 17 * (4 * g + j)
                    t = PE.op(lambda e, kt=kt, j=j, c=c: e.matmul(
                        otb[32 * j:32 * j + 32, 256 * gg + 128 * kt:256 * gg + 256], Vp[:, r, kt, c:c + 32],
                        PT[:, p, j, gg, 0:256] if kt == 0 else PT[:, p, j, gg, 256:384], start=kt == 0, stop=kt == 1),
                        kt == 1 and j == 3)
            if gg == 1:
                pt_free[p] = t
                AC.wait(t, t_wsq, got(b - 1, "otT"))
                ot_free[0] = AC.op(lambda e: e.activation(
                    OTs[:, g - 1:g + 1, :], otb[:, :].rearrange("p (g c) -> p g c", g=2), ACT.Copy))
                s["OTs"] = ot_free[0]
            if g == 3:
                s["PV"] = t

        l_o = [lane("l_o0"), lane("l_o1")]
        l_m = [lane("l_m0"), lane("l_m1")]

        def A4(b, tt):
            s = a[b]
            for tt in (tt,):
                i, bank = wbank()
                PE.wait(s["OTs"])
                for g in range(4):
                    t = PE.op(lambda e, g=g, tt=tt, bank=bank: e.transpose(
                        bank[:, 128 * g:128 * g + 128], OTs[:, g, 128 * tt:128 * tt + 128], idf), g == 3)
                bv = bank[:, :].rearrange("p (n c) -> p n c", c=32)
                DV.wait(t, a[b - 1]["ost", tt] if b >= 1 else None)
                t2 = DV.op(lambda e, tt=tt, bv=bv: e.reciprocal(rc[:, tt, :], bv[:, :, 16]))
                DV.wait(t2, t_wsq)
                t2 = DV.op(lambda e, tt=tt: e.tensor_tensor(rc[:, tt, :], rc[:, tt, :], wsq[:, tt, :], ALU.mult))
                DV.wait(t2)
                t2 = DV.op(lambda e, tt=tt, bv=bv: e.tensor_tensor(
                    On[:, tt, :, :], bv[:, :, 0:16], rc[:, tt, :].rearrange("p (n a) -> p n a", a=1).broadcast_to([128, NH, 16]),
                    ALU.mult))
                ringW_free[i] = t2
            s["otT"] = t
            s["On"] = t2
            SP.wait(t2)
            for tt in (tt,):
                to = SP.dma(l_o[tt], lambda e, tt=tt: e.dma_start(
                    osc[b, :].rearrange("(n q h) -> q n h", n=NH, h=16)[128 * tt:128 * tt + 128, :, :], On[:, tt, :, :]))
                s["ost", tt] = to

        def A4b(b):
            s = a[b]
            r = b % 2
            SP.wait(s["ost", 0], s["ost", 1], a[b - 2]["mT"] if b >= 2 else None)
            s["M"] = SP.dma(l_m[r], lambda e: e.dma_start(Mm[:, r, :, :], osc[b, :].rearrange("(k p s) -> p k s", p=128, s=256)))

        def A5(b):
            s = a[b]
            r = b % 2
            i, bank = wbank()
            PE.wait(s["M"])
            for dk in range(2):
                for tt in range(2):
                    t = PE.op(lambda e, dk=dk, tt=tt: e.transpose(
                        bank[:, 256 * tt + 128 * dk:256 * tt + 128 * dk + 128], Mm[:, r, dk, 128 * tt:128 * tt + 128], idf),
                        dk == 1 and tt == 1)
            s["mT"] = t
            DV.wait(t)
            xx = XB[:, 2 * b:2 * b + 2, 0:256]
            s["x1"] = ringW_free[i] = DV.op(lambda e: e.tensor_tensor(
                xx, bank[:, :].rearrange("p (t c) -> p t c", t=2), xx, ALU.add))

        def A6s(b):
            a[b]["ls1"] = ln_stats(XB[:, 2 * b:2 * b + 2, 0:256], a[b]["x1"])

        def A6n(b):
            s = a[b]
            s["qn"] = ln_apply(s["ls1"], XB[:, 2 * b:2 * b + 2, 0:256], QN, got(b - 1, "qT"))

        l_cx = [lane("l_cx0")]
        l_sp = [lane("l_sp0"), lane("l_sp1")]

        def A6l(b):
            r = 0
            SP.wait(a[b - 1]["cT"] if b >= 1 else None)
            a[b]["cx"] = SP.dma(l_cx[r], lambda e: e.dma_start(Cn[:, r, :, :], ctx_in[b].rearrange("(t p) d -> p t d", p=128)))

        def A6c(b):
            s = a[b]
            v = SPL[:, 0, :].rearrange("p (s h k c) -> p s h k c", s=2, h=2, k=2)
            tp = transpose_pair([Cn[:, 0, 0, :], Cn[:, 0, 1, :]], [s["cx"]])
            s["cT"] = tp[2]
            s["tc"] = split_T(*tp, v[:, 1, 0, :, :], v[:, 1, 1, :, :], got(b - 1, "spl"), got(b - 1, "gate"))

        def A6q(b):
            s = a[b]
            v = SPL[:, 0, :].rearrange("p (s h k c) -> p s h k c", s=2, h=2, k=2)
            tp = transpose_pair([QN[:, 0, :], QN[:, 1, :]], [s["qn"]])
            s["qT"] = tp[2]
            s["tq"] = split_T(*tp, v[:, 0, 0, :, :], v[:, 0, 1, :, :], got(b - 1, "spl"), got(b - 1, "gate"))
            SP.wait(s["tc"], s["tq"])
            s["spl"] = SP.dma(l_sp[b % 2], lambda e: e.dma_start(qsc[b], SPL[:, 0, :]))

        def A6g(b):
            s = a[b]
            v = SPL[:, 0, :].rearrange("p (s h k c) -> p s h k c", s=2, h=2, k=2)
            PE.wait(s["tc"], s["tq"], t_wgs)
            for tt in range(2):
                n = 0
                c = 16 * (2 * b + tt)
                for sx in range(2):
                    for dk in range(2):
                        for hx, hw in ((0, 0), (0, 1), (1, 0)):
                            t = PE.op(lambda e, sx=sx, dk=dk, hx=hx, hw=hw, tt=tt, n=n, c=c: e.matmul(
                                gates[:, c:c + 16], v[:, sx, hx, dk, 128 * tt:128 * tt + 128],
                                WGs[:, dk, hw, 16 * sx:16 * sx + 16], start=n == 0, stop=n == 11), n == 11 and tt == 1)
                            n += 1
            s["gate"] = t

        QN = sb("QN", [128, 2, 256], F32, ca)
        zfill = sb("zfill", [128, ROW], F32, ca)
        t_z = PO.op(lambda e: e.memset(zfill[:, :], 0.0))
        l_z = lane("l_z")
        SP.wait(t_z)
        t_zf = None
        t_zf = SP.dma(l_z, lambda e: e.dma_start(
            xs[E * REG:XROWS, :].rearrange("(n p) c -> p n c", p=128),
            zfill[:, :].rearrange("p (a c) -> p a c", a=1).broadcast_to([128, (XROWS - E * REG) // 128, ROW])))
        t_zf = SP.dma(l_z, lambda e: e.dma_start(out[TOK:TOK + 128, :], zfill[:, 0:256]))

        wchunk = [0]

        def prep(dst, src, width, n):
            cs = []
            for _ in range(n):
                if wchunk[0] < 32:
                    cs.append(chunk(dst, src, width, wchunk[0]))
                    wchunk[0] += 1
            return cs

        def weights():
            nonlocal t_wl, t_wsq, t_gn, t_wgs
            AC.wait(t_w)
            t_wh = AC.op(lambda e: e.activation(WQh[:, :, :], WQf, ACT.Copy))
            DV.wait(t_wh, t_w)
            t_wl = DV.op(lambda e: e.tensor_tensor(WQl[:, :, :], WQf, WQh[:, :, :], ALU.subtract))
            DV.wait(t_wg)
            t = DV.op(lambda e: e.tensor_tensor(WGf[:, :, 16:32], WGf[:, :, 16:32], WGf[:, :, 32:48], ALU.add))
            DV.wait(t)
            DV.op(lambda e: e.tensor_copy(WGs[:, :, 0, 0:32], WGf[:, :, 0:32]))
            t = DV.op(lambda e: e.tensor_copy(WGs[:, :, 0, 32:40], WGf[:, :, 48:56]))
            DV.wait(t)
            DV.op(lambda e: e.tensor_tensor(WGs[:, :, 1, 0:32], WGf[:, :, 0:32], WGs[:, :, 0, 0:32], ALU.subtract))
            DV.op(lambda e: e.tensor_tensor(WGs[:, :, 1, 32:40], WGf[:, :, 48:56], WGs[:, :, 0, 32:40], ALU.subtract))
            t_gn = DV.op(lambda e: e.tensor_scalar(GN[:, :], GN[:, :], 1.0, None, ALU.add))
            t_wgs = t_gn
            PO.op(lambda e: e.memset(wtmp, 1.0))
            t_w1 = PO.now()
            PE.wait(t_w1, t_wo)
            PE.op(lambda e: e.matmul(banks[0][:, 0:256], OTs[:, 2, 0:128], OTs[:, 0, :], start=True, stop=False), False)
            t_ws = PE.op(lambda e: e.matmul(banks[0][:, 0:256], OTs[:, 2, 0:128], OTs[:, 1, :], start=False, stop=True))
            DV.wait(t_ws)
            for tt in range(2):
                selv = CF[:, C_SEL + 16 * tt:C_SEL + 16 * tt + 16].rearrange("p (a s) -> p a s", a=1).broadcast_to([128, 16, 16])
                t = DV.op(lambda e, selv=selv: e.tensor_tensor(
                    wtmp.rearrange("p (n s) -> p n s", s=16), banks[0][:, 0:256].rearrange("p (n s) -> p n s", s=16),
                    selv, ALU.mult))
                DV.wait(t)
                t = DV.op(lambda e, tt=tt: e.tensor_reduce(wsq[:, tt, :], wtmp.rearrange("p (n s) -> p n s", s=16), AX.X, ALU.add))
                DV.wait(t)
            ringW_free[2] = t
            t_wsq = t


        def ok(b):
            return 0 <= b < B

        for h in range(-4, 2 * B + 5):
            if h == -3:
                weights()
            i, P = h // 2, h % 2
            b3, P3 = (h - 1) // 2, (h - 1) % 2
            bv_ = (h - 2) // 2
            nb, nP = (h + 1) // 2, (h + 1) % 2
            pend = prep(WU, wup, 128, 1) if h >= 0 else []
            for j in range(4):
                if ok(i) and j < 3:
                    QM(i, P, j + 1)
                if ok(b3) and j < 3:
                    QN2(b3, P3, j + 1)
                if ok(i):
                    A2(i, P, j)
                if ok(b3):
                    A3(b3, P3, j)
                if j in (1, 2) and ok(bv_):
                    A3v(bv_, 2 * P + j - 1)
                if j == 0 and P == 0:
                    if ok(i + 2):
                        A0s(i + 2)
                    if ok(i - 3):
                        A6g(i - 3)
                if j == 1 and P == 1 and ok(i - 2):
                    A6s(i - 2)
                if j == 2:
                    for c in pend:
                        split(c)
                if j == 3:
                    if P == 0 and ok(i + 2):
                        A0n(i + 2)
                    if P == 1 and ok(i - 2):
                        A6n(i - 2)
            if ok(i):
                A2e(i, P)
            if P == 0:
                if ok(i + 1):
                    A1(i + 1, "k", 0)
                if ok(i):
                    A2t(i, P)
                if ok(i + 1):
                    A1(i + 1, "k", 1)
                if ok(i - 2):
                    A5(i - 2)
                if ok(nb):
                    QM(nb, nP, 0)
                if ok(i):
                    QN2(i, P, 0)
                if ok(i + 1):
                    A1(i + 1, "q", 0)
                if ok(i + 1):
                    A1(i + 1, "q", 1)
            else:
                if ok(i + 2):
                    A0(i + 2)
                if ok(i + 1):
                    A1v(i + 1)
                if ok(i):
                    A2t(i, P)
                if ok(nb):
                    QM(nb, nP, 0)
                if ok(i):
                    QN2(i, P, 0)
                if ok(i - 1):
                    A4(i - 1, 0)
                if ok(i - 1):
                    A4(i - 1, 1)
                if ok(i - 1):
                    A4b(i - 1)
                if ok(i - 2):
                    A6c(i - 2)
                if ok(i - 2):
                    A6q(i - 2)
                if ok(i - 1):
                    A6l(i - 1)

        def barrier():
            toks = [q.now() for q in (PE, DV, AC, PO)]
            for q in (PE, DV, AC, PO, SP):
                q.wait(*toks)

        barrier()
        for q in (DV, AC, PE, PO):
            q.wait(*[a[b]["spl"] for b in (B - 2, B - 1)], *[a[b]["ost", k] for b in (B - 1,) for k in (0, 1)], t_zf)
        ca.close()

        WD = sb("WD", [128, E * 4096], BF)
        cg = ExitStack()
        t = PO.op(lambda e: e.memset(WD[:, 24576:32768].bitcast(F32), 0.0))
        PO.wait(t)
        t_lr = PO.op(lambda e: e.memset(WD[0:6, 24576:32768], 1.0))
        G = sb("G", [128, NT, 16], F32, cg)
        gi = sb("gi", [128, 256], F32, cg)
        gf = sb("gf", [128, 256], F32, cg)
        zz = sb("zz", [128, 256], F32, cg)
        cs_ = sb("cs_", [128, 256], F32, cg)
        gg_ = sb("gg_", [128, 256], F32, cg)
        MM = sb("MM", [128, 256], F32, cg)
        r1 = sb("r1", [128, 2, 256], F32, cg)
        pp = sb("pp", [128, 6, 256], BF, cg)

        DV.op(lambda e: e.memset(zz[:, :], 0.0))
        t = DV.op(lambda e: e.tensor_tensor(
            G[:, :, :], gates[:, :].rearrange("p (t c) -> p t c", c=16),
            BG[:, 0:16].rearrange("p (a c) -> p a c", a=1).broadcast_to([128, NT, 16]), ALU.add))
        AC.wait(t)
        t = AC.op(lambda e: e.activation(G[:, :, :], G[:, :, :], ACT.Tanh, scale=1.0 / 15.0))
        PE.wait(t)
        Gv = G[:, :, :].rearrange("p (b t) (k h) -> p t k b h", t=2, h=8)
        GT = sb("GT", [128, 4, 128], F32, cg)
        DV.wait(t)
        for k in range(2):
            for tt in range(2):
                t = DV.op(lambda e, k=k, tt=tt: e.tensor_scalar(
                    GT[:, 2 * k + tt, :].rearrange("p (b h) -> p b h", h=8), Gv[:, tt, k, :, :], 15.0, None, ALU.mult))
        PE.wait(t)
        for k in range(4):
            t = PE.op(lambda e, k=k: e.transpose(banks[0][:, 128 * k:128 * k + 128], GT[:, k, :], idf), k == 3)
        DV.wait(t)
        t = DV.op(lambda e: e.tensor_copy(gi[:, :], banks[0][:, 0:256]))
        AC.wait(t)
        t = AC.op(lambda e: e.activation(gf[:, :], banks[0][:, 256:512], ACT.Exp, scale=-1.0))
        AC.wait(t)
        t = AC.op(lambda e: e.activation(gf[:, :], gf[:, :], ACT.Ln, bias=1.0))
        DV.wait(t)
        t = DV.op(lambda e: e.tensor_tensor_scan(cs_[:, :], gf[:, :], zz[:, :], 0.0, ALU.add, ALU.add))
        DV.wait(t)
        t = DV.op(lambda e: e.tensor_tensor(gg_[:, :], gi[:, :], cs_[:, :], ALU.add))
        DV.wait(t)
        t = DV.op(lambda e: e.tensor_tensor_scan(MM[:, :], gg_[:, :], gg_[:, :], NEG, ALU.max, ALU.max))
        DV.wait(t)
        t = DV.op(lambda e: e.tensor_tensor(cs_[:, :], cs_[:, :], MM[:, :], ALU.subtract))
        AC.wait(t)
        t_em = AC.op(lambda e: e.activation(cs_[:, :], cs_[:, :], ACT.Exp))
        PE.wait(t_em)
        for tt in range(2):
            t_em = PE.op(lambda e, tt=tt: e.transpose(banks[1][:, 128 * tt:128 * tt + 128], cs_[:, 128 * tt:128 * tt + 128], idf), tt == 1)
        DV.op(lambda e: e.tensor_scalar(MM[:, :], MM[:, :], -1.0, None, ALU.mult))
        DV.wait(DV.now())
        for k, src in enumerate((gg_, MM)):
            DV.op(lambda e, k=k, src=src: e.tensor_copy(pp[:, 3 * k, :], src[:, :]))
            DV.wait(DV.now())
            DV.op(lambda e, k=k, src=src: e.tensor_tensor(r1[:, 0, :], src[:, :], pp[:, 3 * k, :], ALU.subtract))
            DV.wait(DV.now())
            DV.op(lambda e, k=k: e.tensor_copy(pp[:, 3 * k + 1, :], r1[:, 0, :]))
            DV.wait(DV.now())
            DV.op(lambda e, k=k: e.tensor_tensor(r1[:, 1, :], r1[:, 0, :], pp[:, 3 * k + 1, :], ALU.subtract))
            DV.wait(DV.now())
            DV.op(lambda e, k=k: e.tensor_copy(pp[:, 3 * k + 2, :], r1[:, 1, :]))
            DV.wait(DV.now())
        t = DV.now()
        l_g = lane("l_g")
        SP.wait(t)
        t_g = SP.dma(l_g, lambda e: e.dma_start(gsc.rearrange("k p c -> p k c"), pp[:, :, :]))
        DV.wait(t_em)
        t_em = DV.op(lambda e: e.tensor_copy(EM[:, :, :], banks[1][:, 0:256].rearrange("p (t c) -> p t c", t=2)))
        barrier()
        for q in (PE, DV, AC, PO, SP):
            q.wait(t_g)
        cg.close()

        cb = ExitStack()
        QC = sb("QC", [128, 2, 1024], BF, cb)
        LH = WD[:, 24576:28672].rearrange("p (r h c) -> p r h c", r=2, h=8)
        RH = WD[:, 28672:32768].rearrange("p (r h c) -> p r h c", r=2, h=8)
        CX = sb("CX", [128, 2, 2, 256], F32, cb)
        SD = sb("SD", [128, 6, 512], F32, cb)
        dsel = CF[:, C_MASK:C_MASK + 64].rearrange("p (k c) -> p k c", k=2)
        OB = sb("OB", [128, 768], F32, cb)
        QB = sb("QB", [128, 4, 1024], BF, cb)
        sq = sb("sq", [128, 2, 256], F32, cb)
        sm = sb("sm", [128, 5, 2, 8], F32, cb)
        hh = sb("hh", [128, 2, 256], F32, cb)
        x3T = sb("x3T", [128, 2, 2, 256], BF, cb)

        t_qz = PO.op(lambda e: e.memset(QB[:, :, :].rearrange("p j c -> p (j c)").bitcast(F32), 0.0))
        PO.op(lambda e: e.memset(dsel[:, :, :], 0.0))
        PO.wait(PO.now())
        PO.op(lambda e: e.memset(dsel[:, 0, 0:1], 1.0))
        t_ds = PO.op(lambda e: e.memset(dsel[:, 1, 1:2], 1.0))

        l_qc = [lane(f"l_qc{k}") for k in range(2)]
        l_lh = [lane(f"l_lh{k}") for k in range(2)]
        l_rh = [lane(f"l_rh{k}") for k in range(2)]
        l_cb = [lane(f"l_cb{k}") for k in range(2)]
        bb_ = [dict() for _ in range(B)]

        def B1(b):
            r = b % 2
            s = bb_[b]
            p = bb_[b - 2] if b >= 2 else {}
            SP.wait(p.get("S"), p.get("PV"), t_g)
            s["qc"] = SP.dma(l_qc[r], lambda e: e.dma_start(QC[:, r, :], qsc[b, :, 1024:2048]))
            s["cx"] = SP.dma(l_cb[r], lambda e: e.dma_start(CX[:, r, :, :], ctx_in[b].rearrange("(t p) d -> p t d", p=128)))

        def B1g(b):
            s = bb_[b]
            r = b % 2
            SP.wait(bb_[b - 2]["D"] if b >= 2 else None, t_lr, t_g)
            s["lh"] = SP.dma(l_lh[r], lambda e: e.dma_start(LH[0:3, r, :, :], gsc[0:3, 8 * b:8 * b + 8, :]))
            s["rh"] = SP.dma(l_rh[r], lambda e: e.dma_start(RH[3:6, r, :, :], gsc[3:6, 8 * b:8 * b + 8, :]))

        sdb, sdb_free = [(banks[0], banks[1]), (banks[2], banks[3])], [None, None]
        sd_free = [None] * 6
        un = [0]
        ob, den, tb = banks[4], banks[5], banks[6]
        lgb = banks[7]
        ob_free, den_free, tb_free = [None], [None], [None]

        qb_free = [None] * 4
        l_qb = [lane(f"l_qb{k}") for k in range(4)]

        def BQ(b, j):
            s = bb_[b]
            SP.wait(t_qz, qb_free[j])
            s["QB", j] = SP.dma(l_qb[j], lambda e: e.dma_start(
                QB[32 * j:32 * j + 32, j, :], qsc[b, 32 * j:32 * j + 32, 0:1024]))

        def B2u(b, st, j):
            r = b % 2
            s = bb_[b]
            k2, k6 = un[0] % 2, un[0] % 6
            un[0] += 1
            sbk, dbk = sdb[k2]
            w = 256 if st == 0 else 128
            t0, s0 = 256 - w, 128 * st
            v = QC[:, r, :].rearrange("p (h k c) -> p h k c", h=2, k=2)
            q = QB[:, j, :].rearrange("p (h k c) -> p h k c", h=2, k=2)
            PE.wait(sdb_free[k2], s["lh"], s["rh"], s["qc"])
            for dk in range(2):
                t = PE.op(lambda e, dk=dk: e.matmul(
                    dbk[:, w * dk:w * dk + w], LH[:, r, 4 * dk + j, s0:s0 + 128], RH[:, r, 4 * dk + j, t0:256],
                    start=True, stop=True), dk == 1)
            s["D"] = t
            AC.wait(t, sd_free[k6])
            te = AC.op(lambda e: e.activation(SD[:, k6, 0:2 * w], dbk[:, 0:2 * w], ACT.Exp))
            PE.wait(s["QB", j])
            for dk in range(2):
                for n, (hc, hq) in enumerate(((0, 0), (0, 1), (1, 0))):
                    t = PE.op(lambda e, dk=dk, n=n, hc=hc, hq=hq: e.matmul(
                        sbk[:, w * dk:w * dk + w], v[:, hc, dk, s0:s0 + 128], q[:, hq, dk, t0:256],
                        start=n == 0, stop=n == 2), dk == 1 and n == 2)
            s["S"] = t
            if st == 1:
                qb_free[j] = t
            DV.wait(te, t)
            t1 = DV.op(lambda e: e.tensor_tensor(SD[:, k6, 0:2 * w], sbk[:, 0:2 * w], SD[:, k6, 0:2 * w], ALU.mult))
            sdb_free[k2] = t1
            PO.wait(t1)
            dg = SD[:, k6, 0:2 * w].rearrange("p (j c) -> p j c", c=w)[:, :, 0:128]
            s["SD", st, j] = (k6, PO.op(lambda e: e.affine_select(
                out=dg, in_=dg, pattern=[[0, 2], [1, 128]], compare_op=ALU.is_ge, fill=0.0, base=0, channel_multiplier=-1)))

        def B2v(b, st):
            r = b % 2
            s = bb_[b]
            if st == 0:
                PE.wait(ob_free[0], den_free[0], t_ds, s["cx"])
            w = 256 if st == 0 else 128
            o0 = 256 - w
            sl = [s["SD", st, j][0] for j in range(4)]
            PE.wait(*[s["SD", st, j][1] for j in range(4)])
            for dk in range(2):
                for j in range(4):
                    PE.op(lambda e, j=j, dk=dk: e.matmul(
                        ob[32 * j:32 * j + 32, 256 * dk + o0:256 * dk + 256], CX[:, r, st, 128 * dk + 32 * j:128 * dk + 32 * j + 32],
                        SD[:, sl[j], w * dk:w * dk + w], start=st == 0 and dk == 0, stop=st == 1 and dk == 1,
                        skip_group_check=True), False)
            for dk in range(2):
                for j in range(4):
                    t = PE.op(lambda e, j=j, dk=dk: e.matmul(
                        den[32 * j:32 * j + 32, o0:256], dsel[:, dk, :], SD[:, sl[j], w * dk:w * dk + w],
                        start=dk == 0 and st == 0, stop=dk == 1 and st == 1,
                        skip_group_check=True), dk == 1 and j == 3)
            for j in range(4):
                sd_free[sl[j]] = t
            s["PV"] = t

        l_x2 = [lane(f"l_x2{k}") for k in range(2)]
        ISQ = float(1.0 / (32.0 ** 0.5))

        def B3(b):
            s = bb_[b]
            r = b % 2
            prev = bb_[b - 1] if b >= 1 else {}
            AC.wait(s["PV"], prev.get("obT"))
            ob_free[0] = AC.op(lambda e: e.activation(OB[:, 0:512], ob[:, :], ACT.Copy))
            den_free[0] = t = AC.op(lambda e: e.activation(OB[:, 512:768], den[:, 0:256], ACT.Copy))
            s["ob"] = t

        ISQ32 = float(1.0 / 32.0)
        hh_free = [None]

        def B4(b):
            s = bb_[b]
            r = b % 2
            PE.wait(s["ob"], tb_free[0])
            for tt in range(2):
                for k in range(2):
                    PE.op(lambda e, k=k, tt=tt: e.transpose(
                        tb[:, 256 * tt + 128 * k:256 * tt + 128 * k + 128], OB[:, 256 * k + 128 * tt:256 * k + 128 * tt + 128], idf), False)
            PE.wait(sm_free[0])
            for tt in range(2):
                t = PE.op(lambda e, tt=tt: e.transpose(
                    lgb[:, 256 + 128 * tt:384 + 128 * tt], OB[:, 512 + 128 * tt:640 + 128 * tt], idf), tt == 1)
            s["obT"] = t
            AC.wait(t, hh_free[0])
            t_s = AC.op(lambda e: e.activation(sq[:, :, :], tb[:, :].rearrange("p (t c) -> p t c", t=2), ACT.Square, scale=ISQ32))
            t_h = AC.op(lambda e: e.activation(hh[:, :, :], tb[:, :].rearrange("p (t c) -> p t c", t=2), ACT.Copy, scale=ISQ))
            tb_free[0] = t_h
            em = EM[:, :, 8 * b:8 * b + 8].rearrange("p t (k j) -> p t k j", k=2)
            v4 = [sm[:, k, :, :].rearrange("p t (k j) -> p t k j", k=2) for k in range(5)]

            def dsum(tt):
                return lgb[:, 256 + 128 * tt:384 + 128 * tt].rearrange("p (j c) -> p c j", c=32)[:, 0:2, :]

            DV.wait(t, hh_free[0])
            for tt in range(2):
                t = DV.op(lambda e, tt=tt: e.tensor_scalar(v4[4][:, tt], dsum(tt), ISQ, None, ALU.mult))
            DV.wait(t, t_em)
            for tt in range(2):
                t = DV.op(lambda e, tt=tt: e.scalar_tensor_tensor(v4[0][:, tt], dsum(tt), -ISQ, v4[4][:, tt], ALU.mult, ALU.max))
            sm_free[0] = t
            DV.wait(t)
            t = DV.op(lambda e: e.tensor_tensor(sm[:, 1, :, :], sm[:, 0, :, :], EM[:, :, 8 * b:8 * b + 8], ALU.max))
            DV.wait(t)
            t = DV.op(lambda e: e.tensor_scalar(sm[:, 0, :, :], sm[:, 1, :, :], 5e-5, None, ALU.add))
            DV.wait(t)
            DV.op(lambda e: e.tensor_tensor(sm[:, 1, :, :], sm[:, 0, :, :], sm[:, 0, :, :], ALU.mult))
            s["sq"], s["hh"] = t_s, t_h

        def B4r(b):
            s = bb_[b]
            DV.wait(s["sq"])
            t = DV.op(lambda e: e.tensor_reduce(sm[:, 2, :, :], sq[:, :, :].rearrange("p t (h c) -> p t h c", c=32), AX.X, ALU.add))
            DV.wait(t)
            t = DV.op(lambda e: e.scalar_tensor_tensor(sm[:, 3, :, :], sm[:, 1, :, :], 1e-6, sm[:, 2, :, :], ALU.mult, ALU.add))
            s["ms"] = t

        def B4p(b):
            s = bb_[b]
            PO.wait(s["ms"])
            s["rs"] = PO.op(lambda e: e.tensor_tensor(
                sm[:, 4, :, :], sm[:, 3, :, :], mhalf[:, :].rearrange("p (a c) -> p a c", a=1).broadcast_to([128, 2, 8]), ALU.pow))

        def B4x(b):
            s = bb_[b]
            r = b % 2
            DV.wait(s["rs"], s["hh"])
            hv = hh[:, :, :].rearrange("p t (h c) -> p (t h) c", c=32)
            t = DV.op(lambda e: e.tensor_tensor(
                hv, hv, sm[:, 4, :, :].rearrange("p t (h a) -> p (t h) a", a=1).broadcast_to([128, 16, 32]), ALU.mult))
            s["hx"] = t

        def B4y(b):
            s = bb_[b]
            DV.wait(s["hx"], t_gn)
            s["hy"] = DV.op(lambda e: e.tensor_tensor(
                hh[:, :, :], hh[:, :, :], GN[:, :].rearrange("p (a c) -> p a c", a=1).broadcast_to([128, 2, 256]), ALU.mult))

        def B4z(b):
            s = bb_[b]
            DV.wait(s["hy"])
            xx = XB[:, 2 * b:2 * b + 2, 0:256]
            hh_free[0] = s["x2"] = t = DV.op(lambda e: e.tensor_tensor(xx, xx, hh[:, :, :], ALU.add))

        def B4o(b):
            s = bb_[b]
            r = b % 2
            SP.wait(s["x2"])
            ov = out[0:TOK, :].rearrange("(t p) d -> p t d", p=128)
            s["x2o"] = SP.dma(l_x2[r], lambda e: e.dma_start(ov[:, 2 * b:2 * b + 2, :], XB[:, 2 * b:2 * b + 2, 0:256]))

        sm_free = [None]

        def B5s(b):
            bb_[b]["ls"] = ln_stats(XB[:, 2 * b:2 * b + 2, 0:256], bb_[b]["x2"])

        def B5n(b):
            xx = XB[:, 2 * b:2 * b + 2, 0:256]
            bb_[b]["x3"] = ln_apply(bb_[b]["ls"], xx, xx, bb_[b]["x2o"])

        def B5(b):
            s = bb_[b]
            PE.wait(s["x3"], tb_free[0])
            for tt in range(2):
                for dk in range(2):
                    t = PE.op(lambda e, tt=tt, dk=dk: e.transpose(
                        tb[:, 256 * dk + 128 * tt:256 * dk + 128 * tt + 128], XB[:, 2 * b + tt, 128 * dk:128 * dk + 128], idf),
                        tt == 1 and dk == 1)
            bv = tb[:, :].rearrange("p (k c) -> p k c", k=2)
            AC.wait(t, bb_[b - 1]["lg"] if b >= 1 else None)
            th = AC.op(lambda e: e.activation(x3T[:, 0, :, :], bv, ACT.Copy))
            DV.wait(th)
            tl = DV.op(lambda e: e.tensor_tensor(x3T[:, 1, :, :], bv, x3T[:, 0, :, :], ALU.subtract))
            tb_free[0] = tl
            s["x3T"] = tl

        def B6(b):
            s = bb_[b]
            PE.wait(s["x3T"], sm_free[0])
            for tt in range(2):
                n = 0
                c = 8 * (2 * b + tt)
                for dk in range(2):
                    for hx, hw in ((0, 0), (0, 1), (1, 0)):
                        t = PE.op(lambda e, dk=dk, hx=hx, hw=hw, tt=tt, n=n, c=c: e.matmul(
                            lgb[:, c:c + 8], x3T[:, hx, dk, 128 * tt:128 * tt + 128], WGs[:, dk, hw, 32:40],
                            start=n == 0, stop=n == 5), n == 5 and tt == 1)
                        n += 1
            s["lg"] = t

        RV = CF[:, C_MASK + 64:C_MASK + 64 + 224].rearrange("p (k t c) -> p k t c", k=7, c=8)
        LG, PR, EQ, KY, O1, O2, TOT = (RV[:, k] for k in range(7))
        WV = WGf[:, :, :].rearrange("p a c -> p (a c)")
        CUM = WV[:, 0:32]
        MX, SM, KM, W2, S1, S2 = (WV[:, 32 + 4 * k:36 + 4 * k] for k in range(6))
        CNT, E0, ADJ = (WV[:, 56 + 8 * k:64 + 8 * k] for k in range(3))
        MB = WV[:, 80:96].bitcast(BF)
        SLI = WV[:, 96:112].bitcast(I32).rearrange("p (r k t) -> p r k t", r=2, k=2)
        ek = CF[:, C_EK:C_EK + 8].rearrange("p (a c) -> p a c", a=1).broadcast_to([128, 4, E])

        def dv(fn):
            t = DV.op(fn)
            DV.wait(t)
            return t

        dv(lambda e: e.tensor_copy(CNT, CF[:, C_RB:C_RB + 8]))

        def bt(x):
            return x.rearrange("p (t a) -> p t a", a=1).broadcast_to([128, 4, E])

        rt = [dict() for _ in range(B // 2)]

        def R1(b):
            if b % 2 == 0:
                return
            s = rt[b // 2]
            c = 16 * (b - 1)
            DV.wait(bb_[b]["lg"])
            sm_free[0] = dv(lambda e: e.tensor_tensor(
                LG, lgb[:, c:c + 32].rearrange("p (t c) -> p t c", c=8),
                BG[:, 16:24].rearrange("p (a c) -> p a c", a=1).broadcast_to([128, 4, E]), ALU.add))
            dv(lambda e: e.tensor_reduce(MX, LG, AX.X, ALU.max))
            t = dv(lambda e: e.tensor_tensor(LG, LG, bt(MX), ALU.subtract))
            AC.wait(t)
            s["ex"] = AC.op(lambda e: e.activation(PR, LG, ACT.Exp))

        def pick(src, wt, oh):
            dv(lambda e: e.tensor_reduce(wt, src, AX.X, ALU.max))
            dv(lambda e: e.tensor_tensor(EQ, src, bt(wt), ALU.is_equal))
            dv(lambda e: e.tensor_tensor(KY, EQ, ek, ALU.mult))
            dv(lambda e: e.tensor_reduce(KM, KY, AX.X, ALU.max))
            dv(lambda e: e.tensor_tensor(oh, KY, bt(KM), ALU.is_equal))

        def R2(b):
            if b % 2 == 0:
                return
            t0 = 2 * b - 2
            DV.wait(rt[b // 2]["ex"])
            dv(lambda e: e.tensor_reduce(SM, PR, AX.X, ALU.add))
            dv(lambda e: e.reciprocal(SM, SM))
            dv(lambda e: e.tensor_tensor(PR, PR, bt(SM), ALU.mult))
            pick(PR, MX, O1)
            dv(lambda e: e.tensor_scalar(XB[:, t0:t0 + 4, 259], KM, -1.0, 8.0, ALU.mult, ALU.add))

        def R3(b):
            if b % 2 == 0:
                return
            s = rt[b // 2]
            t0 = 2 * b - 2
            dv(lambda e: e.scalar_tensor_tensor(LG, O1, -2.0, PR, ALU.mult, ALU.add))
            pick(LG, W2, O2)
            DV.op(lambda e: e.tensor_copy(XB[:, t0:t0 + 4, 257], W2))
            DV.op(lambda e: e.tensor_tensor(XB[:, t0:t0 + 4, 258], MX, W2, ALU.subtract))
            DV.op(lambda e: e.tensor_copy(XB[:, t0:t0 + 4, 256], CF[:, C_TOK + t0:C_TOK + t0 + 4]))
            DV.wait(rt[b // 2 - 1]["mm"] if b > 1 else None)
            s["mb"] = dv(lambda e: e.tensor_tensor(MB.rearrange("p (c t) -> p t c", t=4), O1, O2, ALU.add))

        def R4(b):
            if b % 2 == 0:
                return
            s = rt[b // 2]
            PE.wait(s["mb"], t_cb, t_ones, sm_free[0])
            PE.op(lambda e: e.matmul(lgb[:, 256:288], Ub[:, :], MB, start=True, stop=True), False)
            s["mm"] = PE.op(lambda e: e.matmul(lgb[:, 288:320], onesb[:, :], MB, start=True, stop=True))

        def R5(b):
            if b % 2 == 0:
                return
            s = rt[b // 2]
            ring = (b // 2) % 2
            tot = TOT.rearrange("p t c -> p (t c)")
            ev = tot.rearrange("p (c t) -> p c t", t=4)
            DV.wait(s["mm"])
            dv(lambda e: e.tensor_copy(tot, lgb[:, 288:320]))
            dv(lambda e: e.tensor_tensor_scan(CUM, tot, tot, 0.0, ALU.add, ALU.max))
            dv(lambda e: e.tensor_tensor(tot, CUM, tot, ALU.subtract))
            dv(lambda e: e.tensor_copy(E0, ev[:, :, 0]))
            dv(lambda e: e.tensor_tensor(ADJ, CNT, E0, ALU.subtract))
            dv(lambda e: e.tensor_tensor(CNT, ADJ, CUM.rearrange("p (c t) -> p c t", t=4)[:, :, 3], ALU.add))
            dv(lambda e: e.tensor_tensor(ev, ev, ADJ.rearrange("p (c a) -> p c a", a=1).broadcast_to([128, E, 4]), ALU.add))
            sm_free[0] = dv(lambda e: e.tensor_tensor(tot, lgb[:, 256:288], tot, ALU.add))

        def R6(b):
            if b % 2 == 0:
                return
            s = rt[b // 2]
            t0 = 2 * b - 2
            ring = (b // 2) % 2
            et = TOT.rearrange("p t c -> p (t c)").rearrange("p (c t) -> p t c", t=4)
            DV.wait(*(rt[b // 2 - 2]["sc"] if b > 3 else ()))
            for k, (o, sx) in enumerate(((O1, S1), (O2, S2))):
                dv(lambda e, o=o: e.tensor_tensor(o, o, et, ALU.mult))
                dv(lambda e, o=o, sx=sx: e.tensor_reduce(sx, o, AX.X, ALU.add))
                t = dv(lambda e, sx=sx, k=k: e.tensor_copy(SLI[:, ring, k, :], sx))
            s["sc"] = []
            for tt in range(4):
                for k in range(2):
                    todo_sc.append((s, t, t0 + tt, SLI[:, ring, k, tt:tt + 1]))

        NS = 4
        l_sc = [lane(f"l_sc{k}") for k in range(NS)]
        t_sc = [None] * NS
        todo_sc, n_sc = [], [0]

        def scatter():
            s, t, tl, sl = todo_sc.pop(0)
            k = n_sc[0] % NS
            n_sc[0] += 1
            PO.wait(t, t_sc[k])
            t_sc[k] = PO.dma(l_sc[k], lambda e: e.indirect_dma_start(
                out=xs, out_offset=bass.IndirectOffsetOnAxis(ap=sl, axis=0),
                in_=XB[:, tl, :], in_offset=None, bounds_check=XROWS - 1, oob_is_err=True))
            s["sc"].append(t_sc[k])

        wchunk[0] = 0
        pend = []
        B1(0)
        B1g(0)
        B1(1)
        B1g(1)
        todo = []
        for j in range(4):
            BQ(0, j)
        STEPS = ((0, 2, B4z), (0, 3, B5), (1, 2, B4o), (1, 3, B6), (2, 1, B4), (3, 1, B4r), (4, 1, B4p), (4, 2, B5s), (6, 2, B5n),
                 (6, 1, B4x), (7, 1, B4y),
                 (1, 3, R1), (3, 3, R2), (5, 3, R3), (6, 3, R4), (7, 3, R5), (0, 4, R6))
        for i in range(B + 4):
            pend = prep(WD, wdn, 256, 2) if i < B and wchunk[0] < 24 else prep(WD, wdn, 256, 2) if i >= B else []
            for n in range(8):
                if i < B:
                    B2u(i, n // 4, n % 4)
                if n >= 4 and i + 1 < B:
                    BQ(i + 1, n - 4)
                if n in (1, 5) and todo:
                    B2v(*todo[0])
                    if todo[0][1] == 1:
                        B3(todo[0][0])
                    todo.pop(0)
                if n == 3 and i < B:
                    todo.append((i, 0))
                if n == 7 and i < B:
                    todo.append((i, 1))
                if n in (1, 5) and pend:
                    splitb(pend.pop(0))
                if n == 1 and 1 <= i < B - 1:
                    B1(i + 1)
                    B1g(i + 1)
                if todo_sc and (n % 2 == 1 or i >= B):
                    scatter()
                for at, lag, fn in STEPS:
                    if n == at and 0 <= i - lag < B:
                        fn(i - lag)

        while todo_sc:
            scatter()
        for q in (DV, AC, PE, SP):
            q.wait(PO.now(), PE.now(), AC.now(), DV.now())
        cb.close()

        cr = ExitStack()
        TE = sb("TE", [128, NTILE], F32)
        TEi = sb("TEi", [128, NTILE], I32)
        RBi = sb("RBi", [128, NTILE], I32)
        RB = sb("RB", [128, NTILE], F32, cr)
        t8 = sb("t8", [128, 8, E], F32, cr)
        t8i = sb("t8i", [128, E], I32, cr)
        cni = sb("cni", [128, E], I32, cr)
        te8 = sb("te8", [128, NTILE, E], F32, cr)
        t_ci = dv(lambda e: e.tensor_copy(cni[:, :], CNT))
        l_ze = [lane("l_ze0"), lane("l_ze1")]
        zr, t_ze = {}, [None, None]
        for q in (SP, AC):
            q.wait(t_ci, t_zf)
        for c in range(E):
            q = (SP, AC)[c % 2]
            q.raw(lambda e, c=c: zr.__setitem__(c, e.value_load(cni[0:1, c:c + 1], min_val=REG * c, max_val=REG * c + TOK)))
            t_ze[c % 2] = q.dma(l_ze[c % 2], lambda e, c=c: e.dma_start(xs[bass.ds(zr[c], 128), :], xs[E * REG:E * REG + 128, :]))
        dv(lambda e: e.tensor_tensor(t8[:, 1, :], CNT, CF[:, C_RB:C_RB + 8], ALU.subtract))
        dv(lambda e: e.tensor_scalar(t8i[:, :], t8[:, 1, :], 63.5, 1.0 / 128.0, ALU.add, ALU.mult))
        dv(lambda e: e.tensor_copy(t8[:, 2, :], t8i[:, :]))
        dv(lambda e: e.tensor_tensor_scan(t8[:, 4, :], t8[:, 2, :], t8[:, 2, :], 0.0, ALU.add, ALU.max))
        dv(lambda e: e.tensor_scalar(t8[:, 3, :], t8[:, 2, :], -128.0, float(REG), ALU.mult, ALU.add))
        dv(lambda e: e.tensor_tensor(
            te8[:, :, :], t8[:, 4, :].rearrange("p (a c) -> p a c", a=1).broadcast_to([128, NTILE, E]),
            CF[:, C_J:C_J + NTILE].rearrange("p (j a) -> p j a", a=1).broadcast_to([128, NTILE, E]), ALU.is_le))
        dv(lambda e: e.tensor_reduce(TE[:, :], te8[:, :, :], AX.X, ALU.add))
        dv(lambda e: e.tensor_scalar(TE[:, :], TE[:, :], 7.0, None, ALU.min))
        t_te = dv(lambda e: e.tensor_copy(TEi[:, :], TE[:, :]))
        dv(lambda e: e.tensor_tensor(
            te8[:, :, :], te8[:, :, :], t8[:, 3, :].rearrange("p (a c) -> p a c", a=1).broadcast_to([128, NTILE, E]), ALU.mult))
        dv(lambda e: e.tensor_reduce(RB[:, :], te8[:, :, :], AX.X, ALU.add))
        dv(lambda e: e.scalar_tensor_tensor(RB[:, :], CF[:, C_J:C_J + NTILE], 128.0, RB[:, :], ALU.mult, ALU.add))
        t_rb = dv(lambda e: e.tensor_copy(RBi[:, :], RB[:, :]))
        for q in (PE, DV, AC, SP, PO):
            q.wait(t_rb, *t_sc)
        SP.wait(*t_ze)
        cr.close()

        NX = 3
        XS = sb("XS", [128, NX, ROW], F32)
        XTs = sb("XTs", [128, 2, 2, 2, 128], BF)
        Hf = sb("Hf", [128, 2, 1024], F32)
        Hh = sb("Hh", [128, 2, 1024], BF)
        Hl = sb("Hl", [128, 2, 1024], BF)
        Yf = sb("Yf", [128, 2, 256], F32)
        yt = sb("yt", [128, 2, 256], F32)
        ix = sb("ix", [128, 3, 5], F32)
        ixi = sb("ixi", [128, 3, 1], I32)
        l_xs = [lane(f"l_xs{k}") for k in range(NX)]
        l_y = [lane(f"l_y{k}") for k in range(2)]
        f = [dict() for _ in range(NTILE)]
        xtb = [banks[0], banks[1]]
        upb = [(banks[2], banks[3]), (banks[4], banks[5])]
        yb = [banks[6], banks[7]]

        def F0(j):
            SP.wait(*(f[j - NX][k] for k in ("T", "w")) if j >= NX else ())
            reg = {}
            SP.raw(lambda e: reg.__setitem__("r", e.value_load(RBi[0:1, j:j + 1], min_val=0, max_val=XROWS - 128)))
            f[j]["x"] = SP.dma(l_xs[j % NX], lambda e: e.dma_start(XS[:, j % NX, :], xs[bass.ds(reg["r"], 128), :]))

        def F1(j):
            s = f[j]
            r, rx = j % 2, j % NX
            p = f[j - 2] if j >= 2 else {}
            PE.wait(s["x"], p.get("xl"))
            for dk in range(2):
                t = PE.op(lambda e, dk=dk: e.transpose(xtb[r][:, 128 * dk:128 * dk + 128], XS[:, rx, 128 * dk:128 * dk + 128], idf), dk == 1)
            s["T"] = t
            bv = xtb[r][:, 0:256].rearrange("p (k c) -> p k c", k=2)
            AC.wait(t, p.get("up"))
            th = AC.op(lambda e: e.activation(XTs[:, r, 0, :, :], bv, ACT.Copy))
            DV.wait(th)
            s["xl"] = DV.op(lambda e: e.tensor_tensor(XTs[:, r, 1, :, :], bv, XTs[:, r, 0, :, :], ALU.subtract))
            q = j % 3
            old = f[j - 3] if j >= 3 else {"y": None, "y1": None, "sc": None}
            PO.wait(s["x"], old["y"], old["y1"], old["sc"])
            v = XS[:, rx, 256:257]
            PO.op(lambda e: e.tensor_scalar(ix[:, q, 0:1], v, 0.0, CF[:, C_DUMP:C_DUMP + 1], ALU.is_equal, ALU.mult))
            t = PO.op(lambda e: e.tensor_scalar(ix[:, q, 2:3], XS[:, rx, 259:260], TE[:, j:j + 1], XS[:, rx, 258:259], ALU.is_equal, ALU.mult))
            PO.op(lambda e: e.tensor_scalar(ix[:, q, 1:2], v, -1.0, None, ALU.add))
            PO.wait(PO.now())
            PO.op(lambda e: e.tensor_tensor(ix[:, q, 4:5], ix[:, q, 0:1], ix[:, q, 1:2], ALU.add))
            PO.wait(PO.now())
            PO.op(lambda e: e.tensor_copy(ixi[:, q, 0:1], ix[:, q, 4:5]))
            s["w"] = PO.op(lambda e: e.tensor_tensor(ix[:, q, 3:4], ix[:, q, 2:3], XS[:, rx, 257:258], ALU.add))

        def F2(j, fm):
            s = f[j]
            r = j % 2
            p = f[j - 2] if j >= 2 else {}
            if fm == 0:
                PE.wait(s["xl"], t_te)
                reg = s["reg"] = {}
                PE.raw(lambda e: reg.__setitem__("e", e.value_load(TEi[0:1, j:j + 1], min_val=0, max_val=7)))
            reg = s["reg"]
            k = fm // 4
            bank = upb[r][k]
            if fm % 4 == 0:
                PE.wait(p.get(("h", k)))
            n = 0
            for dk in range(2):
                for hw, hx in ((0, 0), (0, 1), (1, 0)):
                    off = 512 * fm + 256 * dk + 128 * hw
                    t = PE.op(lambda e, off=off, hx=hx, dk=dk, n=n: e.matmul(
                        bank[:, 128 * (fm % 4):128 * (fm % 4) + 128], WU[:, bass.ds(reg["e"] * 4096 + off, 128)],
                        XTs[:, r, hx, dk, :], start=n == 0, stop=n == 5), n == 5 and fm % 4 == 3)
                    n += 1
            if fm % 4 == 3:
                hs = slice(512 * k, 512 * k + 512)
                AC.wait(t, p.get(("hl", k)))
                s["h", k] = th = AC.op(lambda e: e.activation(Hf[:, r, hs], bank[:, :], ACT.Gelu))
                DV.wait(th, p.get("dn"))
                t2 = DV.op(lambda e: e.tensor_copy(Hh[:, r, hs], Hf[:, r, hs]))
                DV.wait(t2)
                s["hl", k] = DV.op(lambda e: e.tensor_tensor(Hl[:, r, hs], Hf[:, r, hs], Hh[:, r, hs], ALU.subtract))
                s["up"] = t

        def F3(j, fk):
            s = f[j]
            r, q = j % 2, j % 3
            p = f[j - 2] if j >= 2 else {}
            PE.wait(s["hl", fk // 4], *((p.get("y"), p.get("y1")) if fk == 0 else ()))
            reg = s["reg"]
            hsl = slice(128 * fk, 128 * fk + 128)
            PE.op(lambda e: e.matmul(
                yb[r][:, 0:512], Hh[:, r, hsl], WD[:, bass.ds(reg["e"] * 4096 + 512 * fk, 512)], start=fk == 0, stop=False,
                skip_group_check=True), False)
            t = PE.op(lambda e: e.matmul(
                yb[r][:, 0:256], Hl[:, r, hsl], WD[:, bass.ds(reg["e"] * 4096 + 512 * fk, 256)], start=False, stop=fk == 7,
                skip_group_check=True), fk == 7)
            if fk < 7:
                return
            s["dn"] = t
            AC.wait(t, s["w"], p.get("y"))
            t1 = AC.op(lambda e: e.activation(yt[:, r, :], yb[r][:, 256:512], ACT.Copy, scale=ix[:, q, 3:4]))
            s["y1"] = t1
            DV.wait(t1, s["w"], p.get("sc"))
            s["y"] = t2 = DV.op(lambda e: e.scalar_tensor_tensor(
                Yf[:, r, :], yb[r][:, 0:256], ix[:, q, 3:4], yt[:, r, :], ALU.mult, ALU.add))
            PO.wait(t2, s["w"], f[j - 1]["sc"] if j else None)
            s["sc"] = PO.dma(l_y[r], lambda e: e.indirect_dma_start(
                out=out, out_offset=bass.IndirectOffsetOnAxis(ap=ixi[:, q, 0:1], axis=0), in_=Yf[:, r, :], in_offset=None,
                bounds_check=TOK + 127, oob_is_err=True, compute_op=ALU.add))

        F0(0)
        F0(1)
        F1(0)
        for g in range(8 * NTILE + LAG):
            j, k = divmod(g, 8)
            if j < NTILE:
                F2(j, k)
            if g >= LAG:
                F3(*divmod(g - LAG, 8))
            if k == 0 and j + 2 < NTILE:
                F0(j + 2)
            if k == KF1 and j + 1 < NTILE:
                F1(j + 1)
        SP.wait(f[NTILE - 1]["sc"], f[NTILE - 2]["sc"], t_zf)
        PO.wait(f[NTILE - 1]["sc"], f[NTILE - 2]["sc"])

        with nc.Block() as block:
            @block.sync
            def _(e):
                SP.run(e)

            @block.gpsimd
            def _(e):
                PO.run(e)

            @block.scalar
            def _(e):
                AC.run(e)

            @block.vector
            def _(e):
                DV.run(e)

            @block.tensor
            def _(e):
                PE.run(e)


_INS = ["x", "ctx", "wqkv", "wout", "wg", "bg", "gain", "wr", "br", "wup", "wdn", "cst"]


def constants():
    import numpy as np
    c = np.zeros((128, C_END), np.float32)
    p = np.arange(128)
    c[:, C_ID:C_ID + 128] = np.eye(128)
    c[:, C_MASK:C_MASK + 128] = np.where(p[None, :] > p[:, None], NEG, 0.0)
    c[:, C_U:C_U + 128] = p[:, None] < p[None, :]
    for tt in range(2):
        for s in range(16):
            c[:, C_SEL + 16 * tt + s] = s == 8 * tt + p // 16
    c[:, C_M0] = p % 32 < 16
    c[:, C_M1] = -1.0 * (p % 32 >= 16)
    c[:, C_C17] = (p % 32 == 16) | (p % 32 == 17)
    c[:, C_TOK:C_TOK + 32] = 128 * np.arange(32)[None, :] + p[:, None] + 1
    c[:, C_EK:C_EK + 8] = 8 - np.arange(8)
    c[:, C_J:C_J + NTILE] = np.arange(NTILE)
    c[:, C_DUMP] = TOK + p + 1
    c[:, C_RB:C_RB + 8] = REG * np.arange(8)
    for j in range(4):
        c[:, C_SL + j] = p // 32 == j
    return c


def layout(inputs):
    import numpy as np
    i = {k: np.asarray(v) for k, v in inputs.items()}
    w = i["L0_attn_W_qkv"].reshape(4, 4, D, 3, 16)
    q = w[:, :, :, 0, :].transpose(2, 0, 1, 3)
    k = w[:, :, :, 1, :].transpose(2, 0, 1, 3)
    v = w[:, :, :, 2, :].transpose(2, 0, 1, 3).reshape(D, 256)
    q2 = np.concatenate([q, q], axis=3).reshape(D, 512)
    k2 = np.concatenate([k, k], axis=3).reshape(D, 512)
    wq = np.concatenate([q2, k2, v], axis=1).reshape(2, 128, 1280).transpose(1, 0, 2)
    ig = i["L0_xattn_ifgate_w"].reshape(16, 3, 2, 128)
    wg = ig.transpose(3, 2, 1, 0).reshape(128, 2, 48)
    wr = i["L0_ffn_router_w"].reshape(2, 128, 8).transpose(1, 0, 2)
    wup = i["L0_ffn_expert_up"].reshape(8, 8, 128, 2, 128).transpose(4, 0, 1, 3, 2).reshape(128, 16384)
    wdn = i["L0_ffn_expert_down"].reshape(8, 256, 8, 128).transpose(3, 0, 2, 1).reshape(128, 16384)
    arrays = {"x": i["x"], "ctx": i["ctx_1024"], "wqkv": wq, "wout": i["L0_attn_W_out"].reshape(256, 256), "wg": wg,
              "bg": i["L0_xattn_ifgate_b"], "gain": i["L0_xattn_outnorm_w"], "wr": wr, "br": i["L0_ffn_router_b"],
              "wup": wup, "wdn": wdn, "cst": constants()}
    return {n: np.ascontiguousarray(a) for n, a in arrays.items()}


def kernel(**inputs):
    import concourse.bacc as _bacc
    from concourse import mybir as _mybir
    from concourse.bass_utils import run_bass_kernel_spmd as _run

    arrays = layout(inputs)
    nc = _bacc.Bacc("TRN2", target_bir_lowering=False, num_devices=1)
    args = [nc.dram_tensor(n + "_in", arrays[n].shape, F32, kind="ExternalInput").ap() for n in _INS]
    out = nc.dram_tensor("out_d", (TOK + 128, D), F32, kind="ExternalOutput").ap()
    build(nc, *args, out)
    r = _run(nc, [{n + "_in": arrays[n] for n in _INS}], core_ids=[0])
    return r.results[0]["out_d"][:TOK].reshape(B, S, D)
```
